# Optimizing a Trainium2 kernel written in Bass

```python
import numpy as np
import jax
import jax.numpy as jnp

def _softmax(x, axis=-1):
    return jax.nn.softmax(x, axis=axis)
def _gelu(x):
    return jax.nn.gelu(x, approximate=True)
def _silu(x):
    return jax.nn.silu(x)
def _sigmoid(x):
    return jax.nn.sigmoid(x)
def _layernorm(x, axis=-1, eps=1e-5):
    m = jnp.mean(x, axis=axis, keepdims=True)
    v = jnp.var(x, axis=axis, keepdims=True)
    return (x - m) / jnp.sqrt(v + eps)
def _scatter_add(tgt, idx, src, axis=0):
    return tgt.at[idx].add(src)
def _segment_sum(src, seg, n):
    return jax.ops.segment_sum(src, seg, n)

kernel_name = 'mk_adj_resnorm_d4_adj_512_0ef04c'

def setup_inputs(seed: int = 0):
    np.random.seed(seed)
    _w = jnp.asarray
    def _rec_inputs():
        import jax
        import jax.numpy as jnp
        _gk = jax.random.key(seed)
        x = 7.22e-05 + 1 * jax.random.normal(jax.random.fold_in(_gk, 1), (128, 64, 512), jnp.float32)
        _w = (1.0 + jnp.arange(64, dtype=jnp.float32)) ** -0.5
        _w = _w / _w.mean()
        _pij = jnp.clip(0.0625 * _w[:, None] * _w[None, :], 0.0, 1.0)
        _a = jax.random.uniform(jax.random.fold_in(_gk, 2), (128, 64, 64)) < _pij
        _a = jnp.logical_or(_a, jnp.swapaxes(_a, -1, -2))
        _a = jnp.logical_or(_a, jnp.eye(64, dtype=bool))
        _af = _a.astype(jnp.float32)
        _af = _af * jax.random.uniform(jax.random.fold_in(_gk, 3), (128, 64, 64), jnp.float32, 0.05, 1)
        adj = _af
        _nm = jnp.ones((128, 64), dtype=bool)
        nodemask = _nm
        return x, adj, nodemask
    x, adj, nodemask = _rec_inputs()
    def _L0_gnn_setup():
        import jax, jax.numpy as jnp
        import numpy as np
        EPS_LN = 1e-05

        def hypergraph_conv(x, adj, W, b):
            N, C, _ = adj.shape
            H = (adj != 0).astype(x.dtype)
            w = adj.reshape(N, -1)[:, :C]
            xw = jnp.einsum('ncd,hd->nch', x, W)
            Dn = jnp.einsum('nce,ne->nc', H, w)
            Dn = jnp.where(Dn > 0, 1.0 / Dn, 0.0)
            Be = H.sum(axis=1)
            Be = jnp.where(Be > 0, 1.0 / Be, 0.0)
            m = Be[:, :, None] * jnp.einsum('nce,nch->neh', H, xw)
            out = Dn[:, :, None] * jnp.einsum('nce,neh->nch', H, m)
            return out + b

        def layer_norm(x, g, b):
            mu = jnp.mean(x, axis=-1, keepdims=True)
            var = jnp.var(x, axis=-1, keepdims=True)
            return (x - mu) * jax.lax.rsqrt(var + EPS_LN) * g + b
        key = jax.random.key(seed)
        ks = jax.random.split(key, 4)
        N, C, Din, Dh, Dout = (16, 1024, 512, 1024, 512)
        x = jax.random.normal(ks[0], (N, C, Din), dtype=jnp.float32)
        adj = jax.random.uniform(ks[1], (N, C, C), dtype=jnp.float32, minval=0.1, maxval=1.0)
        W1 = jax.random.normal(ks[2], (Dh, Din), dtype=jnp.float32) * (1.0 / np.sqrt(Din))
        b1 = jnp.zeros((Dh,), dtype=jnp.float32)
        gamma = jnp.ones((Dh,), dtype=jnp.float32)
        beta = jnp.zeros((Dh,), dtype=jnp.float32)
        W2 = jax.random.normal(ks[3], (Dout, Dh), dtype=jnp.float32) * (1.0 / np.sqrt(Dh))
        b2 = jnp.zeros((Dout,), dtype=jnp.float32)
        return {'x': x, 'adj': adj, 'W1': W1, 'b1': b1, 'gamma': gamma, 'beta': beta, 'W2': W2, 'b2': b2}
    _L0_gnn_all = _L0_gnn_setup()
    _L0_gnn_in = {k: v for k, v in _L0_gnn_all.items() if k in ('W1', 'b1', 'gamma', 'beta', 'W2', 'b2', )}
    del _L0_gnn_all

    def _L1_gnn_setup():
        import jax, jax.numpy as jnp
        import numpy as np
        B, N, D_IN, D_OUT = (4, 4096, 512, 512)
        key = jax.random.key(seed)
        k1, k2, k3, k4 = jax.random.split(key, 4)
        x = jax.random.normal(k1, (B, N, D_IN), dtype=jnp.float32)
        A_shape = jax.random.uniform(k2, (B, N, N), dtype=jnp.float32)
        w = jax.random.normal(k3, (D_IN, D_OUT), dtype=jnp.float32)
        a = jax.random.normal(k4, (D_OUT,), dtype=jnp.float32)
        return {'x': x, 'A_shape': A_shape, 'w': w, 'a': a}
    _L1_gnn_all = _L1_gnn_setup()
    _L1_gnn_in = {k: v for k, v in _L1_gnn_all.items() if k in ('w', 'a', )}
    del _L1_gnn_all

    def _L2_gnn_setup():
        import jax, jax.numpy as jnp
        import numpy as np
        B, N, F_IN, F_HID, F_OUT = (32, 1024, 512, 512, 512)

        def _gcn_layer(x, adj, W, b):
            support = jnp.einsum('bnf,fh->bnh', x, W)
            return jnp.einsum('bnm,bmh->bnh', adj, support) + b
        key = jax.random.key(seed)
        ks = jax.random.split(key, 8)

        def xavier(k, fan_in, fan_out):
            bound = float(np.sqrt(6.0 / (fan_in + fan_out)))
            return jax.random.uniform(k, (fan_in, fan_out), jnp.float32, -bound, bound)
        return {'batch_graph': jax.random.normal(ks[0], (B, N, F_IN), jnp.float32), 'adj': jax.random.uniform(ks[1], (B, N, N), jnp.float32), 'W1': xavier(ks[2], F_IN, F_HID), 'b1': jnp.zeros((F_HID,), jnp.float32), 'W2': xavier(ks[3], F_HID, F_HID), 'b2': jnp.zeros((F_HID,), jnp.float32), 'W3': xavier(ks[4], F_HID, F_OUT), 'b3': jnp.zeros((F_OUT,), jnp.float32)}
    _L2_gnn_all = _L2_gnn_setup()
    _L2_gnn_in = {k: v for k, v in _L2_gnn_all.items() if k in ('W1', 'b1', 'W2', 'b2', 'W3', 'b3', )}
    del _L2_gnn_all

    def _L3_gnn_setup():
        import jax, jax.numpy as jnp
        import numpy as np
        HEADS = 8
        DIM_HEAD = 64
        LA = 0.33
        LD = 0.33
        LG = 0.33
        key = jax.random.key(seed)
        ks = jax.random.split(key, 6)
        B, N, D = (4, 1024, 512)
        inner = HEADS * DIM_HEAD
        x = jax.random.normal(ks[0], (B, N, D), jnp.float32)
        mask = jax.random.uniform(ks[1], (B, N)) < 0.9
        adjacency_mat = (jax.random.uniform(ks[2], (B, N, N)) < 0.05).astype(jnp.float32)
        distance_mat = jax.random.uniform(ks[3], (B, N, N), jnp.float32) * 5.0
        W_qkv = jax.random.normal(ks[4], (D, inner * 3), jnp.float32) * 0.02
        W_out = jax.random.normal(ks[5], (inner, D), jnp.float32) * 0.02
        b_out = jnp.zeros((D,), jnp.float32)
        return {'x': x, 'mask': mask, 'adjacency_mat': adjacency_mat, 'distance_mat': distance_mat, 'W_qkv': W_qkv, 'W_out': W_out, 'b_out': b_out}
    _L3_gnn_all = _L3_gnn_setup()
    _L3_gnn_in = {k: v for k, v in _L3_gnn_all.items() if k in ('W_qkv', 'W_out', 'b_out', )}
    del _L3_gnn_all

    return {
        "x": x,
        "adj": adj,
        "nodemask": nodemask,
        "L0_gnn_W1": _L0_gnn_in["W1"],
        "L0_gnn_b1": _L0_gnn_in["b1"],
        "L0_gnn_gamma": _L0_gnn_in["gamma"],
        "L0_gnn_beta": _L0_gnn_in["beta"],
        "L0_gnn_W2": _L0_gnn_in["W2"],
        "L0_gnn_b2": _L0_gnn_in["b2"],
        "L1_gnn_w": _L1_gnn_in["w"],
        "L1_gnn_a": _L1_gnn_in["a"],
        "L2_gnn_W1": _L2_gnn_in["W1"],
        "L2_gnn_b1": _L2_gnn_in["b1"],
        "L2_gnn_W2": _L2_gnn_in["W2"],
        "L2_gnn_b2": _L2_gnn_in["b2"],
        "L2_gnn_W3": _L2_gnn_in["W3"],
        "L2_gnn_b3": _L2_gnn_in["b3"],
        "L3_gnn_W_qkv": _L3_gnn_in["W_qkv"],
        "L3_gnn_W_out": _L3_gnn_in["W_out"],
        "L3_gnn_b_out": _L3_gnn_in["b_out"],
    }

def reference(x, adj, nodemask, L0_gnn_W1, L0_gnn_b1, L0_gnn_gamma, L0_gnn_beta, L0_gnn_W2, L0_gnn_b2, L1_gnn_w, L1_gnn_a, L2_gnn_W1, L2_gnn_b1, L2_gnn_W2, L2_gnn_b2, L2_gnn_W3, L2_gnn_b3, L3_gnn_W_qkv, L3_gnn_W_out, L3_gnn_b_out):
    import jax
    import jax.numpy as jnp
    def _L0_gnn_ref(x, adj, W1, b1, gamma, beta, W2, b2):
        import jax, jax.numpy as jnp
        import numpy as np
        EPS_LN = 1e-05

        def hypergraph_conv(x, adj, W, b):
            N, C, _ = adj.shape
            H = (adj != 0).astype(x.dtype)
            w = adj.reshape(N, -1)[:, :C]
            xw = jnp.einsum('ncd,hd->nch', x, W)
            Dn = jnp.einsum('nce,ne->nc', H, w)
            Dn = jnp.where(Dn > 0, 1.0 / Dn, 0.0)
            Be = H.sum(axis=1)
            Be = jnp.where(Be > 0, 1.0 / Be, 0.0)
            m = Be[:, :, None] * jnp.einsum('nce,nch->neh', H, xw)
            out = Dn[:, :, None] * jnp.einsum('nce,neh->nch', H, m)
            return out + b

        def layer_norm(x, g, b):
            mu = jnp.mean(x, axis=-1, keepdims=True)
            var = jnp.var(x, axis=-1, keepdims=True)
            return (x - mu) * jax.lax.rsqrt(var + EPS_LN) * g + b
        h = jax.nn.relu(hypergraph_conv(x, adj, W1, b1))
        h = layer_norm(h, gamma, beta)
        y = hypergraph_conv(h, adj, W2, b2)
        return y + x

    def _L1_gnn_ref(x, A_shape, w, a):
        import jax, jax.numpy as jnp
        import numpy as np
        B, N, D_IN, D_OUT = (4, 4096, 512, 512)
        y = x @ w
        s = y @ a
        A = s[..., :, None] + s[..., None, :]
        A = jnp.tanh(A / 8.0) * 8.0
        A = jnp.where(A >= 0, A, 0.1 * A)
        A = jnp.exp(A) * A_shape
        A = A / jnp.sum(A, axis=-1, keepdims=True)
        A = A * jnp.sum(A_shape, axis=-1, keepdims=True)
        out = A @ x @ w
        return out

    def _L2_gnn_ref(batch_graph, adj, W1, b1, W2, b2, W3, b3):
        import jax, jax.numpy as jnp
        import numpy as np
        B, N, F_IN, F_HID, F_OUT = (32, 1024, 512, 512, 512)

        def _gcn_layer(x, adj, W, b):
            support = jnp.einsum('bnf,fh->bnh', x, W)
            return jnp.einsum('bnm,bmh->bnh', adj, support) + b
        x = jax.nn.relu(_gcn_layer(batch_graph, adj, W1, b1))
        x = jax.nn.relu(_gcn_layer(x, adj, W2, b2))
        out = _gcn_layer(x, adj, W3, b3)
        return out

    def _L3_gnn_ref(x, mask, adjacency_mat, distance_mat, W_qkv, W_out, b_out):
        import jax, jax.numpy as jnp
        import numpy as np
        HEADS = 8
        DIM_HEAD = 64
        LA = 0.33
        LD = 0.33
        LG = 0.33
        B, N, _ = x.shape
        scale = DIM_HEAD ** (-0.5)
        qkv = (x @ W_qkv).reshape(B, N, HEADS, 3, DIM_HEAD)
        q, k, v = (jnp.transpose(qkv[..., i, :], (0, 2, 1, 3)) for i in range(3))
        dots = jnp.einsum('bhid,bhjd->bhij', q, k) * scale
        big = jnp.finfo(dots.dtype).max
        m2 = mask[:, None, :, None] & mask[:, None, None, :]
        dots = jnp.where(m2, dots, -big)
        attn = jax.nn.softmax(dots, axis=-1) * LA
        adj = jnp.where(m2, adjacency_mat[:, None], 0.0)
        dist = jnp.where(m2, distance_mat[:, None], big)
        attn = attn + LG * adj + LD * jnp.exp(-dist)
        out = jnp.einsum('bhij,bhjd->bhid', attn, v)
        out = jnp.transpose(out, (0, 2, 1, 3)).reshape(B, N, HEADS * DIM_HEAD)
        return out @ W_out + b_out

    x = _layernorm(x + _L0_gnn_ref(x, adj, L0_gnn_W1, L0_gnn_b1, L0_gnn_gamma, L0_gnn_beta, L0_gnn_W2, L0_gnn_b2), axis=-1)
    x = _layernorm(x + _L1_gnn_ref(x, adj, L1_gnn_w, L1_gnn_a), axis=-1)
    x = _layernorm(x + _L2_gnn_ref(x, adj, L2_gnn_W1, L2_gnn_b1, L2_gnn_W2, L2_gnn_b2, L2_gnn_W3, L2_gnn_b3), axis=-1)
    x = _layernorm(x + _L3_gnn_ref(x, nodemask, adj, adj, L3_gnn_W_qkv, L3_gnn_W_out, L3_gnn_b_out), axis=-1)
    return x


_drawn_inputs = setup_inputs


def setup_inputs(seed=0):
    import zlib

    import numpy as np

    out = dict(_drawn_inputs(seed))
    spreads = {'L0_gnn_b1': (0.0, 0.1),
     'L0_gnn_gamma': (1.0, 0.2),
     'L0_gnn_beta': (0.0, 0.1),
     'L0_gnn_b2': (0.0, 0.1),
     'L2_gnn_b1': (0.0, 0.423),
     'L2_gnn_b2': (0.0, 0.8),
     'L2_gnn_b3': (0.0, 2.0),
     'L3_gnn_b_out': (0.0, 0.351)}
    factors = {}
    for name, (base, spread) in spreads.items():
        noise = np.random.default_rng([zlib.crc32(name.encode()), seed]).standard_normal(out[name].shape)
        drawn = base * np.exp(spread * noise) if base else spread * noise
        out[name] = jnp.asarray(drawn.astype(out[name].dtype))
    for name, factor in factors.items():
        out[name] = (out[name] * factor).astype(out[name].dtype)
    return out
```

```python
from contextlib import ExitStack

import concourse.bass as bass
from concourse import mybir
from concourse.alu_op_type import AluOpType as ALU

F32 = mybir.dt.float32
F32R = mybir.dt.float32r
U8 = mybir.dt.uint8
ACT = mybir.ActivationFunctionType
AX = mybir.AxisListType

P = 128
C = 64
D = 512
DH = 1024
CH = 4
EPS = 1e-5
TINY = 1.2e-38
KD, KH = D // P, DH // P


def rounds(steps, chains):
    last = max(o for _, o in steps)
    return [(name, r - o) for r in range(chains + last) for name, o in steps if 0 <= r - o < chains]


def hypergraph_and_pairwise(nc, semaphores, x, adj, W1T, b1, gamma, beta, W2T, b2, w, wT, a, x2):
    tiles = x.shape[0] * x.shape[1] // P
    iters = tiles // CH
    x_rows = x.rearrange("(t g) c d -> t (g c) d", g=P // C)
    adj_t = adj.rearrange("(t g) c e -> t g c e", g=P // C)

    with ExitStack() as ctx:
        def sb(name, shape, dt=F32):
            return ctx.enter_context(nc.sbuf_tensor(name, shape, dt))

        def sem(name):
            semaphores.append(nc.alloc_semaphore(name))
            return semaphores[-1]

        W1h, W1l = sb("W1h", [P, KD, DH], F32R), sb("W1l", [P, KD, DH], F32R)
        W2h, W2l = sb("W2h", [P, KH, D], F32R), sb("W2l", [P, KH, D], F32R)
        Wh, Wl = sb("Wh", [P, KD, D], F32R), sb("Wl", [P, KD, D], F32R)
        ident = sb("ident", [P, P])
        ones = sb("ones", [P, 2])
        ones_row = sb("ones_row", [2, P], F32R)
        b1_rows = sb("b1_rows", [2, DH], F32R)
        b2_all = sb("b2_all", [P, D])
        v_all = sb("v_all", [P, D])
        wa_all = sb("wa_all", [P, D])
        tmp = sb("tmp", [P, D])
        gam = sb("gam", [P, KH])
        bet = sb("bet", [P, KH])
        a_col = sb("a_col", [P, KD])
        mhalf = sb("mhalf", [P, 1])
        A = sb("A", [P, CH, P])
        ATn = sb("ATn", [P, CH, P + 1])
        ATc = sb("ATc", [P, CH, P + 1])
        HT = sb("HT", [P, CH, P], F32R)
        HBh, HBl = sb("HBh", [P, CH, P], F32R), sb("HBl", [P, CH, P], F32R)
        DI = sb("DI", [P, CH, P])
        GT = sb("GT", [P, CH, P])
        GTh, GTl = sb("GTh", [P, CH, P], F32R), sb("GTl", [P, CH, P], F32R)
        Fp = sb("Fp", [P, CH, P])
        A1h, A1l = sb("A1h", [P, CH, P], F32R), sb("A1l", [P, CH, P], F32R)
        X = sb("X", [P, CH, D])
        Hh, Hl = sb("Hh", [P, CH, DH], F32R), sb("Hl", [P, CH, DH], F32R)
        Th, Tl = sb("Th", [P, CH, DH], F32R), sb("Tl", [P, CH, DH], F32R)
        R = sb("R", [P, CH, DH])
        sm = sb("sm", [P, CH, 40])
        WCOL, CNT, CNTM, BINV, G1, VE, RS, NM, S, S8, RI, CI = range(12)
        MV, BN = 12, 14

        def col(c, k, n=1):
            return sm[:, c, k:k + n]

        psA = [ctx.enter_context(nc.psum_tensor(f"psA{c}", [P, D], F32)) for c in range(CH)]
        psB = [ctx.enter_context(nc.psum_tensor(f"psB{c}", [P, D], F32)) for c in range(CH)]

        consts_ok, ident0 = sem("consts_ok"), sem("ident0")
        vec_in, staged, split_hi, split_lo, slot_read, v_ps, v_sb, wa_ps, wa_sb, rows_ok = map(sem, (
            "vec_in", "staged", "split_hi", "split_lo", "slot_read", "v_ps", "v_sb", "wa_ps", "wa_sb", "rows_ok"))
        stage_in = [sem(f"stage_in{i}") for i in range(4)]
        adj_in = [sem(f"adj_in{c}") for c in range(CH)]
        x_in = [sem(f"x_in{c}") for c in range(CH)]
        x2_stored = [sem(f"x2_stored{c}") for c in range(CH)]
        (adjT_ps, adjT_sb, inc_sb, cnt_ok, cntm_ok, binv_ok, hbh_ok, hb_sb, deg_ps, dmx_ok, drec_ok, dinv_ok,
         gt_f, gt_h, gt_sb, g1_ps, g1_sb, xh_ok, xl_ok, adjT_cur, tx_ps, t1h, t1_sb, u1_ok, u2_ok, u3_ok, u_ok,
         r_psA, r_psB, r_sbA, r_sbB, bn1, mv1, ve1, rs1, g2f, rh_ok, g2h, g2_ok, t2_psA, t2_psB, t2hA, t2hB,
         t2_sb, y2_ps, z1, bn2, mv2, ve2, rs2, x1_ok, s_ok, x1h, x1l, s8_ok, sb_ps, tanh_ok, lrelu_ok, exp_ok,
         af_ok, a1h, a1_ok, t3_ps, t3h, ri_ok, t3_sb, y3_ps, z2, bn3, mv3, ve3, rs3, x2_ok) = map(sem, (
            "adjT_ps adjT_sb inc_sb cnt_ok cntm_ok binv_ok hbh_ok hb_sb deg_ps dmx_ok drec_ok dinv_ok "
            "gt_f gt_h gt_sb g1_ps g1_sb xh_ok xl_ok adjT_cur tx_ps t1h t1_sb u1_ok u2_ok u3_ok u_ok "
            "r_psA r_psB r_sbA r_sbB bn1 mv1 ve1 rs1 g2f rh_ok g2h g2_ok t2_psA t2_psB t2hA t2hB "
            "t2_sb y2_ps z1 bn2 mv2 ve2 rs2 x1_ok s_ok x1h x1l s8_ok sb_ps tanh_ok lrelu_ok exp_ok "
            "af_ok a1h a1_ok t3_ps t3h ri_ok t3_sb y3_ps z2 bn3 mv3 ve3 rs3 x2_ok").split())

        W1v = W1T.rearrange("(k p) n -> p k n", p=P)
        W2v = W2T.rearrange("(k p) n -> p k n", p=P)
        wv = w.rearrange("(k p) n -> p k n", p=P)
        wTv = wT.rearrange("(k p) n -> p k n", p=P)
        pieces = ([(W1v[:, k, :], W1h[:, k, :], W1l[:, k, :], None) for k in range(KD)]
                  + [(wv[:, k:k + 2, :], Wh[:, k:k + 2, :], Wl[:, k:k + 2, :], None) for k in (0, 2)]
                  + [(W2v[:, k:k + 2, :], W2h[:, k:k + 2, :], W2l[:, k:k + 2, :], k) for k in range(0, KH, 2)])
        first_g = KD + 2
        slots = 4

        def stage(n, two_chunks=True):
            s = R[:, n % slots, :]
            return s.rearrange("p (k n) -> p k n", k=2) if two_chunks else s

        ORDER_PREP = rounds([("adjT", 0), ("inc", 0), ("xsplit", 0), ("deg", 1), ("g", 1), ("g1", 2)], CH)
        ORDER = (
            [("cur", c) for c in range(CH)]
            + rounds([("tx", 0), ("txe", 0)], CH)
            + rounds([("u", 0), ("y1", 0), ("relu", 0), ("st1", 0), ("rs1", 0), ("rsplit", 1)], CH)
            + rounds([("t2", 0), ("t2e", 0)], CH)
            + rounds([("y2", 0), ("z1", 0), ("adjT", 0), ("rs2", 0), ("inc", 0), ("x1", 1), ("x1split", 1), ("deg", 1), ("g", 1),
                      ("g1", 2), ("sb", 2), ("f", 2), ("xsplit", 2), ("t3", 3), ("t3e", 3),
                      ("y3", 4), ("z2", 4), ("rs3", 4), ("x2", 5)], CH))
        b1_raw = [Fp[0:2, :, :].rearrange("p c j -> p (c j)"), tmp[0:2, :]]
        block = ctx.enter_context(nc.Block())

        @block.sync
        def _(sp):
            for c in range(CH):
                if c == 0:
                    sp.wait_ge(consts_ok, 6)
                for g in range(P // C):
                    sp.dma_start(A[g * C:(g + 1) * C, c, g * C:(g + 1) * C], adj_t[c, g]).then_inc(adj_in[c], 16)
                sp.dma_start(X[:, c, :], x_rows[c]).then_inc(x_in[c], 16)
            sp.dma_start(gam[:, :], gamma.rearrange("(k p) -> p k", p=P), allow_slow_non_contiguous=True).then_inc(vec_in, 16)
            sp.dma_start(bet[:, :], beta.rearrange("(k p) -> p k", p=P), allow_slow_non_contiguous=True).then_inc(vec_in, 16)
            sp.dma_start(a_col[:, :], a.rearrange("(k p) -> p k", p=P), allow_slow_non_contiguous=True).then_inc(vec_in, 16)
            sp.dma_start(b2_all[:, :], b2.partition_broadcast(P)).then_inc(vec_in, 16)
            for half in range(2):
                sp.dma_start(b1_raw[half], b1[half * D:(half + 1) * D].partition_broadcast(2)).then_inc(vec_in, 16)
            for n, (src, _, _, _) in enumerate(pieces):
                if n >= slots:
                    sp.wait_ge(split_lo, n - slots + 1)
                    if n - slots >= first_g:
                        sp.wait_ge(v_ps, n - slots - first_g + 1)
                sp.dma_start(stage(n, n >= KD), src).then_inc(stage_in[n % slots], 16)
            for k in (0, 2):
                n = len(pieces) + k // 2
                sp.wait_ge(split_lo, n - slots + 1)
                if n - slots >= first_g:
                    sp.wait_ge(v_ps, n - slots - first_g + 1)
                sp.dma_start(stage(n), wTv[:, k:k + 2, :]).then_inc(stage_in[n % slots], 16)
            for c in range(CH):
                sp.sem_inc(x2_stored[c], 16)
            with sp.Fori(0, iters) as it:
                nxt = sp.snap(((it + 1) % iters) * CH)
                t0 = sp.snap(it * CH)
                for c in range(CH):
                    sp.wait_ge(adjT_ps, sp.snap(t0 + (c + 1)))
                    for g in range(P // C):
                        sp.dma_start(A[g * C:(g + 1) * C, c, g * C:(g + 1) * C],
                                     adj_t[bass.ds(nxt + c, 1), g].rearrange("a c e -> (a c) e")).then_inc(adj_in[c], 16)
                for c in range(CH):
                    sp.wait_ge(z1, sp.snap(t0 + (c + 1)))
                    sp.dma_start(X[:, c, :], x_rows[bass.ds(nxt + c, 1)].rearrange("a r d -> (a r) d")).then_inc(x_in[c], 16)
                for c in range(CH):
                    sp.wait_ge(x2_ok, sp.snap(t0 + (c + 1)))
                    sp.dma_start(x2[bass.ds(t0 + c, 1)].rearrange("a r d -> (a r) d"), R[:, c, 0:D]).then_inc(x2_stored[c], 16)
            for c in range(CH):
                sp.wait_ge(x2_stored[c], 16 * (iters + 1))
                sp.wait_ge(x_in[c], 16 * (iters + 1))
                sp.wait_ge(adj_in[c], 32 * (iters + 1))

        @block.gpsimd
        def _(pool):
            pool.memset(ident[:, :], 0.0).then_inc(ident0, 1)
            pool.wait_ge(ident0, 1)
            pool.affine_select(out=ident[:, :], in_=ident[:, :], compare_op=ALU.not_equal, fill=1.0, base=0,
                               pattern=[[-1, P]], channel_multiplier=1).then_inc(consts_ok, 1)
            pool.memset(ones[:, :], 1.0).then_inc(consts_ok, 1)
            pool.memset(ones_row[:, :].bitcast(F32), 1.0).then_inc(consts_ok, 1)
            pool.memset(mhalf[:, :], -0.5).then_inc(consts_ok, 1)
            pool.memset(A[:, :, :], 0.0).then_inc(consts_ok, 1)
            pool.memset(tmp[:, 0:2], 0.0).then_inc(consts_ok, 1)

            def alone(sem, value):
                pool.wait_ge(consts_ok, 6)
                pool.wait_ge(sem, value)

            def rstd(c, n, mv, ve, col_rs=RS):
                alone(mv, n[c])
                pool.tensor_scalar(col(c, VE), col(c, MV + 1), EPS, None, ALU.add).then_inc(ve, 1)
                pool.wait_ge(ve, n[c])
                return pool.tensor_tensor(col(c, RS), col(c, VE), mhalf[:, :], ALU.pow)

            def xsplit(c, n):
                pool.wait_ge(xh_ok, n[c])
                pool.tensor_tensor(Hl[:, c, D:DH], X[:, c, :], Hh[:, c, D:DH].bitcast(F32), ALU.subtract).then_inc(xl_ok, 1)

            def cur(c, n):
                alone(gt_f, n[c])
                pool.tensor_copy(ATc[:, c, :], ATn[:, c, :]).then_inc(adjT_cur, 1)

            def u(c, n):
                alone(g1_sb, n[c])
                pool.tensor_scalar(tmp[:, :], v_all[:, :], col(c, G1), None, ALU.mult).then_inc(u1_ok, 1)
                pool.wait_ge(u1_ok, n[c])
                pool.tensor_tensor(tmp[:, :], tmp[:, :], b2_all[:, :], ALU.add).then_inc(u2_ok, 1)
                pool.tensor_scalar(X[:, c, :], X[:, c, :], 2.0, None, ALU.mult).then_inc(u3_ok, 1)
                pool.wait_ge(u3_ok, n[c])
                pool.tensor_tensor(X[:, c, :], X[:, c, :], tmp[:, :], ALU.add).then_inc(u_ok, 1)

            def rs_first(c, n):
                alone(mv1, n[c])
                pool.tensor_scalar(col(c, NM), col(c, MV), -1.0, None, ALU.mult)
                rstd(c, n, mv1, ve1).then_inc(rs1, 1)
                alone(rs1, n[c])
                pool.tensor_scalar(GT[:, c, :], GT[:, c, :], col(c, RS), None, ALU.mult).then_inc(g2f, 1)

            def rs_second(c, n):
                rstd(c, n, mv2, ve2).then_inc(rs2, 1)

            def x1split(c, n):
                pool.wait_ge(x1h, n[c])
                pool.tensor_tensor(Hl[:, c, 0:D], R[:, c, D:DH], Hh[:, c, 0:D].bitcast(F32), ALU.subtract).then_inc(x1l, 1)

            def rs_third(c, n):
                rstd(c, n, mv3, ve3).then_inc(rs3, 1)

            first = [c + 1 for c in range(CH)]
            for step, c in ORDER_PREP:
                if step == "xsplit":
                    xsplit(c, first)
            pool.wait_ge(v_sb, 1)
            pool.wait_ge(vec_in, 6 * 16)
            with pool.Fori(0, iters) as it:
                now = [pool.to_reg(it * CH + (c + 1)) for c in range(CH)]
                nxt = [pool.snap(it * CH + (CH + c + 1)) for c in range(CH)]
                for step, c in ORDER:
                    if step == "cur":
                        cur(c, now)
                    if step == "u":
                        u(c, now)
                    if step == "rs1":
                        rs_first(c, now)
                    if step == "rs2":
                        rs_second(c, now)
                    if step == "x1split":
                        x1split(c, now)
                    if step == "xsplit":
                        xsplit(c, nxt)
                    if step == "rs3":
                        rs_third(c, now)

        @block.scalar
        def _(act):
            act.wait_ge(vec_in, 6 * 16)
            for half in range(2):
                act.copy(b1_rows[:, half * D:(half + 1) * D], b1_raw[half]).then_inc(rows_ok, 1)

            for n, (_, hi, _, g) in enumerate(pieces):
                act.wait_ge(stage_in[n % slots], 16 * (n // slots + 1))
                if g is None:
                    act.copy(hi, stage(n, n >= KD)).then_inc(split_hi, 1)
                else:
                    act.activation(hi[:, 0, :], stage(n)[:, 0, :], ACT.Copy, scale=gam[:, g:g + 1])
                    act.activation(hi[:, 1, :], stage(n)[:, 1, :], ACT.Copy, scale=gam[:, g + 1:g + 2]).then_inc(split_hi, 1)
            act.wait_ge(v_ps, 4)
            act.copy(v_all[:, :], psA[0][:, :]).then_inc(v_sb, 1)
            act.wait_ge(wa_ps, 2)
            act.copy(wa_all[:, :], psA[1][:, :]).then_inc(wa_sb, 1)

            def adjT(c, n, after=None):
                act.wait_ge(adjT_ps, n[c])
                if after:
                    act.wait_ge(adjT_cur, after[c])
                act.copy(ATn[:, c, 0:P], psB[c][:, 0:P]).then_inc(adjT_sb, 1)

            def g(c, n):
                act.wait_ge(gt_f, n[c])
                act.copy(GTh[:, c, :], GT[:, c, :]).then_inc(gt_h, 1)

            def xsplit(c, k):
                act.wait_ge(x_in[c], k)
                act.copy(Hh[:, c, D:DH], X[:, c, :]).then_inc(xh_ok, 1)

            def txe(c, n):
                act.wait_ge(tx_ps, n[c])
                act.copy(Th[:, c, 0:D], psA[c][:, :]).then_inc(t1h, 1)

            def relu(c, n, stored):
                act.wait_ge(r_psA, n[c])
                act.wait_ge(x2_stored[c], stored)
                act.activation(R[:, c, 0:D], psA[c][:, :], ACT.Relu).then_inc(r_sbA, 1)
                act.wait_ge(r_psB, n[c])
                act.activation(R[:, c, D:DH], psB[c][:, :], ACT.Relu).then_inc(r_sbB, 1)

            def rsplit(c, n):
                act.wait_ge(rs1, n[c])
                act.activation(Hh[:, c, :], R[:, c, :], ACT.Identity, bias=col(c, NM)).then_inc(rh_ok, 1)
                act.wait_ge(g2f, n[c])
                act.copy(GTh[:, c, :], GT[:, c, :]).then_inc(g2h, 1)

            def t2e(c, n):
                act.wait_ge(t2_psA, n[c])
                act.copy(Th[:, c, 0:D], psA[c][:, :]).then_inc(t2hA, 1)
                act.wait_ge(t2_psB, n[c])
                act.copy(Th[:, c, D:DH], psB[c][:, :]).then_inc(t2hB, 1)

            def x1split(c, n):
                act.wait_ge(x1_ok, n[c])
                act.copy(Hh[:, c, 0:D], R[:, c, D:DH]).then_inc(x1h, 1)
                act.wait_ge(s_ok, n[c])
                act.mul(col(c, S8), col(c, S), 0.125).then_inc(s8_ok, 1)

            def f(c, n):
                act.wait_ge(sb_ps, n[c])
                act.wait_ge(s8_ok, n[c])
                act.activation(Fp[:, c, :], psB[c][:, 0:P], ACT.Tanh, bias=col(c, S8), scale=0.125).then_inc(tanh_ok, 1)
                act.wait_ge(lrelu_ok, n[c])
                act.activation(Fp[:, c, :], Fp[:, c, :], ACT.Exp, scale=8.0).then_inc(exp_ok, 1)
                act.wait_ge(af_ok, n[c])
                act.copy(A1h[:, c, :], Fp[:, c, :]).then_inc(a1h, 1)

            def t3e(c, n):
                act.wait_ge(t3_ps, n[c])
                act.copy(Th[:, c, 0:D], psA[c][:, :]).then_inc(t3h, 1)

            first = [c + 1 for c in range(CH)]
            for step, c in ORDER_PREP:
                if step == "adjT":
                    adjT(c, first)
                if step == "g":
                    g(c, first)
                if step == "xsplit":
                    xsplit(c, 16)
            with act.Fori(0, iters) as it:
                now = [act.snap(it * CH + (c + 1)) for c in range(CH)]
                nxt = [act.snap(it * CH + (CH + c + 1)) for c in range(CH)]
                stored = act.snap(it * 16 + 16)
                loaded = act.snap(it * 16 + 32)
                for step, c in ORDER:
                    if step == "adjT":
                        adjT(c, nxt, now)
                    if step == "g":
                        g(c, nxt)
                    if step == "xsplit":
                        xsplit(c, loaded)
                    if step == "txe":
                        txe(c, now)
                    if step == "relu":
                        relu(c, now, stored)
                    if step == "rsplit":
                        rsplit(c, now)
                    if step == "t2e":
                        t2e(c, now)
                    if step == "x1split":
                        x1split(c, now)
                    if step == "f":
                        f(c, now)
                    if step == "t3e":
                        t3e(c, now)

        @block.vector
        def _(dve):
            dve.wait_ge(consts_ok, 6)
            for half in range(2):
                hi, lo = b1_rows[:, half * D:(half + 1) * D], b1_raw[half]
                dve.wait_ge(rows_ok, 2 + 3 * half)
                dve.tensor_tensor(lo, lo, hi.bitcast(F32), ALU.subtract).then_inc(rows_ok, 1)
                dve.wait_ge(rows_ok, 3 + 3 * half)
                dve.tensor_scalar(lo, lo, ident[0:2, 1:2], None, ALU.mult).then_inc(rows_ok, 1)
                dve.wait_ge(rows_ok, 4 + 3 * half)
                dve.scalar_tensor_tensor(hi, hi.bitcast(F32), ident[0:2, 0:1], lo, ALU.mult, ALU.add).then_inc(rows_ok, 1)

            for n, (_, hi, lo, g) in enumerate(pieces):
                dve.wait_ge(split_hi, n + 1)
                if g is None:
                    dve.tensor_tensor(lo, stage(n, n >= KD), hi.bitcast(F32), ALU.subtract).then_inc(split_lo, 1)
                else:
                    for k in range(2):
                        last = dve.scalar_tensor_tensor(lo[:, k, :], stage(n)[:, k, :], gam[:, g + k:g + k + 1],
                                                        hi[:, k, :].bitcast(F32), ALU.mult, ALU.subtract)
                    last.then_inc(split_lo, 1)

            def alone(sem, value):
                dve.wait_ge(consts_ok, 6)
                dve.wait_ge(sem, value)

            def inc(c, n):
                dve.wait_ge(adjT_sb, n[c])
                dve.tensor_tensor(col(c, WCOL), ATn[:, c, 0:1], ATn[:, c, C:C + 1], ALU.add)
                dve.tensor_scalar(HT[:, c, :], ATn[:, c, 0:P], 0.0, None, ALU.not_equal).then_inc(inc_sb, 1)
                dve.wait_ge(inc_sb, n[c])
                dve.reduce_sum(col(c, CNT), HT[:, c, :].bitcast(F32), AX.X).then_inc(cnt_ok, 1)
                dve.wait_ge(cnt_ok, n[c])
                dve.tensor_scalar(col(c, CNTM), col(c, CNT), 1.0, None, ALU.max).then_inc(cntm_ok, 1)
                dve.wait_ge(cntm_ok, n[c])
                dve.reciprocal(col(c, BINV), col(c, CNTM)).then_inc(binv_ok, 1)
                dve.wait_ge(binv_ok, n[c])
                dve.tensor_scalar(HBh[:, c, :], HT[:, c, :].bitcast(F32), col(c, BINV), None, ALU.mult).then_inc(hbh_ok, 1)
                dve.wait_ge(hbh_ok, n[c])
                dve.scalar_tensor_tensor(HBl[:, c, :], HT[:, c, :].bitcast(F32), col(c, BINV), HBh[:, c, :].bitcast(F32),
                                         ALU.mult, ALU.subtract).then_inc(hb_sb, 1)

            def g(c, n):
                dve.wait_ge(deg_ps, n[c])
                dve.tensor_copy(ATn[:, c, P:P + 1], psB[c][:, 3 * P:3 * P + 1])
                dve.tensor_scalar(DI[:, c, :], psB[c][:, P:2 * P], TINY, None, ALU.max).then_inc(dmx_ok, 1)
                dve.wait_ge(dmx_ok, n[c])
                dve.reciprocal(DI[:, c, :], DI[:, c, :]).then_inc(drec_ok, 1)
                dve.wait_ge(drec_ok, n[c])
                dve.scalar_tensor_tensor(DI[:, c, :], psB[c][:, P:2 * P], 0.0, DI[:, c, :], ALU.is_gt, ALU.mult).then_inc(dinv_ok, 1)
                dve.wait_ge(dinv_ok, n[c])
                dve.tensor_tensor(GT[:, c, :], psB[c][:, 2 * P:3 * P], DI[:, c, :], ALU.mult).then_inc(gt_f, 1)
                dve.wait_ge(gt_h, n[c])
                dve.tensor_tensor(GTl[:, c, :], GT[:, c, :], GTh[:, c, :].bitcast(F32), ALU.subtract).then_inc(gt_sb, 1)

            def g1(c, n):
                dve.wait_ge(g1_ps, n[c])
                dve.tensor_copy(col(c, G1), psB[c][:, 3 * P + 2:3 * P + 3]).then_inc(g1_sb, 1)

            def txe(c, n):
                dve.wait_ge(t1h, n[c])
                dve.tensor_tensor(Tl[:, c, 0:D], psA[c][:, :], Th[:, c, 0:D].bitcast(F32), ALU.subtract).then_inc(t1_sb, 1)

            def st1(c, n):
                dve.wait_ge(r_sbA, n[c])
                dve.bn_stats(col(c, BN, 6), R[:, c, 0:D])
                dve.wait_ge(r_sbB, n[c])
                dve.bn_stats(col(c, BN + 6, 6), R[:, c, D:DH]).then_inc(bn1, 1)
                alone(bn1, n[c])
                dve.bn_aggr(col(c, MV, 2), col(c, BN, 12)).then_inc(mv1, 1)

            def rsplit(c, n):
                dve.wait_ge(rh_ok, n[c])
                dve.scalar_tensor_tensor(Hl[:, c, :], R[:, c, :], col(c, NM), Hh[:, c, :].bitcast(F32), ALU.add, ALU.subtract)
                dve.wait_ge(g2h, n[c])
                dve.tensor_tensor(GTl[:, c, :], GT[:, c, :], GTh[:, c, :].bitcast(F32), ALU.subtract).then_inc(g2_ok, 1)

            def t2e(c, n):
                dve.wait_ge(t2hA, n[c])
                dve.tensor_tensor(Tl[:, c, 0:D], psA[c][:, :], Th[:, c, 0:D].bitcast(F32), ALU.subtract)
                dve.wait_ge(t2hB, n[c])
                dve.tensor_tensor(Tl[:, c, D:DH], psB[c][:, :], Th[:, c, D:DH].bitcast(F32), ALU.subtract).then_inc(t2_sb, 1)

            def stats(c, n, bn, mv):
                dve.bn_stats(col(c, BN, 6), R[:, c, 0:D]).then_inc(bn, 1)
                alone(bn, n[c])
                dve.bn_aggr(col(c, MV, 2), col(c, BN, 6)).then_inc(mv, 1)

            def z_first(c, n):
                dve.wait_ge(y2_ps, n[c])
                dve.wait_ge(u_ok, n[c])
                dve.tensor_tensor(R[:, c, 0:D], psA[c][:, :], X[:, c, :], ALU.add).then_inc(z1, 1)
                dve.wait_ge(z1, n[c])
                stats(c, n, bn2, mv2)

            def x1(c, n):
                dve.wait_ge(rs2, n[c])
                dve.tensor_scalar(R[:, c, D:DH], R[:, c, 0:D], col(c, MV), col(c, RS), ALU.subtract, ALU.mult).then_inc(x1_ok, 1)
                dve.wait_ge(x1_ok, n[c])
                dve.tensor_tensor_reduce(R[:, c, 0:D], R[:, c, D:DH], wa_all[:, :], 1.0, 0.0, ALU.mult, ALU.add,
                                         col(c, S)).then_inc(s_ok, 1)

            def f(c, n):
                dve.wait_ge(tanh_ok, n[c])
                dve.scalar_tensor_tensor(Fp[:, c, :], Fp[:, c, :], 0.1, Fp[:, c, :], ALU.mult, ALU.max).then_inc(lrelu_ok, 1)
                dve.wait_ge(exp_ok, n[c])
                dve.wait_ge(adjT_cur, n[c])
                dve.tensor_tensor(Fp[:, c, :], Fp[:, c, :], ATc[:, c, 0:P], ALU.mult).then_inc(af_ok, 1)
                dve.wait_ge(a1h, n[c])
                dve.tensor_tensor(A1l[:, c, :], Fp[:, c, :], A1h[:, c, :].bitcast(F32), ALU.subtract).then_inc(a1_ok, 1)

            def t3e(c, n):
                dve.wait_ge(t3_ps, n[c])
                dve.reciprocal(col(c, RI), psB[c][:, P:P + 1]).then_inc(ri_ok, 1)
                dve.wait_ge(ri_ok, n[c])
                dve.tensor_tensor(col(c, CI), col(c, RI), ATc[:, c, P:P + 1], ALU.mult)
                dve.wait_ge(t3h, n[c])
                dve.tensor_tensor(Tl[:, c, 0:D], psA[c][:, :], Th[:, c, 0:D].bitcast(F32), ALU.subtract).then_inc(t3_sb, 1)

            def z_second(c, n):
                dve.wait_ge(y3_ps, n[c])
                dve.wait_ge(t3_sb, n[c])
                dve.scalar_tensor_tensor(R[:, c, 0:D], psA[c][:, :], col(c, CI), R[:, c, D:DH], ALU.mult, ALU.add).then_inc(z2, 1)
                dve.wait_ge(z2, n[c + CH])
                stats(c, n, bn3, mv3)

            def x2_norm(c, n):
                dve.wait_ge(rs3, n[c])
                dve.tensor_scalar(R[:, c, 0:D], R[:, c, 0:D], col(c, MV), col(c, RS), ALU.subtract, ALU.mult).then_inc(x2_ok, 1)

            first = [c + 1 for c in range(CH)]
            for step, c in ORDER_PREP:
                if step == "inc":
                    inc(c, first)
                if step == "g":
                    g(c, first)
                if step == "g1":
                    g1(c, first)
            dve.sem_inc(z2, CH)
            dve.wait_ge(wa_sb, 1)
            with dve.Fori(0, iters) as it:
                now = [dve.snap(it * CH + (c + 1)) for c in range(2 * CH)]
                nxt = now[CH:]
                for step, c in ORDER:
                    if step == "inc":
                        inc(c, nxt)
                    if step == "g":
                        g(c, nxt)
                    if step == "g1":
                        g1(c, nxt)
                    if step == "txe":
                        txe(c, now)
                    if step == "st1":
                        st1(c, now)
                    if step == "rsplit":
                        rsplit(c, now)
                    if step == "t2e":
                        t2e(c, now)
                    if step == "z1":
                        z_first(c, now)
                    if step == "x1":
                        x1(c, now)
                    if step == "f":
                        f(c, now)
                    if step == "t3e":
                        t3e(c, now)
                    if step == "z2":
                        z_second(c, now)
                    if step == "x2":
                        x2_norm(c, now)

        @block.tensor
        def _(pe):
            pe.wait_ge(consts_ok, 6)
            pe.wait_ge(vec_in, 6 * 16)

            def products(out, terms, start=True):
                for i, (lhsT, rhs) in enumerate(terms):
                    mm = pe.matmul(out, lhsT, rhs, start=start and i == 0, stop=i == len(terms) - 1)
                return mm

            def three(lh, ll, rh, rl):
                return [(lh, rh), (lh, rl), (ll, rh)]

            def adjT(c, k):
                pe.wait_ge(adj_in[c], k)
                pe.transpose(psB[c][:, 0:P], A[:, c, :], ident[:, :]).then_inc(adjT_ps, 1)

            def deg(c, n):
                pe.wait_ge(hb_sb, n[c])
                products(psB[c][:, P:2 * P], [(col(c, WCOL).to_broadcast([P, P]), HT[:, c, :].bitcast(F32))])
                products(psB[c][:, 2 * P:3 * P], [(HBh[:, c, :], HT[:, c, :]), (HBl[:, c, :], HT[:, c, :])])
                products(psB[c][:, 3 * P:3 * P + 1], [(ATn[:, c, 0:P], ones[:, 0:1])]).then_inc(deg_ps, 1)

            def g1(c, n):
                pe.wait_ge(gt_sb, n[c])
                products(psB[c][:, 3 * P + 2:3 * P + 3], [(GT[:, c, :], ones[:, 0:1])]).then_inc(g1_ps, 1)

            def mix(out, c, h0, k, Gh, Gl):
                for j in range(k):
                    f = slice(h0 + j * P, h0 + (j + 1) * P)
                    mm = products(out[:, j * P:(j + 1) * P], three(Hh[:, c, f], Hl[:, c, f], Gh[:, c, :], Gl[:, c, :]))
                return mm

            def project(out, c, k, Rh, Rl, terms=()):
                terms = list(terms)
                for j in range(k):
                    f = slice(j * P, (j + 1) * P)
                    terms += three(Th[:, c, f], Tl[:, c, f], Rh(j), Rl(j))
                return products(out, terms)

            def tx(c, n):
                pe.wait_ge(gt_sb, n[c])
                pe.wait_ge(xl_ok, n[c])
                pe.wait_ge(z2, n[c])
                mix(psA[c][:, :], c, D, KD, GTh, GTl).then_inc(tx_ps, 1)

            def y1(c, n):
                pe.wait_ge(t1_sb, n[c])
                pe.wait_ge(g1_sb, n[c])
                for half, (ps, ready) in enumerate(((psA, r_psA), (psB, r_psB))):
                    h = slice(half * D, (half + 1) * D)
                    project(ps[c][:, :], c, KD, lambda j: W1h[:, j, h], lambda j: W1l[:, j, h],
                            [(ones_row[:, :], b1_rows[:, h])]).then_inc(ready, 1)

            def t2(c, n):
                pe.wait_ge(g2_ok, n[c])
                mix(psA[c][:, :], c, 0, KD, GTh, GTl).then_inc(t2_psA, 1)
                mix(psB[c][:, :], c, D, KD, GTh, GTl).then_inc(t2_psB, 1)

            def y2(c, n):
                pe.wait_ge(t2_sb, n[c])
                project(psA[c][:, :], c, KH, lambda j: W2h[:, j, :], lambda j: W2l[:, j, :]).then_inc(y2_ps, 1)

            def sbc(c, n, after):
                pe.wait_ge(s_ok, n[c])
                pe.wait_ge(g1_sb, after[c])
                products(psB[c][:, 0:P], [(col(c, S).to_broadcast([P, P]), ident[:, :])]).then_inc(sb_ps, 1)

            def t3(c, n):
                pe.wait_ge(a1_ok, n[c])
                pe.wait_ge(x1l, n[c])
                products(psB[c][:, P:P + 1], [(Fp[:, c, :], ones[:, 0:1])])
                mix(psA[c][:, :], c, 0, KD, A1h, A1l).then_inc(t3_ps, 1)

            def y3(c, n):
                pe.wait_ge(t3_sb, n[c])
                project(psA[c][:, :], c, KD, lambda j: Wh[:, j, :], lambda j: Wl[:, j, :]).then_inc(y3_ps, 1)

            for i in range(4):
                n = first_g + i
                pe.wait_ge(stage_in[n % slots], 16 * (n // slots + 1))
                for k in range(2):
                    mm = pe.matmul(psA[0][:, :], bet[:, 2 * i + k:2 * i + k + 1].to_broadcast([P, P]), stage(n)[:, k, :],
                                   start=(i + k == 0), stop=(i == 3 and k == 1))
                mm.then_inc(v_ps, 1)
            for i in range(2):
                n = len(pieces) + i
                pe.wait_ge(stage_in[n % slots], 16 * (n // slots + 1))
                for k in range(2):
                    mm = pe.matmul(psA[1][:, :], a_col[:, 2 * i + k:2 * i + k + 1].to_broadcast([P, P]), stage(n)[:, k, :],
                                   start=(i + k == 0), stop=(i == 1 and k == 1))
                mm.then_inc(wa_ps, 1)
            first = [c + 1 for c in range(CH)]
            for step, c in ORDER_PREP:
                if step == "adjT":
                    adjT(c, 32)
                if step == "deg":
                    deg(c, first)
                if step == "g1":
                    g1(c, first)
            pe.wait_ge(split_lo, len(pieces))
            pe.wait_ge(rows_ok, 8)
            pe.wait_ge(v_sb, 1)
            pe.wait_ge(wa_sb, 1)
            with pe.Fori(0, iters) as it:
                now = [pe.snap(it * CH + (c + 1)) for c in range(CH)]
                nxt = [pe.snap(it * CH + (CH + c + 1)) for c in range(CH)]
                loaded = pe.snap(it * 32 + 64)
                for step, c in ORDER:
                    if step == "adjT":
                        adjT(c, loaded)
                    if step == "deg":
                        deg(c, nxt)
                    if step == "g1":
                        g1(c, nxt)
                    if step == "tx":
                        tx(c, now)
                    if step == "y1":
                        y1(c, now)
                    if step == "t2":
                        t2(c, now)
                    if step == "y2":
                        y2(c, now)
                    if step == "sb":
                        sbc(c, now, nxt)
                    if step == "t3":
                        t3(c, now)
                    if step == "y3":
                        y3(c, now)


HEADS, DHEAD = 8, 64
HG = HEADS // 2
LA = LD = LG = 0.33
SCALE = DHEAD ** -0.5
MASKED = 2.0 ** 100
OUTSIDE = 2.0 ** 126


def convolutions_and_attention(nc, semaphores, x2, adj, mask_rows, mask_cols, W1, b1, W2, b2, W3, b3, Wqkv, Wout, bout, out):
    tiles = x2.shape[0]
    iters = tiles // CH
    out_rows = out.rearrange("(t g) c d -> t (g c) d", g=P // C)
    adj_t = adj.rearrange("(t g) c e -> t g c e", g=P // C)

    with ExitStack() as ctx:
        def sb(name, shape, dt=F32):
            return ctx.enter_context(nc.sbuf_tensor(name, shape, dt))

        def sem(name):
            semaphores.append(nc.alloc_semaphore(name))
            return semaphores[-1]

        GW = [(sb(f"GW{i}h", [P, KD, D], F32R), sb(f"GW{i}l", [P, KD, D], F32R)) for i in range(3)]
        WQh, WQl = sb("WQh", [P, KD, 3, D], F32R), sb("WQl", [P, KD, 3, D], F32R)
        WOh, WOl = sb("WOh", [P, KD, D], F32R), sb("WOl", [P, KD, D], F32R)
        ident = sb("ident2", [P, P])
        identr = sb("identr", [P, P], F32R)
        ones_row = sb("ones_row2", [P, P], F32R)
        rows = sb("rows", [P, D], F32R)
        inside = sb("inside", [P, P])
        outside = sb("outside", [P, P])
        mhalf = sb("mhalf2", [P, 1])
        A = sb("A2", [P, CH, P])
        ATh, ATl = sb("ATh", [P, CH, P], F32R), sb("ATl", [P, CH, P], F32R)
        mrow = sb("mrow", [P, CH, P], U8)
        mcol = sb("mcol", [P, CH, 4], U8)
        MM, BT = sb("MM", [P, P]), sb("BT", [P, P])
        BS = sb("BS", [P, CH, P], F32R)
        Cm = sb("Cm", [P, CH, P])
        X = sb("X2", [P, CH, D])
        Hh, Hl = sb("H2h", [P, CH, D], F32R), sb("H2l", [P, CH, D], F32R)
        Th, Tl = sb("T2h", [P, KD, CH * P], F32R), sb("T2l", [P, KD, CH * P], F32R)
        QKh, QKl = sb("QKh", [P, 2 * KD, 2 * P], F32R), sb("QKl", [P, 2 * KD, 2 * P], F32R)
        E = sb("E", [P, 2, HEADS, P])
        AAh, AAl = sb("AAh", [P, HEADS, P], F32R), sb("AAl", [P, HEADS, P], F32R)
        Z = sb("Z", [P, 2, D])
        sm = sb("sm2", [P, CH, 64])
        MC, VE, RS = range(3)
        MV, BN, NMX, NB, SUM, REC, RLA = 4, 8, 16, 24, 32, 40, 48

        def col(c, k, n=1):
            return sm[:, c, k:k + n]

        psA = [ctx.enter_context(nc.psum_tensor(f"qsA{c}", [P, D], F32)) for c in range(CH)]
        psB = [ctx.enter_context(nc.psum_tensor(f"qsB{c}", [P, D], F32)) for c in range(CH)]

        consts_ok, ident0, blocks0, rows_in, rows_ok, split_hi, split_lo = map(sem, (
            "consts_ok2", "ident02", "blocks0", "rows_in", "rows_ok2", "split_hi2", "split_lo2"))
        slots = 3
        stage_in = [sem(f"stage2_in{i}") for i in range(slots)]
        adj_in = [sem(f"adj2_in{c}") for c in range(CH)]
        x_in = [sem(f"x2_in{c}") for c in range(CH)]
        out_stored = [sem(f"out_stored{i}") for i in range(2)]
        qk_ps, qkh, qk_sb = ([sem(f"{n}{b}") for b in range(4)] for n in ("qk_ps", "qkh", "qk_sb"))
        t_ps, th, t_sb, g_ps, gh, g_sb = ([sem(f"{n}{i}") for i in range(3)] for n in ("t_ps", "th", "t_sb", "g_ps", "gh", "g_sb"))
        (adjT_ps, ath, at_sb, xh_ok, xl_ok, mc_ok, mm_ok, bt1, bt2, bs_ok, mm2, exp_adj, cm1, bt3, cm2, cm_ok, z3, bn3, mv3,
         ve3, rs3, x3_ok, xp_ps, xph, xp_sb, v_ps, vh, v_sb, s_psA, s_psB, max_ok, nb_ok, ex_ok, rec_ok, rla_ok, attn_ok,
         ta_psA, ta_psB, taA, taB, ta_sb, av_psA, av_psB, avA, avB, av_sb, wo_ps, z4, bn4, mv4, ve4, rs4, x4_ok) = map(sem, (
            "adjT_ps2 ath at_sb xh_ok2 xl_ok2 mc_ok mm_ok bt1 bt2 bs_ok mm2 exp_adj cm1 bt3 cm2 cm_ok z3 bn3_2 mv3_2 "
            "ve3_2 rs3_2 x3_ok xp_ps xph xp_sb v_ps2 vh v_sb2 s_psA s_psB max_ok nb_ok ex_ok rec_ok rla_ok attn_ok "
            "ta_psA ta_psB taA taB ta_sb av_psA av_psB avA avB av_sb wo_ps z4 bn4 mv4 ve4 rs4 x4_ok").split())

        BIASES = (b1, b2, b3, bout)
        raw = Z[:, 0, :]

        def chunks(W):
            return W.rearrange("(k p) n -> p k n", p=P)

        pieces = [(chunks(W)[:, k:k + 2, :], h[:, k:k + 2, :], l[:, k:k + 2, :])
                  for W, (h, l) in zip((W1, W2, W3, Wout), GW + [(WOh, WOl)]) for k in (0, 2)]
        for k in range(KD):
            for half in range(2):
                src = chunks(Wqkv)[:, k, half * 3 * D // 2:(half + 1) * 3 * D // 2].rearrange("p (h i d) -> p h i d", i=3, d=DHEAD)
                dst = [W[:, k, :, half * D // 2:(half + 1) * D // 2].rearrange("p i (h d) -> p h i d", d=DHEAD) for W in (WQh, WQl)]
                pieces.append((src, *dst))

        def stage(n):
            s = Z[:, :, :].rearrange("p a b -> p (a b)") if n % slots == 2 else E[:, n % slots, :, :].rearrange("p h j -> p (h j)")
            if n < 8:
                return s.rearrange("p (k n) -> p k n", k=2)
            return s[:, 0:3 * D // 2].rearrange("p (h i d) -> p h i d", i=3, d=DHEAD)

        ORDER_PREP = rounds([("adjT", 0), ("xsplit", 0)], CH)
        ORDER = (
            rounds([("t0", 0), ("cm", 0)], CH) + rounds([("g0", 0)], CH)
            + rounds([("t1", 0)], CH) + rounds([("g1", 0)], CH)
            + rounds([("t2", 0)], CH) + rounds([("g2", 0), ("z3", 0), ("rs3", 0), ("x3", 1), ("xp", 2)], CH)
            + rounds([("v", 0)], CH)
            + [("qk", 0), ("s", 0), ("s", 1), ("sm", 0), ("sm", 1), ("qk", 1), ("ta", 0), ("av", 0), ("ta", 1), ("av", 1), ("s", 2), ("s", 3),
               ("sm", 2), ("wo", 0), ("z4", 0), ("rs4", 0), ("adjT", 0), ("sm", 3), ("x4", 0), ("xsplit", 0),
               ("wo", 1), ("z4", 1), ("rs4", 1), ("adjT", 1), ("ta", 2), ("av", 2), ("x4", 1), ("xsplit", 1), ("ta", 3), ("av", 3),
               ("wo", 2), ("z4", 2), ("rs4", 2), ("adjT", 2), ("x4", 2), ("xsplit", 2),
               ("wo", 3), ("z4", 3), ("rs4", 3), ("adjT", 3), ("x4", 3), ("xsplit", 3)])
        block = ctx.enter_context(nc.Block())

        @block.sync
        def _(sp):
            def load(c, tile):
                for g in range(P // C):
                    sp.dma_start(A[g * C:(g + 1) * C, c, g * C:(g + 1) * C],
                                 adj_t[bass.ds(tile, 1), g].rearrange("a c e -> (a c) e")).then_inc(adj_in[c], 16)
                sp.dma_start(mrow[:, c, :], mask_rows[bass.ds(tile, 1)].rearrange("a j -> (a j)").partition_broadcast(P))\
                    .then_inc(adj_in[c], 16)
                sp.dma_start(mcol[:, c, 0:1], mask_cols[:, bass.ds(tile, 1)], allow_slow_non_contiguous=True).then_inc(adj_in[c], 16)

            def load_x(c, tile):
                sp.dma_start(X[:, c, :], x2[bass.ds(tile, 1)].rearrange("a r d -> (a r) d")).then_inc(x_in[c], 16)

            for i, b in enumerate(BIASES):
                sp.dma_start(raw[32 * i:32 * i + 2, :], b.partition_broadcast(2)).then_inc(rows_in, 16)
            for n, (src, _, _) in enumerate(pieces):
                if n == 2:
                    sp.wait_ge(rows_ok, 4 * len(BIASES))
                if n >= slots:
                    sp.wait_ge(split_lo, n - slots + 1)
                sp.dma_start(stage(n), src).then_inc(stage_in[n % slots], 16)
                if n == 1:
                    sp.wait_ge(consts_ok, 7)
                    for c in range(CH):
                        load(c, c)
                        load_x(c, c)
            for i in range(2):
                sp.sem_inc(out_stored[i], 16)
            with sp.Fori(0, iters) as it:
                nxt = sp.snap(((it + 1) % iters) * CH)
                t0 = sp.snap(it * CH)
                now = [sp.snap(t0 + (c + 1)) for c in range(CH)]
                for c in range(CH):
                    sp.wait_ge(adjT_ps, now[c])
                    sp.wait_ge(cm_ok, now[c])
                    load(c, nxt + c)
                for c in range(CH):
                    sp.wait_ge(z4, now[c])
                    load_x(c, nxt + c)
                    if c:
                        store(c - 1)
                    def store(c):
                        sp.wait_ge(x4_ok, now[c])
                        sp.dma_start(out_rows[bass.ds(t0 + c, 1)].rearrange("a r d -> (a r) d"), Z[:, c % 2, :])\
                            .then_inc(out_stored[c % 2], 16)
                store(CH - 1)
            for c in range(CH):
                sp.wait_ge(x_in[c], 16 * (iters + 1))
                sp.wait_ge(adj_in[c], 64 * (iters + 1))
            for i in range(2):
                sp.wait_ge(out_stored[i], 16 * (iters * CH // 2 + 1))

        @block.gpsimd
        def _(pool):
            pool.memset(ident[:, :], 0.0).then_inc(ident0, 1)
            pool.wait_ge(ident0, 1)
            pool.affine_select(out=ident[:, :], in_=ident[:, :], compare_op=ALU.not_equal, fill=1.0, base=0,
                               pattern=[[-1, P]], channel_multiplier=1).then_inc(consts_ok, 1)
            pool.memset(ones_row[:, :].bitcast(F32), 1.0).then_inc(consts_ok, 1)
            pool.memset(mhalf[:, :], -0.5).then_inc(consts_ok, 1)
            pool.memset(A[:, :, :], 0.0).then_inc(consts_ok, 1)
            pool.memset(inside[:, :], 0.0).then_inc(blocks0, 1)
            pool.memset(outside[:, :], -OUTSIDE).then_inc(blocks0, 1)
            pool.wait_ge(blocks0, 2)
            for g in range(P // C):
                b = slice(g * C, (g + 1) * C)
                pool.memset(inside[b, b], 1.0)
                pool.memset(outside[b, b], 0.0).then_inc(consts_ok, 1)
            pool.wait_ge(consts_ok, 6)
            pool.tensor_copy(identr[:, :], ident[:, :]).then_inc(consts_ok, 1)

            def alone(sem, value):
                pool.wait_ge(blocks0, 2)
                pool.wait_ge(sem, value)

            def rstd(c, n, mv, ve):
                alone(mv, n[c])
                pool.tensor_scalar(col(c, VE), col(c, MV + 1), EPS, None, ALU.add).then_inc(ve, 1)
                pool.wait_ge(ve, n[c])
                return pool.tensor_tensor(col(c, RS), col(c, VE), mhalf[:, :], ALU.pow)

            def xsplit(c, n):
                pool.wait_ge(xh_ok, n[c])
                pool.tensor_tensor(Hl[:, c, :], X[:, c, :], Hh[:, c, :].bitcast(F32), ALU.subtract).then_inc(xl_ok, 1)

            def cm(c, n, loaded):
                alone(adj_in[c], loaded)
                pool.tensor_copy(col(c, MC), mcol[:, c, 0:1]).then_inc(mc_ok, 1)
                alone(mc_ok, n[c])
                pool.tensor_scalar(MM[:, :], mrow[:, c, :], col(c, MC), None, ALU.mult).then_inc(mm_ok, 1)
                alone(mm_ok, n[c])
                pool.tensor_scalar(BT[:, :], MM[:, :], MASKED, -MASKED, ALU.mult, ALU.add).then_inc(bt1, 1)
                pool.wait_ge(bt1, n[c])
                pool.tensor_tensor(BT[:, :], BT[:, :], inside[:, :], ALU.mult).then_inc(bt2, 1)
                pool.tensor_tensor(MM[:, :], MM[:, :], inside[:, :], ALU.mult).then_inc(mm2, 1)
                pool.wait_ge(bt2, n[c])
                pool.tensor_tensor(BS[:, c, :], BT[:, :], outside[:, :], ALU.add).then_inc(bs_ok, 1)
                alone(exp_adj, n[c])
                pool.tensor_scalar(Cm[:, c, :], Cm[:, c, :], LD, None, ALU.mult).then_inc(cm1, 1)
                alone(bs_ok, n[c])
                pool.tensor_scalar(BT[:, :], A[:, c, :], LG, None, ALU.mult).then_inc(bt3, 1)
                pool.wait_ge(bt3, n[c])
                pool.tensor_tensor(Cm[:, c, :], Cm[:, c, :], BT[:, :], ALU.add).then_inc(cm2, 1)
                pool.wait_ge(cm2, n[c])
                pool.tensor_tensor(Cm[:, c, :], Cm[:, c, :], MM[:, :], ALU.mult).then_inc(cm_ok, 1)

            first = [c + 1 for c in range(CH)]
            for step, c in ORDER_PREP:
                if step == "xsplit":
                    xsplit(c, first)
            with pool.Fori(0, iters) as it:
                now = [pool.to_reg(it * CH + (c + 1)) for c in range(CH)]
                nxt = [pool.to_reg(it * CH + (CH + c + 1)) for c in range(CH)]
                loaded = pool.to_reg(it * 64 + 64)
                for step, c in ORDER:
                    if step == "cm":
                        cm(c, now, loaded)
                    if step == "rs3":
                        rstd(c, now, mv3, ve3).then_inc(rs3, 1)
                    if step == "rs4":
                        rstd(c, now, mv4, ve4).then_inc(rs4, 1)
                    if step == "xsplit":
                        xsplit(c, nxt)

        def T(W, c):
            return W[:, :, c * P:(c + 1) * P]

        def by_chunk(ps):
            return ps[:, :].rearrange("p (k j) -> p k j", k=KD)

        def pair_out(W, p, b):
            return W[:, 2 * b:2 * b + 2, :]

        def bank(p, b):
            return (psA, psB)[b % 2][2 * p + b // 2]

        def pair_of(W, m):
            return W[:, :, :].rearrange("p (b m) j -> p b m j", b=2)[:, :, m, :]

        @block.scalar
        def _(act):
            act.wait_ge(rows_in, 16 * len(BIASES))
            for i in range(len(BIASES)):
                q = slice(32 * i, 32 * i + 2)
                act.copy(rows[q, :], raw[q, :]).then_inc(rows_ok, 1)
            for n, (_, hi, _) in enumerate(pieces):
                act.wait_ge(stage_in[n % slots], 16 * (n // slots + 1))
                act.copy(hi, stage(n)).then_inc(split_hi, 1)

            def adjT(c, n):
                act.wait_ge(adjT_ps, n[c])
                act.copy(ATh[:, c, :], psB[c][:, 0:P]).then_inc(ath, 1)

            def xsplit(c, k):
                act.wait_ge(x_in[c], k)
                act.copy(Hh[:, c, :], X[:, c, :]).then_inc(xh_ok, 1)

            first = [c + 1 for c in range(CH)]
            for step, c in ORDER_PREP:
                if step == "adjT":
                    adjT(c, first)
                if step == "xsplit":
                    xsplit(c, 16)
            with act.Fori(0, iters) as it:
                n = [act.to_reg(it * CH + (c + 1)) for c in range(CH)]
                nxt = [act.to_reg(it * CH + (CH + c + 1)) for c in range(CH)]
                pair = [act.to_reg(it * 2 + (p + 1)) for p in range(2)]
                loaded, adj_loaded = act.to_reg(it * 16 + 32), act.to_reg(it * 64 + 64)
                for step, c in ORDER:
                    if step in ("t0", "t1", "t2"):
                        i = int(step[1])
                        act.wait_ge(t_ps[i], n[c])
                        act.copy(T(Th, c), by_chunk(psA[c])).then_inc(th[i], 1)
                    if step in ("g0", "g1"):
                        i = int(step[1])
                        act.wait_ge(g_ps[i], n[c])
                        act.activation(Hh[:, c, :], psB[c][:, :], ACT.Relu).then_inc(gh[i], 1)
                    if step == "cm":
                        act.wait_ge(adj_in[c], adj_loaded)
                        act.activation(Cm[:, c, :], A[:, c, :], ACT.Exp, scale=-1.0).then_inc(exp_adj, 1)
                    if step == "xp":
                        act.wait_ge(xp_ps, n[c])
                        act.copy(T(Th, c), by_chunk(psA[c])).then_inc(xph, 1)
                    if step == "v":
                        act.wait_ge(v_ps, n[c])
                        act.copy(Hh[:, c, :], psB[c][:, :]).then_inc(vh, 1)
                    if step == "qk":
                        for b in range(4):
                            act.wait_ge(qk_ps[b], pair[c])
                            act.copy(pair_out(QKh, c, b), bank(c, b)[:, :].rearrange("p (k j) -> p k j", k=2)).then_inc(qkh[b], 1)
                    if step == "sm":
                        act.wait_ge(nb_ok, n[c])
                        for h in range(HEADS):
                            ps = (psA, psB)[h // HG][c]
                            last = act.activation(E[:, c % 2, h, :], ps[:, h % HG * P:(h % HG + 1) * P], ACT.Exp,
                                                  bias=col(c, NB + h), scale=SCALE, accum_out=col(c, SUM + h))
                        last.then_inc(ex_ok, 1)
                    if step == "ta":
                        act.wait_ge(ta_psA, n[c])
                        act.copy(AAh[:, 0:HG, :], by_chunk(psA[c])).then_inc(taA, 1)
                        act.wait_ge(ta_psB, n[c])
                        act.copy(AAh[:, HG:HEADS, :], by_chunk(psB[c])).then_inc(taB, 1)
                    if step == "av":
                        for b, (ps, ready, done) in enumerate(((psA, av_psA, avA), (psB, av_psB, avB))):
                            act.wait_ge(ready, n[c])
                            for s in range(2):
                                q = slice(s * DHEAD, (s + 1) * DHEAD)
                                last = act.copy(T(Th, c)[q, 2 * b:2 * b + 2, :],
                                                ps[c][q, :].rearrange("p (m s j) -> p m s j", m=2, s=2)[:, :, s, :])
                            last.then_inc(done, 1)
                    if step == "adjT":
                        adjT(c, nxt)
                    if step == "xsplit":
                        xsplit(c, loaded)

        @block.vector
        def _(dve):
            dve.wait_ge(consts_ok, 7)
            for i in range(len(BIASES)):
                q = slice(32 * i, 32 * i + 2)
                hi, lo = rows[q, :], raw[q, :]
                dve.wait_ge(rows_ok, 4 + 3 * i)
                dve.tensor_tensor(lo, lo, hi.bitcast(F32), ALU.subtract).then_inc(rows_ok, 1)
                dve.wait_ge(rows_ok, 5 + 3 * i)
                dve.tensor_scalar(lo, lo, ident[q, 32 * i + 1:32 * i + 2], None, ALU.mult).then_inc(rows_ok, 1)
                dve.wait_ge(rows_ok, 6 + 3 * i)
                dve.scalar_tensor_tensor(hi, hi.bitcast(F32), ident[q, 32 * i:32 * i + 1], lo, ALU.mult, ALU.add).then_inc(rows_ok, 1)
            for n, (_, hi, lo) in enumerate(pieces):
                dve.wait_ge(split_hi, n + 1)
                dve.tensor_tensor(lo, stage(n), hi.bitcast(F32), ALU.subtract).then_inc(split_lo, 1)

            def alone(sem, value):
                dve.wait_ge(blocks0, 2)
                dve.wait_ge(sem, value)

            def rest(lo, ps, hi):
                return dve.tensor_tensor(lo, ps, hi.bitcast(F32), ALU.subtract)

            def adjT(c, n):
                dve.wait_ge(ath, n[c])
                rest(ATl[:, c, :], psB[c][:, 0:P], ATh[:, c, :]).then_inc(at_sb, 1)

            def stats(src, c, n, bn, mv):
                dve.bn_stats(col(c, BN, 6), src).then_inc(bn, 1)
                alone(bn, n[c])
                dve.bn_aggr(col(c, MV, 2), col(c, BN, 6)).then_inc(mv, 1)

            first = [c + 1 for c in range(CH)]
            for step, c in ORDER_PREP:
                if step == "adjT":
                    adjT(c, first)
            with dve.Fori(0, iters) as it:
                n = [dve.to_reg(it * CH + (c + 1)) for c in range(CH)]
                nxt = [dve.to_reg(it * CH + (CH + c + 1)) for c in range(CH)]
                pair = [dve.to_reg(it * 2 + (p + 1)) for p in range(2)]
                stored = [dve.to_reg(it * 32 + 16 * (r + 1)) for r in range(2)]
                for step, c in ORDER:
                    if step in ("t0", "t1", "t2"):
                        i = int(step[1])
                        dve.wait_ge(th[i], n[c])
                        rest(T(Tl, c), by_chunk(psA[c]), T(Th, c)).then_inc(t_sb[i], 1)
                    if step in ("g0", "g1"):
                        i = int(step[1])
                        dve.wait_ge(gh[i], n[c])
                        dve.scalar_tensor_tensor(Hl[:, c, :], psB[c][:, :], 0.0, Hh[:, c, :].bitcast(F32), ALU.max, ALU.subtract)\
                            .then_inc(g_sb[i], 1)
                    if step == "z3":
                        dve.wait_ge(g_ps[2], n[c])
                        dve.tensor_tensor(X[:, c, :], psB[c][:, :], X[:, c, :], ALU.add).then_inc(z3, 1)
                        dve.wait_ge(z3, n[c])
                        stats(X[:, c, :], c, n, bn3, mv3)
                    if step == "x3":
                        dve.wait_ge(rs3, n[c])
                        dve.tensor_scalar(X[:, c, :], X[:, c, :], col(c, MV), col(c, RS), ALU.subtract, ALU.mult).then_inc(x3_ok, 1)
                    if step == "xp":
                        dve.wait_ge(xph, n[c])
                        rest(T(Tl, c), by_chunk(psA[c]), T(Th, c)).then_inc(xp_sb, 1)
                    if step == "v":
                        dve.wait_ge(vh, n[c])
                        rest(Hl[:, c, :], psB[c][:, :], Hh[:, c, :]).then_inc(v_sb, 1)
                    if step == "qk":
                        for b in range(4):
                            dve.wait_ge(qkh[b], pair[c])
                            rest(pair_out(QKl, c, b), bank(c, b)[:, :].rearrange("p (k j) -> p k j", k=2), pair_out(QKh, c, b))\
                                .then_inc(qk_sb[b], 1)
                    if step == "s":
                        dve.wait_ge(s_psA, n[c])
                        dve.reduce_max(col(c, NMX, HG), by_chunk(psA[c]), AX.X)
                        dve.wait_ge(s_psB, n[c])
                        dve.reduce_max(col(c, NMX + HG, HG), by_chunk(psB[c]), AX.X).then_inc(max_ok, 1)
                        dve.wait_ge(max_ok, n[c])
                        dve.tensor_scalar(col(c, NB, HEADS), col(c, NMX, HEADS), -SCALE, None, ALU.mult).then_inc(nb_ok, 1)
                    if step == "sm":
                        dve.wait_ge(ex_ok, n[c])
                        dve.reciprocal(col(c, REC, HEADS), col(c, SUM, HEADS)).then_inc(rec_ok, 1)
                        dve.wait_ge(rec_ok, n[c])
                        dve.tensor_scalar(col(c, RLA, HEADS), col(c, REC, HEADS), LA, None, ALU.mult).then_inc(rla_ok, 1)
                        dve.wait_ge(rla_ok, n[c])
                        dve.wait_ge(cm_ok, n[c])
                        for h in range(HEADS):
                            last = dve.scalar_tensor_tensor(E[:, c % 2, h, :], E[:, c % 2, h, :], col(c, RLA + h), Cm[:, c, :],
                                                            ALU.mult, ALU.add)
                        last.then_inc(attn_ok, 1)
                    if step == "ta":
                        dve.wait_ge(taA, n[c])
                        rest(AAl[:, 0:HG, :], by_chunk(psA[c]), AAh[:, 0:HG, :])
                        dve.wait_ge(taB, n[c])
                        rest(AAl[:, HG:HEADS, :], by_chunk(psB[c]), AAh[:, HG:HEADS, :]).then_inc(ta_sb, 1)
                    if step == "av":
                        for b, (ps, ready) in enumerate(((psA, avA), (psB, avB))):
                            dve.wait_ge(ready, n[c])
                            for s in range(2):
                                q = slice(s * DHEAD, (s + 1) * DHEAD)
                                last = rest(T(Tl, c)[q, 2 * b:2 * b + 2, :],
                                            ps[c][q, :].rearrange("p (m s j) -> p m s j", m=2, s=2)[:, :, s, :],
                                            T(Th, c)[q, 2 * b:2 * b + 2, :])
                        last.then_inc(av_sb, 1)
                    if step == "z4":
                        dve.wait_ge(wo_ps, n[c])
                        dve.wait_ge(out_stored[c % 2], stored[c // 2])
                        dve.tensor_tensor(Z[:, c % 2, :], psA[c][:, :], X[:, c, :], ALU.add).then_inc(z4, 1)
                        dve.wait_ge(z4, n[c])
                        stats(Z[:, c % 2, :], c, n, bn4, mv4)
                    if step == "x4":
                        dve.wait_ge(rs4, n[c])
                        dve.tensor_scalar(Z[:, c % 2, :], Z[:, c % 2, :], col(c, MV), col(c, RS), ALU.subtract, ALU.mult)\
                            .then_inc(x4_ok, 1)
                    if step == "adjT":
                        adjT(c, nxt)

        @block.tensor
        def _(pe):
            pe.wait_ge(consts_ok, 7)

            def products(out, terms):
                for i, (lhsT, rhs) in enumerate(terms):
                    mm = pe.matmul(out, lhsT, rhs, start=i == 0, stop=i == len(terms) - 1)
                return mm

            def three(lh, ll, rh, rl):
                return [(lh, rh), (lh, rl), (ll, rh)]

            def bias(i):
                return [(ones_row[32 * i:32 * i + 2, :], rows[32 * i:32 * i + 2, :])]

            def project(out, c, W, terms=()):
                terms = list(terms)
                for k in range(KD):
                    terms += three(T(Th, c)[:, k, :], T(Tl, c)[:, k, :], W[0][:, k, :], W[1][:, k, :])
                return products(out, terms)

            def adjT(c, k):
                pe.wait_ge(adj_in[c], k)
                pe.transpose(psB[c][:, 0:P], A[:, c, :], ident[:, :]).then_inc(adjT_ps, 1)

            for step, c in ORDER_PREP:
                if step == "adjT":
                    adjT(c, 64)
            pe.wait_ge(split_lo, len(pieces))
            pe.wait_ge(rows_ok, 4 * len(BIASES))
            with pe.Fori(0, iters) as it:
                n = [pe.to_reg(it * CH + (c + 1)) for c in range(CH)]
                pair = [pe.to_reg(it * 2 + (p + 1)) for p in range(2)]
                loaded = pe.to_reg(it * 64 + 128)
                for step, c in ORDER:
                    if step in ("t0", "t1", "t2"):
                        i = int(step[1])
                        if i == 0:
                            pe.wait_ge(at_sb, n[c])
                            pe.wait_ge(xl_ok, n[c])
                        else:
                            pe.wait_ge(g_sb[i - 1], n[c])
                        for k in range(KD):
                            f = slice(k * P, (k + 1) * P)
                            mm = products(psA[c][:, f], three(Hh[:, c, f], Hl[:, c, f], ATh[:, c, :], ATl[:, c, :]))
                        mm.then_inc(t_ps[i], 1)
                    if step in ("g0", "g1", "g2"):
                        i = int(step[1])
                        pe.wait_ge(t_sb[i], n[c])
                        project(psB[c][:, :], c, GW[i], bias(i)).then_inc(g_ps[i], 1)
                    if step == "xp":
                        pe.wait_ge(x3_ok, n[c])
                        for k in range(KD):
                            mm = pe.transpose(psA[c][:, k * P:(k + 1) * P], X[:, c, k * P:(k + 1) * P], ident[:, :])
                        mm.then_inc(xp_ps, 1)
                    if step == "v":
                        pe.wait_ge(xp_sb, n[c])
                        project(psB[c][:, :], c, (WQh[:, :, 2, :], WQl[:, :, 2, :])).then_inc(v_ps, 1)
                    if step == "qk":
                        pe.wait_ge(v_sb, n[2 * c + 1])
                        cols = slice(2 * c * P, (2 * c + 2) * P)
                        for b in range(4):
                            for m in range(2):
                                i, f = divmod((2 * b + m) * P, D)
                                terms = []
                                for k in range(KD):
                                    terms += three(WQh[:, k, i, f:f + P], WQl[:, k, i, f:f + P], Th[:, k, cols], Tl[:, k, cols])
                                mm = products(bank(c, b)[:, m * 2 * P:(m + 1) * 2 * P], terms)
                            mm.then_inc(qk_ps[b], 1)
                    if step == "s":
                        if c % 2 == 0:
                            for b in range(4):
                                pe.wait_ge(qk_sb[b], pair[c // 2])
                        pe.wait_ge(bs_ok, n[c])
                        rows_c = slice(c % 2 * P, (c % 2 + 1) * P)
                        for ps in (psA, psB):
                            pe.matmul(ps[c][:, :], identr[:, :], BS[:, c, :].unsqueeze(1).to_broadcast([P, HG, P]), start=True, stop=False)
                        for m in range(HG):
                            for j in range(3):
                                for odd, (ps, ready) in enumerate(((psA, s_psA), (psB, s_psB))):
                                    q = slice(odd * DHEAD, (odd + 1) * DHEAD)
                                    terms = three(*(W[q, i * KD + m, rows_c] for i in range(2) for W in (QKh, QKl)))
                                    mm = pe.matmul(ps[c][:, m * P:(m + 1) * P], *terms[j], start=False, stop=m == HG - 1 and j == 2)
                                    if m == HG - 1 and j == 2:
                                        mm.then_inc(ready, 1)
                    if step == "ta":
                        pe.wait_ge(attn_ok, n[c])
                        for ps, h0, ready in ((psA, 0, ta_psA), (psB, HG, ta_psB)):
                            for h in range(h0, h0 + HG):
                                mm = pe.transpose(ps[c][:, (h - h0) * P:(h - h0 + 1) * P], E[:, c % 2, h, :], ident[:, :])
                            mm.then_inc(ready, 1)
                    if step == "av":
                        pe.wait_ge(ta_sb, n[c])
                        for m in range(HG):
                            ps, ready = ((psA, av_psA), (psB, av_psB))[m // 2]
                            f = slice(m * P, (m + 1) * P)
                            mm = products(ps[c][:, m % 2 * 2 * P:(m % 2 + 1) * 2 * P],
                                          three(Hh[:, c, f], Hl[:, c, f], pair_of(AAh, m), pair_of(AAl, m)))
                            if m % 2:
                                mm.then_inc(ready, 1)
                    if step == "wo":
                        pe.wait_ge(av_sb, n[c])
                        project(psA[c][:, :], c, (WOh, WOl), bias(3)).then_inc(wo_ps, 1)
                    if step == "adjT":
                        adjT(c, loaded)


def kernel(**inputs):
    import numpy as np
    import concourse.bacc as bacc
    from concourse.bass_utils import run_bass_kernel_spmd

    nc = bacc.Bacc("TRN2", target_bir_lowering=False, num_devices=1)
    given = {k: np.asarray(v) for k, v in inputs.items()}
    n, c, d = given["x"].shape
    tiles = n * c // P
    mask = given["nodemask"].reshape(tiles, P)
    arrays = {
        "x": given["x"], "adj": given["adj"], "mask_rows": mask, "mask_cols": mask.T,
        "L0_W1T": given["L0_gnn_W1"].T, "L0_b1": given["L0_gnn_b1"], "L0_gamma": given["L0_gnn_gamma"],
        "L0_beta": given["L0_gnn_beta"], "L0_W2T": given["L0_gnn_W2"].T, "L0_b2": given["L0_gnn_b2"],
        "L1_w": given["L1_gnn_w"], "L1_wT": given["L1_gnn_w"].T, "L1_a": given["L1_gnn_a"],
        "L2_W1": given["L2_gnn_W1"], "L2_b1": given["L2_gnn_b1"], "L2_W2": given["L2_gnn_W2"], "L2_b2": given["L2_gnn_b2"],
        "L2_W3": given["L2_gnn_W3"], "L2_b3": given["L2_gnn_b3"],
        "L3_Wqkv": given["L3_gnn_W_qkv"], "L3_Wout": given["L3_gnn_W_out"], "L3_bout": given["L3_gnn_b_out"],
    }
    arrays = {k: np.ascontiguousarray(v) for k, v in arrays.items()}
    ap = {k: nc.dram_tensor("in_" + k, v.shape, mybir.dt.from_np(v.dtype), kind="ExternalInput").ap() for k, v in arrays.items()}
    out = nc.dram_tensor("out", (n, c, d), F32, kind="ExternalOutput").ap()
    x2 = nc.dram_tensor("x2", (tiles, P, d), F32, kind="Internal").ap()
    semaphores = []
    hypergraph_and_pairwise(nc, semaphores, ap["x"], ap["adj"], ap["L0_W1T"], ap["L0_b1"], ap["L0_gamma"], ap["L0_beta"],
                            ap["L0_W2T"], ap["L0_b2"], ap["L1_w"], ap["L1_wT"], ap["L1_a"], x2)
    nc.clear_and_free_semaphores(semaphores)
    nc.all_engine_barrier()
    convolutions_and_attention(nc, [], x2, ap["adj"], ap["mask_rows"], ap["mask_cols"], ap["L2_W1"], ap["L2_b1"],
                               ap["L2_W2"], ap["L2_b2"], ap["L2_W3"], ap["L2_b3"], ap["L3_Wqkv"], ap["L3_Wout"],
                               ap["L3_bout"], out)
    r = run_bass_kernel_spmd(nc, [{"in_" + k: v for k, v in arrays.items()}], core_ids=[0])
    return r.results[0]["out"]
```

```python
from contextlib import ExitStack

import concourse.bass as bass
from concourse import mybir
from concourse.alu_op_type import AluOpType as ALU

F32 = mybir.dt.float32
F32R = mybir.dt.float32r
U8 = mybir.dt.uint8
ACT = mybir.ActivationFunctionType
AX = mybir.AxisListType

P = 128
C = 64
D = 512
DH = 1024
CH = 4
EPS = 1e-5
TINY = 1.2e-38
KD, KH = D // P, DH // P


def rounds(steps, chains):
    last = max(o for _, o in steps)
    return [(name, r - o) for r in range(chains + last) for name, o in steps if 0 <= r - o < chains]


def order(text):
    return [(step, int(chain)) for step, chain in (entry.split(".") for entry in text.split())]


def hypergraph_and_pairwise(nc, semaphores, x, adj, W1T, b1, gamma, beta, W2T, b2, w, wT, a, x2):
    tiles = x.shape[0] * x.shape[1] // P
    iters = tiles // CH
    x_rows = x.rearrange("(t g) c d -> t (g c) d", g=P // C)
    adj_t = adj.rearrange("(t g) c e -> t g c e", g=P // C)

    with ExitStack() as ctx:
        def sb(name, shape, dt=F32):
            return ctx.enter_context(nc.sbuf_tensor(name, shape, dt))

        def sem(name):
            semaphores.append(nc.alloc_semaphore(name))
            return semaphores[-1]

        W1h, W1l = sb("W1h", [P, KD, DH], F32R), sb("W1l", [P, KD, DH], F32R)
        W2h, W2l = sb("W2h", [P, KH, D], F32R), sb("W2l", [P, KH, D], F32R)
        Wh, Wl = sb("Wh", [P, KD, D], F32R), sb("Wl", [P, KD, D], F32R)
        ident = sb("ident", [P, P])
        ones = sb("ones", [P, 2])
        ones_row = sb("ones_row", [2, P], F32R)
        b1_rows = sb("b1_rows", [2, DH], F32R)
        b2_all = sb("b2_all", [P, D])
        v_all = sb("v_all", [P, D])
        wa_all = sb("wa_all", [P, D])
        ubias = sb("ubias", [P, CH, D])
        gam = sb("gam", [P, KH])
        bet = sb("bet", [P, KH])
        a_col = sb("a_col", [P, KD])
        mhalf = sb("mhalf", [P, 1])
        A = sb("A", [P, CH, P])
        ATn = sb("ATn", [P, CH, P + 1])
        ATc = sb("ATc", [P, CH, P + 1])
        HT = sb("HT", [P, CH, P], F32R)
        HBh, HBl = sb("HBh", [P, CH, P], F32R), sb("HBl", [P, CH, P], F32R)
        DI = sb("DI", [P, CH, P])
        GT = sb("GT", [P, CH, P])
        Fp = sb("Fp", [P, CH, P])
        X = sb("X", [P, CH, D])
        Th, Tl = sb("Th", [P, CH, DH], F32R), sb("Tl", [P, CH, DH], F32R)
        R = sb("R", [P, CH, DH])
        sm = sb("sm", [P, CH, 40])
        WCOL, CNT, CNTM, BINV, G1, VE, RS, S, S8, RI, CI = range(11)
        MV, BN = 12, 14

        def col(c, k, n=1):
            return sm[:, c, k:k + n]

        psA = [ctx.enter_context(nc.psum_tensor(f"psA{c}", [P, D], F32)) for c in range(CH)]
        psB = [ctx.enter_context(nc.psum_tensor(f"psB{c}", [P, D], F32)) for c in range(CH)]

        consts_ok, ident0 = sem("consts_ok"), sem("ident0")
        vec_in, staged, split_hi, split_lo, slot_read, v_ps, v_sb, wa_ps, wa_sb, rows_ok = map(sem, (
            "vec_in", "staged", "split_hi", "split_lo", "slot_read", "v_ps", "v_sb", "wa_ps", "wa_sb", "rows_ok"))
        stage_in = [sem(f"stage_in{i}") for i in range(4)]
        adj_in = [sem(f"adj_in{c}") for c in range(CH)]
        x_in = [sem(f"x_in{c}") for c in range(CH)]
        x2_stored = [sem(f"x2_stored{c}") for c in range(CH)]
        (adjT_ps, adjT_sb, inc_sb, cnt_ok, cntm_ok, binv_ok, hbh_ok, hb_sb, deg_ps, dmx_ok, drec_ok, dinv_ok,
         gt_sb, g1_ps, g1_sb, adjT_cur, tx_ps, t1h, t1_sb, bias_ok, twice_ok, u_ok,
         r_psA, r_psB, r_sbA, r_sbB, bn1, mv1, ve1, rs1, rc_ok, g2_ok, t2_psA, t2_psB, t2hA, t2hB,
         t2_sb, y2_ps, z1, bn2, mv2, ve2, rs2, x1_ok, s_ok, s8_ok, sb_ps, tanh_ok, lrelu_ok, exp_ok,
         af_ok, t3_ps, t3h, ri_ok, t3_sb, y3_ps, z2, bn3, mv3, ve3, rs3, x2_ok) = map(sem, (
            "adjT_ps adjT_sb inc_sb cnt_ok cntm_ok binv_ok hbh_ok hb_sb deg_ps dmx_ok drec_ok dinv_ok "
            "gt_sb g1_ps g1_sb adjT_cur tx_ps t1h t1_sb bias_ok twice_ok u_ok "
            "r_psA r_psB r_sbA r_sbB bn1 mv1 ve1 rs1 rc_ok g2_ok t2_psA t2_psB t2hA t2hB "
            "t2_sb y2_ps z1 bn2 mv2 ve2 rs2 x1_ok s_ok s8_ok sb_ps tanh_ok lrelu_ok exp_ok "
            "af_ok t3_ps t3h ri_ok t3_sb y3_ps z2 bn3 mv3 ve3 rs3 x2_ok").split())

        W1v = W1T.rearrange("(k p) n -> p k n", p=P)
        W2v = W2T.rearrange("(k p) n -> p k n", p=P)
        wv = w.rearrange("(k p) n -> p k n", p=P)
        wTv = wT.rearrange("(k p) n -> p k n", p=P)
        pieces = ([(W1v[:, k, :], W1h[:, k, :], W1l[:, k, :], None) for k in range(KD)]
                  + [(wv[:, k:k + 2, :], Wh[:, k:k + 2, :], Wl[:, k:k + 2, :], None) for k in (0, 2)]
                  + [(W2v[:, k:k + 2, :], W2h[:, k:k + 2, :], W2l[:, k:k + 2, :], k) for k in range(0, KH, 2)])
        first_g = KD + 2
        slots = 4

        def stage(n, two_chunks=True):
            s = R[:, n % slots, :]
            return s.rearrange("p (k n) -> p k n", k=2) if two_chunks else s

        ORDER_PREP = rounds([("adjT", 0), ("inc", 0), ("deg", 1), ("g", 1), ("g1", 2)], CH)
        ORDER = order(
            "cur.0 tx.0 cur.1 cur.2 tx.1 tx.2 txe.0 cur.3 txe.1 tx.3 y1.0 u.0 relu.0 st1.0 rs1.0 gs.0 y1.1 txe.2 t2.0 "
            "y1.2 t2e.0 y2.0 txe.3 relu.1 relu.2 u.1 st1.1 rs1.1 gs.1 st1.2 rs1.2 u.2 t2.1 adjT.0 u.3 y1.3 inc.0 z1.0 "
            "deg.0 t2e.1 rs2.0 g.0 x1.0 relu.3 gs.2 y2.1 s8.0 st1.3 rs1.3 gs.3 adjT.1 t2.2 z1.1 sb.0 rs2.1 t2e.2 f.0 "
            "x1.1 t2.3 y2.2 inc.1 t2e.3 z1.2 s8.1 deg.1 adjT.2 sb.1 g.1 f.1 rs2.2 g1.0 y2.3 adjT.3 x1.2 inc.2 z1.3 "
            "t3.0 g1.1 rs2.3 t3.1 t3e.0 sb.2 deg.2 inc.3 s8.2 y3.0 x1.3 sb.3 g.2 t3e.1 deg.3 f.2 g1.2 s8.3 g.3 f.3 "
            "y3.1 t3.2 g1.3 t3e.2 z2.0 t3.3 y3.2 t3e.3 rs3.0 z2.1 z2.2 rs3.1 rs3.2 y3.3 z2.3 x2.0 x2.1 rs3.3 x2.2 "
            "x2.3")
        b1_raw = [Fp[0:2, :, :].rearrange("p c j -> p (c j)"), ubias[0:2, 0, :]]
        block = ctx.enter_context(nc.Block())

        @block.sync
        def _(sp):
            for c in range(CH):
                if c == 0:
                    sp.wait_ge(consts_ok, 5)
                for g in range(P // C):
                    sp.dma_start(A[g * C:(g + 1) * C, c, g * C:(g + 1) * C], adj_t[c, g]).then_inc(adj_in[c], 16)
                sp.dma_start(X[:, c, :], x_rows[c]).then_inc(x_in[c], 16)
            sp.dma_start(gam[:, :], gamma.rearrange("(k p) -> p k", p=P), allow_slow_non_contiguous=True).then_inc(vec_in, 16)
            sp.dma_start(bet[:, :], beta.rearrange("(k p) -> p k", p=P), allow_slow_non_contiguous=True).then_inc(vec_in, 16)
            sp.dma_start(a_col[:, :], a.rearrange("(k p) -> p k", p=P), allow_slow_non_contiguous=True).then_inc(vec_in, 16)
            sp.dma_start(b2_all[:, :], b2.partition_broadcast(P)).then_inc(vec_in, 16)
            for half in range(2):
                sp.dma_start(b1_raw[half], b1[half * D:(half + 1) * D].partition_broadcast(2)).then_inc(vec_in, 16)
            for n, (src, _, _, _) in enumerate(pieces):
                if n >= slots:
                    sp.wait_ge(split_lo, n - slots + 1)
                    if n - slots >= first_g:
                        sp.wait_ge(v_ps, n - slots - first_g + 1)
                sp.dma_start(stage(n, n >= KD), src).then_inc(stage_in[n % slots], 16)
            for k in (0, 2):
                n = len(pieces) + k // 2
                sp.wait_ge(split_lo, n - slots + 1)
                if n - slots >= first_g:
                    sp.wait_ge(v_ps, n - slots - first_g + 1)
                sp.dma_start(stage(n), wTv[:, k:k + 2, :]).then_inc(stage_in[n % slots], 16)
            for c in range(CH):
                sp.sem_inc(x2_stored[c], 16)
            with sp.Fori(0, iters) as it:
                nxt = sp.snap(((it + 1) % iters) * CH)
                t0 = sp.snap(it * CH)
                for c in range(CH):
                    sp.wait_ge(adjT_ps, sp.snap(t0 + (c + 1)))
                    for g in range(P // C):
                        sp.dma_start(A[g * C:(g + 1) * C, c, g * C:(g + 1) * C],
                                     adj_t[bass.ds(nxt + c, 1), g].rearrange("a c e -> (a c) e")).then_inc(adj_in[c], 16)
                for c in range(CH):
                    sp.wait_ge(z1, sp.snap(t0 + (c + 1)))
                    sp.dma_start(X[:, c, :], x_rows[bass.ds(nxt + c, 1)].rearrange("a r d -> (a r) d")).then_inc(x_in[c], 16)
                for c in range(CH):
                    sp.wait_ge(x2_ok, sp.snap(t0 + (c + 1)))
                    sp.dma_start(x2[bass.ds(t0 + c, 1)].rearrange("a r d -> (a r) d"), R[:, c, 0:D]).then_inc(x2_stored[c], 16)
            for c in range(CH):
                sp.wait_ge(x2_stored[c], 16 * (iters + 1))
                sp.wait_ge(x_in[c], 16 * (iters + 1))
                sp.wait_ge(adj_in[c], 32 * (iters + 1))

        @block.gpsimd
        def _(pool):
            pool.memset(ident[:, :], 0.0).then_inc(ident0, 1)
            pool.wait_ge(ident0, 1)
            pool.affine_select(out=ident[:, :], in_=ident[:, :], compare_op=ALU.not_equal, fill=1.0, base=0,
                               pattern=[[-1, P]], channel_multiplier=1).then_inc(consts_ok, 1)
            pool.memset(ones[:, :], 1.0).then_inc(consts_ok, 1)
            pool.memset(ones_row[:, :].bitcast(F32), 1.0).then_inc(consts_ok, 1)
            pool.memset(mhalf[:, :], -0.5).then_inc(consts_ok, 1)
            pool.memset(A[:, :, :], 0.0).then_inc(consts_ok, 1)

            def alone(sem, value):
                pool.wait_ge(consts_ok, 5)
                pool.wait_ge(sem, value)

            def rstd(c, n, mv, ve):
                alone(mv, n[c])
                pool.tensor_scalar(col(c, VE), col(c, MV + 1), EPS, None, ALU.add).then_inc(ve, 1)
                pool.wait_ge(ve, n[c])
                return pool.tensor_tensor(col(c, RS), col(c, VE), mhalf[:, :], ALU.pow)

            def cur(c, n):
                alone(gt_sb, n[c])
                pool.tensor_copy(ATc[:, c, :], ATn[:, c, :]).then_inc(adjT_cur, 1)

            def u(c, n):
                pool.wait_ge(tx_ps, n[c])
                pool.tensor_tensor(X[:, c, :], X[:, c, :], X[:, c, :], ALU.add).then_inc(twice_ok, 1)
                pool.wait_ge(twice_ok, n[c])
                pool.wait_ge(bias_ok, n[c])
                pool.tensor_tensor(X[:, c, :], X[:, c, :], ubias[:, c, :], ALU.add).then_inc(u_ok, 1)

            def rs_first(c, n):
                rstd(c, n, mv1, ve1).then_inc(rs1, 1)

            def rs_second(c, n):
                rstd(c, n, mv2, ve2).then_inc(rs2, 1)

            def rs_third(c, n):
                rstd(c, n, mv3, ve3).then_inc(rs3, 1)

            with pool.Fori(0, iters) as it:
                now = [pool.to_reg(it * CH + (c + 1)) for c in range(CH)]
                for step, c in ORDER:
                    if step == "cur":
                        cur(c, now)
                    if step == "u":
                        u(c, now)
                    if step == "rs1":
                        rs_first(c, now)
                    if step == "rs2":
                        rs_second(c, now)
                    if step == "rs3":
                        rs_third(c, now)

        @block.scalar
        def _(act):
            act.wait_ge(vec_in, 6 * 16)
            for half in range(2):
                act.copy(b1_rows[:, half * D:(half + 1) * D], b1_raw[half]).then_inc(rows_ok, 1)

            for n, (_, hi, _, g) in enumerate(pieces):
                act.wait_ge(stage_in[n % slots], 16 * (n // slots + 1))
                if g is None:
                    act.copy(hi, stage(n, n >= KD)).then_inc(split_hi, 1)
                else:
                    act.activation(hi[:, 0, :], stage(n)[:, 0, :], ACT.Copy, scale=gam[:, g:g + 1])
                    act.activation(hi[:, 1, :], stage(n)[:, 1, :], ACT.Copy, scale=gam[:, g + 1:g + 2]).then_inc(split_hi, 1)
            act.wait_ge(v_ps, 4)
            act.copy(v_all[:, :], psA[0][:, :]).then_inc(v_sb, 1)
            act.wait_ge(wa_ps, 2)
            act.copy(wa_all[:, :], psA[1][:, :]).then_inc(wa_sb, 1)

            def adjT(c, n, after=None):
                act.wait_ge(adjT_ps, n[c])
                if after:
                    act.wait_ge(adjT_cur, after[c])
                act.copy(ATn[:, c, 0:P], psB[c][:, 0:P]).then_inc(adjT_sb, 1)

            def txe(c, n):
                act.wait_ge(tx_ps, n[c])
                act.copy(Th[:, c, 0:D], psA[c][:, :]).then_inc(t1h, 1)

            def relu(c, n, stored):
                act.wait_ge(r_psA, n[c])
                act.wait_ge(x2_stored[c], stored)
                act.activation(R[:, c, 0:D], psA[c][:, :], ACT.Relu).then_inc(r_sbA, 1)
                act.wait_ge(r_psB, n[c])
                act.activation(R[:, c, D:DH], psB[c][:, :], ACT.Relu).then_inc(r_sbB, 1)

            def gs(c, n):
                act.wait_ge(rs1, n[c])
                act.mul(GT[:, c, :], GT[:, c, :], col(c, RS)).then_inc(g2_ok, 1)

            def t2e(c, n):
                act.wait_ge(t2_psA, n[c])
                act.copy(Th[:, c, 0:D], psA[c][:, :]).then_inc(t2hA, 1)
                act.wait_ge(t2_psB, n[c])
                act.copy(Th[:, c, D:DH], psB[c][:, :]).then_inc(t2hB, 1)

            def s8(c, n):
                act.wait_ge(s_ok, n[c])
                act.mul(col(c, S8), col(c, S), 0.125).then_inc(s8_ok, 1)

            def f(c, n):
                act.wait_ge(sb_ps, n[c])
                act.wait_ge(s8_ok, n[c])
                act.activation(Fp[:, c, :], psA[c][:, 0:P], ACT.Tanh, bias=col(c, S8), scale=0.125).then_inc(tanh_ok, 1)
                act.wait_ge(lrelu_ok, n[c])
                act.activation(Fp[:, c, :], Fp[:, c, :], ACT.Exp, scale=8.0).then_inc(exp_ok, 1)

            def t3e(c, n):
                act.wait_ge(t3_ps, n[c])
                act.copy(Th[:, c, 0:D], psA[c][:, :]).then_inc(t3h, 1)

            first = [c + 1 for c in range(CH)]
            for step, c in ORDER_PREP:
                if step == "adjT":
                    adjT(c, first)
            with act.Fori(0, iters) as it:
                now = [act.snap(it * CH + (c + 1)) for c in range(CH)]
                nxt = [act.snap(it * CH + (CH + c + 1)) for c in range(CH)]
                stored = act.snap(it * 16 + 16)
                for step, c in ORDER:
                    if step == "adjT":
                        adjT(c, nxt, now)
                    if step == "txe":
                        txe(c, now)
                    if step == "relu":
                        relu(c, now, stored)
                    if step == "gs":
                        gs(c, now)
                    if step == "t2e":
                        t2e(c, now)
                    if step == "s8":
                        s8(c, now)
                    if step == "f":
                        f(c, now)
                    if step == "t3e":
                        t3e(c, now)

        @block.vector
        def _(dve):
            dve.wait_ge(consts_ok, 5)
            for half in range(2):
                hi, lo = b1_rows[:, half * D:(half + 1) * D], b1_raw[half]
                dve.wait_ge(rows_ok, 2 + 3 * half)
                dve.tensor_tensor(lo, lo, hi.bitcast(F32), ALU.subtract).then_inc(rows_ok, 1)
                dve.wait_ge(rows_ok, 3 + 3 * half)
                dve.tensor_scalar(lo, lo, ident[0:2, 1:2], None, ALU.mult).then_inc(rows_ok, 1)
                dve.wait_ge(rows_ok, 4 + 3 * half)
                dve.scalar_tensor_tensor(hi, hi.bitcast(F32), ident[0:2, 0:1], lo, ALU.mult, ALU.add).then_inc(rows_ok, 1)

            for n, (_, hi, lo, g) in enumerate(pieces):
                dve.wait_ge(split_hi, n + 1)
                if g is None:
                    dve.tensor_tensor(lo, stage(n, n >= KD), hi.bitcast(F32), ALU.subtract).then_inc(split_lo, 1)
                else:
                    for k in range(2):
                        last = dve.scalar_tensor_tensor(lo[:, k, :], stage(n)[:, k, :], gam[:, g + k:g + k + 1],
                                                        hi[:, k, :].bitcast(F32), ALU.mult, ALU.subtract)
                    last.then_inc(split_lo, 1)

            def alone(sem, value):
                dve.wait_ge(consts_ok, 5)
                dve.wait_ge(sem, value)

            def inc(c, n):
                dve.wait_ge(adjT_sb, n[c])
                dve.tensor_tensor(col(c, WCOL), ATn[:, c, 0:1], ATn[:, c, C:C + 1], ALU.add)
                dve.tensor_scalar(HT[:, c, :], ATn[:, c, 0:P], 0.0, None, ALU.not_equal).then_inc(inc_sb, 1)
                dve.wait_ge(inc_sb, n[c])
                dve.reduce_sum(col(c, CNT), HT[:, c, :].bitcast(F32), AX.X).then_inc(cnt_ok, 1)
                dve.wait_ge(cnt_ok, n[c])
                dve.tensor_scalar(col(c, CNTM), col(c, CNT), 1.0, None, ALU.max).then_inc(cntm_ok, 1)
                dve.wait_ge(cntm_ok, n[c])
                dve.reciprocal(col(c, BINV), col(c, CNTM)).then_inc(binv_ok, 1)
                dve.wait_ge(binv_ok, n[c])
                dve.tensor_scalar(HBh[:, c, :], HT[:, c, :].bitcast(F32), col(c, BINV), None, ALU.mult).then_inc(hbh_ok, 1)
                dve.wait_ge(hbh_ok, n[c])
                dve.scalar_tensor_tensor(HBl[:, c, :], HT[:, c, :].bitcast(F32), col(c, BINV), HBh[:, c, :].bitcast(F32),
                                         ALU.mult, ALU.subtract).then_inc(hb_sb, 1)

            def g(c, n):
                dve.wait_ge(deg_ps, n[c])
                dve.tensor_copy(ATn[:, c, P:P + 1], psB[c][:, 3 * P:3 * P + 1])
                dve.tensor_scalar(DI[:, c, :], psB[c][:, P:2 * P], TINY, None, ALU.max).then_inc(dmx_ok, 1)
                dve.wait_ge(dmx_ok, n[c])
                dve.reciprocal(DI[:, c, :], DI[:, c, :]).then_inc(drec_ok, 1)
                dve.wait_ge(drec_ok, n[c])
                dve.scalar_tensor_tensor(DI[:, c, :], psB[c][:, P:2 * P], 0.0, DI[:, c, :], ALU.is_gt, ALU.mult).then_inc(dinv_ok, 1)
                dve.wait_ge(dinv_ok, n[c])
                dve.tensor_tensor(GT[:, c, :], psB[c][:, 2 * P:3 * P], DI[:, c, :], ALU.mult).then_inc(gt_sb, 1)

            def g1(c, n):
                dve.wait_ge(g1_ps, n[c])
                dve.tensor_copy(col(c, G1), psB[c][:, 3 * P + 2:3 * P + 3]).then_inc(g1_sb, 1)

            def txe(c, n):
                dve.wait_ge(t1h, n[c])
                dve.tensor_tensor(Tl[:, c, 0:D], psA[c][:, :], Th[:, c, 0:D].bitcast(F32), ALU.subtract).then_inc(t1_sb, 1)

            def u(c, n):
                dve.wait_ge(g1_sb, n[c])
                dve.scalar_tensor_tensor(ubias[:, c, :], v_all[:, :], col(c, G1), b2_all[:, :], ALU.mult, ALU.add).then_inc(bias_ok, 1)

            def st1(c, n):
                dve.wait_ge(r_sbA, n[c])
                dve.bn_stats(col(c, BN, 6), R[:, c, 0:D])
                dve.wait_ge(r_sbB, n[c])
                dve.bn_stats(col(c, BN + 6, 6), R[:, c, D:DH]).then_inc(bn1, 1)
                alone(bn1, n[c])
                dve.bn_aggr(col(c, MV, 2), col(c, BN, 12)).then_inc(mv1, 1)
                alone(mv1, n[c])
                dve.tensor_scalar(R[:, c, :], R[:, c, :], col(c, MV), None, ALU.subtract).then_inc(rc_ok, 1)

            def t2e(c, n):
                dve.wait_ge(t2hA, n[c])
                dve.tensor_tensor(Tl[:, c, 0:D], psA[c][:, :], Th[:, c, 0:D].bitcast(F32), ALU.subtract)
                dve.wait_ge(t2hB, n[c])
                dve.tensor_tensor(Tl[:, c, D:DH], psB[c][:, :], Th[:, c, D:DH].bitcast(F32), ALU.subtract).then_inc(t2_sb, 1)

            def stats(c, n, bn, mv):
                dve.bn_stats(col(c, BN, 6), R[:, c, 0:D]).then_inc(bn, 1)
                alone(bn, n[c])
                dve.bn_aggr(col(c, MV, 2), col(c, BN, 6)).then_inc(mv, 1)

            def z_first(c, n):
                dve.wait_ge(y2_ps, n[c])
                dve.wait_ge(u_ok, n[c])
                dve.tensor_tensor(R[:, c, 0:D], psA[c][:, :], X[:, c, :], ALU.add).then_inc(z1, 1)
                dve.wait_ge(z1, n[c])
                stats(c, n, bn2, mv2)

            def x1(c, n):
                dve.wait_ge(rs2, n[c])
                dve.tensor_scalar(R[:, c, D:DH], R[:, c, 0:D], col(c, MV), col(c, RS), ALU.subtract, ALU.mult).then_inc(x1_ok, 1)
                dve.wait_ge(x1_ok, n[c])
                dve.tensor_tensor_reduce(R[:, c, 0:D], R[:, c, D:DH], wa_all[:, :], 1.0, 0.0, ALU.mult, ALU.add,
                                         col(c, S)).then_inc(s_ok, 1)

            def f(c, n):
                dve.wait_ge(tanh_ok, n[c])
                dve.scalar_tensor_tensor(Fp[:, c, :], Fp[:, c, :], 0.1, Fp[:, c, :], ALU.mult, ALU.max).then_inc(lrelu_ok, 1)
                dve.wait_ge(exp_ok, n[c])
                dve.wait_ge(adjT_cur, n[c])
                dve.tensor_tensor(Fp[:, c, :], Fp[:, c, :], ATc[:, c, 0:P], ALU.mult).then_inc(af_ok, 1)

            def t3e(c, n):
                dve.wait_ge(t3_ps, n[c])
                dve.reciprocal(col(c, RI), psB[c][:, P:P + 1]).then_inc(ri_ok, 1)
                dve.wait_ge(ri_ok, n[c])
                dve.tensor_tensor(col(c, CI), col(c, RI), ATc[:, c, P:P + 1], ALU.mult)
                dve.wait_ge(t3h, n[c])
                dve.tensor_tensor(Tl[:, c, 0:D], psA[c][:, :], Th[:, c, 0:D].bitcast(F32), ALU.subtract).then_inc(t3_sb, 1)

            def z_second(c, n):
                dve.wait_ge(y3_ps, n[c])
                dve.wait_ge(t3_sb, n[c])
                dve.scalar_tensor_tensor(R[:, c, 0:D], psA[c][:, :], col(c, CI), R[:, c, D:DH], ALU.mult, ALU.add).then_inc(z2, 1)
                dve.wait_ge(z2, n[c + CH])
                stats(c, n, bn3, mv3)

            def x2_norm(c, n):
                dve.wait_ge(rs3, n[c])
                dve.tensor_scalar(R[:, c, 0:D], R[:, c, 0:D], col(c, MV), col(c, RS), ALU.subtract, ALU.mult).then_inc(x2_ok, 1)

            first = [c + 1 for c in range(CH)]
            for step, c in ORDER_PREP:
                if step == "inc":
                    inc(c, first)
                if step == "g":
                    g(c, first)
                if step == "g1":
                    g1(c, first)
            dve.sem_inc(z2, CH)
            dve.wait_ge(wa_sb, 1)
            dve.wait_ge(v_sb, 1)
            with dve.Fori(0, iters) as it:
                now = [dve.snap(it * CH + (c + 1)) for c in range(2 * CH)]
                nxt = now[CH:]
                for step, c in ORDER:
                    if step == "inc":
                        inc(c, nxt)
                    if step == "g":
                        g(c, nxt)
                    if step == "g1":
                        g1(c, nxt)
                    if step == "txe":
                        txe(c, now)
                    if step == "u":
                        u(c, now)
                    if step == "st1":
                        st1(c, now)
                    if step == "t2e":
                        t2e(c, now)
                    if step == "z1":
                        z_first(c, now)
                    if step == "x1":
                        x1(c, now)
                    if step == "f":
                        f(c, now)
                    if step == "t3e":
                        t3e(c, now)
                    if step == "z2":
                        z_second(c, now)
                    if step == "x2":
                        x2_norm(c, now)

        @block.tensor
        def _(pe):
            pe.wait_ge(consts_ok, 5)
            pe.wait_ge(vec_in, 6 * 16)

            def products(out, terms, start=True):
                for i, (lhsT, rhs) in enumerate(terms):
                    mm = pe.matmul(out, lhsT, rhs, start=start and i == 0, stop=i == len(terms) - 1)
                return mm

            def three(lh, ll, rh, rl):
                return [(lh, rh), (lh, rl), (ll, rh)]

            def adjT(c, k):
                pe.wait_ge(adj_in[c], k)
                pe.transpose(psB[c][:, 0:P], A[:, c, :], ident[:, :]).then_inc(adjT_ps, 1)

            def deg(c, n):
                pe.wait_ge(hb_sb, n[c])
                products(psB[c][:, P:2 * P], [(col(c, WCOL).to_broadcast([P, P]), HT[:, c, :].bitcast(F32))])
                products(psB[c][:, 2 * P:3 * P], [(HBh[:, c, :], HT[:, c, :]), (HBl[:, c, :], HT[:, c, :])])
                products(psB[c][:, 3 * P:3 * P + 1], [(ATn[:, c, 0:P], ones[:, 0:1])]).then_inc(deg_ps, 1)

            def g1(c, n):
                pe.wait_ge(gt_sb, n[c])
                products(psB[c][:, 3 * P + 2:3 * P + 3], [(GT[:, c, :], ones[:, 0:1])]).then_inc(g1_ps, 1)

            def mix(out, rows, M):
                for j in range(KD):
                    f = slice(j * P, (j + 1) * P)
                    mm = products(out[:, f], [(rows[:, f], M)])
                return mm

            def project(out, c, k, Rh, Rl, terms=()):
                terms = list(terms)
                for j in range(k):
                    f = slice(j * P, (j + 1) * P)
                    terms += three(Th[:, c, f], Tl[:, c, f], Rh(j), Rl(j))
                return products(out, terms)

            def tx(c, n, loaded):
                pe.wait_ge(gt_sb, n[c])
                pe.wait_ge(x_in[c], loaded)
                pe.wait_ge(z2, n[c])
                mix(psA[c][:, :], X[:, c, :], GT[:, c, :]).then_inc(tx_ps, 1)

            def y1(c, n):
                pe.wait_ge(t1_sb, n[c])
                pe.wait_ge(g1_sb, n[c])
                for half, (ps, ready) in enumerate(((psA, r_psA), (psB, r_psB))):
                    h = slice(half * D, (half + 1) * D)
                    project(ps[c][:, :], c, KD, lambda j: W1h[:, j, h], lambda j: W1l[:, j, h],
                            [(ones_row[:, :], b1_rows[:, h])]).then_inc(ready, 1)

            def t2(c, n):
                pe.wait_ge(rc_ok, n[c])
                pe.wait_ge(g2_ok, n[c])
                mix(psA[c][:, :], R[:, c, 0:D], GT[:, c, :]).then_inc(t2_psA, 1)
                mix(psB[c][:, :], R[:, c, D:DH], GT[:, c, :]).then_inc(t2_psB, 1)

            def y2(c, n):
                pe.wait_ge(t2_sb, n[c])
                project(psA[c][:, :], c, KH, lambda j: W2h[:, j, :], lambda j: W2l[:, j, :]).then_inc(y2_ps, 1)

            def sbc(c, n):
                pe.wait_ge(s_ok, n[c])
                products(psA[c][:, 0:P], [(col(c, S).to_broadcast([P, P]), ident[:, :])]).then_inc(sb_ps, 1)

            def t3(c, n, after):
                pe.wait_ge(af_ok, n[c])
                pe.wait_ge(g1_sb, after[c])
                products(psB[c][:, P:P + 1], [(Fp[:, c, :], ones[:, 0:1])])
                mix(psA[c][:, :], R[:, c, D:DH], Fp[:, c, :]).then_inc(t3_ps, 1)

            def y3(c, n):
                pe.wait_ge(t3_sb, n[c])
                project(psA[c][:, :], c, KD, lambda j: Wh[:, j, :], lambda j: Wl[:, j, :]).then_inc(y3_ps, 1)

            for i in range(4):
                n = first_g + i
                pe.wait_ge(stage_in[n % slots], 16 * (n // slots + 1))
                for k in range(2):
                    mm = pe.matmul(psA[0][:, :], bet[:, 2 * i + k:2 * i + k + 1].to_broadcast([P, P]), stage(n)[:, k, :],
                                   start=(i + k == 0), stop=(i == 3 and k == 1))
                mm.then_inc(v_ps, 1)
            for i in range(2):
                n = len(pieces) + i
                pe.wait_ge(stage_in[n % slots], 16 * (n // slots + 1))
                for k in range(2):
                    mm = pe.matmul(psA[1][:, :], a_col[:, 2 * i + k:2 * i + k + 1].to_broadcast([P, P]), stage(n)[:, k, :],
                                   start=(i + k == 0), stop=(i == 1 and k == 1))
                mm.then_inc(wa_ps, 1)
            first = [c + 1 for c in range(CH)]
            for step, c in ORDER_PREP:
                if step == "adjT":
                    adjT(c, 32)
                if step == "deg":
                    deg(c, first)
                if step == "g1":
                    g1(c, first)
            pe.wait_ge(split_lo, len(pieces))
            pe.wait_ge(rows_ok, 8)
            pe.wait_ge(v_sb, 1)
            pe.wait_ge(wa_sb, 1)
            with pe.Fori(0, iters) as it:
                now = [pe.snap(it * CH + (c + 1)) for c in range(CH)]
                nxt = [pe.snap(it * CH + (CH + c + 1)) for c in range(CH)]
                loaded = pe.snap(it * 32 + 64)
                x_loaded = pe.snap(it * 16 + 16)
                for step, c in ORDER:
                    if step == "adjT":
                        adjT(c, loaded)
                    if step == "deg":
                        deg(c, nxt)
                    if step == "g1":
                        g1(c, nxt)
                    if step == "tx":
                        tx(c, now, x_loaded)
                    if step == "y1":
                        y1(c, now)
                    if step == "t2":
                        t2(c, now)
                    if step == "y2":
                        y2(c, now)
                    if step == "sb":
                        sbc(c, now)
                    if step == "t3":
                        t3(c, now, nxt)
                    if step == "y3":
                        y3(c, now)


HEADS, DHEAD = 8, 64
HG = HEADS // 2
LA = LD = LG = 0.33
SCALE = DHEAD ** -0.5
MASKED = 2.0 ** 100
OUTSIDE = 2.0 ** 126


def convolutions_and_attention(nc, semaphores, x2, adj, mask_rows, mask_cols, W1, b1, W2, b2, W3, b3, Wqkv, Wout, bout, out):
    tiles = x2.shape[0]
    iters = tiles // CH
    out_rows = out.rearrange("(t g) c d -> t (g c) d", g=P // C)
    adj_t = adj.rearrange("(t g) c e -> t g c e", g=P // C)

    with ExitStack() as ctx:
        def sb(name, shape, dt=F32):
            return ctx.enter_context(nc.sbuf_tensor(name, shape, dt))

        def sem(name):
            semaphores.append(nc.alloc_semaphore(name))
            return semaphores[-1]

        GW = [(sb(f"GW{i}h", [P, KD, D], F32R), sb(f"GW{i}l", [P, KD, D], F32R)) for i in range(3)]
        WQh, WQl = sb("WQh", [P, KD, 3, D], F32R), sb("WQl", [P, KD, 3, D], F32R)
        WOh, WOl = sb("WOh", [P, KD, D], F32R), sb("WOl", [P, KD, D], F32R)
        ident = sb("ident2", [P, P])
        identr = sb("identr", [P, P], F32R)
        ones_row = sb("ones_row2", [P, P], F32R)
        rows = sb("rows", [P, D], F32R)
        inside = sb("inside", [P, P])
        outside = sb("outside", [P, P])
        mhalf = sb("mhalf2", [P, 1])
        A = sb("A2", [P, CH, P])
        AT = sb("AT", [P, CH, P])
        mrow = sb("mrow", [P, CH, P], U8)
        mcol = sb("mcol", [P, CH, 4], U8)
        MM, BT = sb("MM", [P, P]), sb("BT", [P, P])
        BS = sb("BS", [P, CH, P], F32R)
        Cm = sb("Cm", [P, CH, P])
        X = sb("X2", [P, CH, D])
        H = sb("H", [P, CH, D])
        Th, Tl = sb("T2h", [P, KD, CH * P], F32R), sb("T2l", [P, KD, CH * P], F32R)
        QK = sb("QK", [P, 2 * KD, 2 * P])
        E = sb("E", [P, CH, HEADS, P])
        AA = sb("AA", [P, 2, HEADS, P])
        Z = sb("Z", [P, 2, D])
        sm = sb("sm2", [P, CH, 64])
        MC, VE, RS = range(3)
        MV, BN, NMX, NB, SUM, REC, RLA = 4, 8, 16, 24, 32, 40, 48

        def col(c, k, n=1):
            return sm[:, c, k:k + n]

        psA = [ctx.enter_context(nc.psum_tensor(f"qsA{c}", [P, D], F32)) for c in range(CH)]
        psB = [ctx.enter_context(nc.psum_tensor(f"qsB{c}", [P, D], F32)) for c in range(CH)]

        consts_ok, ident0, blocks0, rows_in, rows_ok, split_hi, split_lo = map(sem, (
            "consts_ok2", "ident02", "blocks0", "rows_in", "rows_ok2", "split_hi2", "split_lo2"))
        slots = 3
        stage_in = [sem(f"stage2_in{i}") for i in range(slots)]
        adj_in = [sem(f"adj2_in{c}") for c in range(CH)]
        x_in = [sem(f"x2_in{c}") for c in range(CH)]
        out_stored = [sem(f"out_stored{i}") for i in range(2)]
        qk_ps, qk_sb = ([sem(f"{n}{b}") for b in range(4)] for n in ("qk_ps", "qk_sb"))
        t_ps, th, t_sb, g_ps, g_sb = ([sem(f"{n}{i}") for i in range(3)] for n in ("t_ps", "th", "t_sb", "g_ps", "g_sb"))
        (adjT_ps, at_sb, mc_ok, mm_ok, bt1, bt2, bs_ok, mm2, exp_adj, cm1, bt3, cm2, cm_ok, z3, bn3, mv3,
         ve3, rs3, x3_ok, xp_ps, xph, xp_sb, v_ps, v_sb, s_psA, s_psB, max_ok, nb_ok, ex_ok, rec_ok, rla_ok, attn_ok,
         ta_psA, ta_psB, ta_sbA, ta_sbB, av_ps, avh, av_sb, wo_ps, z4, bn4, mv4, ve4, rs4, x4_ok) = map(sem, (
            "adjT_ps2 at_sb mc_ok mm_ok bt1 bt2 bs_ok mm2 exp_adj cm1 bt3 cm2 cm_ok z3 bn3_2 mv3_2 "
            "ve3_2 rs3_2 x3_ok xp_ps xph xp_sb v_ps2 v_sb2 s_psA s_psB max_ok nb_ok ex_ok rec_ok rla_ok attn_ok "
            "ta_psA ta_psB ta_sbA ta_sbB av_ps avh av_sb wo_ps z4 bn4 mv4 ve4 rs4 x4_ok").split())

        BIASES = (b1, b2, b3, bout)
        raw = Z[:, 0, :]

        def chunks(W):
            return W.rearrange("(k p) n -> p k n", p=P)

        pieces = [(chunks(W)[:, k:k + 2, :], h[:, k:k + 2, :], l[:, k:k + 2, :])
                  for W, (h, l) in zip((W1, W2, W3, Wout), GW + [(WOh, WOl)]) for k in (0, 2)]
        for k in range(KD):
            for half in range(2):
                src = chunks(Wqkv)[:, k, half * 3 * D // 2:(half + 1) * 3 * D // 2].rearrange("p (h i d) -> p h i d", i=3, d=DHEAD)
                dst = [W[:, k, :, half * D // 2:(half + 1) * D // 2].rearrange("p i (h d) -> p h i d", d=DHEAD) for W in (WQh, WQl)]
                pieces.append((src, *dst))

        def stage(n):
            s = Z[:, :, :].rearrange("p a b -> p (a b)") if n % slots == 2 else E[:, n % slots, :, :].rearrange("p h j -> p (h j)")
            if n < 8:
                return s.rearrange("p (k n) -> p k n", k=2)
            return s[:, 0:3 * D // 2].rearrange("p (h i d) -> p h i d", i=3, d=DHEAD)

        ORDER_PREP = rounds([("adjT", 0)], CH)
        ORDER = order(
            "t0.0 cm.0 t0.1 t0.2 t0.3 cm.1 g0.0 g0.1 t1.0 g0.2 g1.0 t1.1 g0.3 g1.1 cm.2 t2.0 t1.2 t2.1 t1.3 g1.2 g2.0 "
            "g2.1 z3.0 t2.2 g1.3 rs3.0 x3.0 z3.1 rs3.1 xp.0 x3.1 t2.3 g2.2 z3.2 g2.3 rs3.2 x3.2 xp.1 v.0 xp.2 cm.3 "
            "z3.3 v.1 rs3.3 x3.3 v.2 xp.3 qk.0 v.3 s.0 s.1 sm.0 sm.1 qk.1 ta.0 s.2 ta.1 sm.2 av.0 s.3 av.1 sm.3 ta.2 "
            "wo.0 wo.1 z4.0 ta.3 rs4.0 x4.0 av.2 z4.1 rs4.1 av.3 adjT.0 wo.2 x4.1 z4.2 wo.3 adjT.1 adjT.2 adjT.3 "
            "rs4.2 z4.3 rs4.3 x4.2 x4.3")
        block = ctx.enter_context(nc.Block())

        @block.sync
        def _(sp):
            def load(c, tile):
                for g in range(P // C):
                    sp.dma_start(A[g * C:(g + 1) * C, c, g * C:(g + 1) * C],
                                 adj_t[bass.ds(tile, 1), g].rearrange("a c e -> (a c) e")).then_inc(adj_in[c], 16)
                sp.dma_start(mrow[:, c, :], mask_rows[bass.ds(tile, 1)].rearrange("a j -> (a j)").partition_broadcast(P))\
                    .then_inc(adj_in[c], 16)
                sp.dma_start(mcol[:, c, 0:1], mask_cols[:, bass.ds(tile, 1)], allow_slow_non_contiguous=True).then_inc(adj_in[c], 16)

            def load_x(c, tile):
                sp.dma_start(X[:, c, :], x2[bass.ds(tile, 1)].rearrange("a r d -> (a r) d")).then_inc(x_in[c], 16)

            for i, b in enumerate(BIASES):
                sp.dma_start(raw[32 * i:32 * i + 2, :], b.partition_broadcast(2)).then_inc(rows_in, 16)
            for n, (src, _, _) in enumerate(pieces):
                if n == 2:
                    sp.wait_ge(rows_ok, 4 * len(BIASES))
                if n >= slots:
                    sp.wait_ge(split_lo, n - slots + 1)
                sp.dma_start(stage(n), src).then_inc(stage_in[n % slots], 16)
                if n == 1:
                    sp.wait_ge(consts_ok, 7)
                    for c in range(CH):
                        load(c, c)
                        load_x(c, c)
            for i in range(2):
                sp.sem_inc(out_stored[i], 16)
            with sp.Fori(0, iters) as it:
                nxt = sp.snap(((it + 1) % iters) * CH)
                t0 = sp.snap(it * CH)
                now = [sp.snap(t0 + (c + 1)) for c in range(CH)]
                for c in range(CH):
                    sp.wait_ge(adjT_ps, now[c])
                    sp.wait_ge(cm_ok, now[c])
                    load(c, nxt + c)
                for c in range(CH):
                    sp.wait_ge(z4, now[c])
                    load_x(c, nxt + c)
                    if c:
                        store(c - 1)
                    def store(c):
                        sp.wait_ge(x4_ok, now[c])
                        sp.dma_start(out_rows[bass.ds(t0 + c, 1)].rearrange("a r d -> (a r) d"), Z[:, c % 2, :])\
                            .then_inc(out_stored[c % 2], 16)
                store(CH - 1)
            for c in range(CH):
                sp.wait_ge(x_in[c], 16 * (iters + 1))
                sp.wait_ge(adj_in[c], 64 * (iters + 1))
            for i in range(2):
                sp.wait_ge(out_stored[i], 16 * (iters * CH // 2 + 1))

        @block.gpsimd
        def _(pool):
            pool.memset(ident[:, :], 0.0).then_inc(ident0, 1)
            pool.wait_ge(ident0, 1)
            pool.affine_select(out=ident[:, :], in_=ident[:, :], compare_op=ALU.not_equal, fill=1.0, base=0,
                               pattern=[[-1, P]], channel_multiplier=1).then_inc(consts_ok, 1)
            pool.memset(ones_row[:, :].bitcast(F32), 1.0).then_inc(consts_ok, 1)
            pool.memset(mhalf[:, :], -0.5).then_inc(consts_ok, 1)
            pool.memset(A[:, :, :], 0.0).then_inc(consts_ok, 1)
            pool.memset(inside[:, :], 0.0).then_inc(blocks0, 1)
            pool.memset(outside[:, :], -OUTSIDE).then_inc(blocks0, 1)
            pool.wait_ge(blocks0, 2)
            for g in range(P // C):
                b = slice(g * C, (g + 1) * C)
                pool.memset(inside[b, b], 1.0)
                pool.memset(outside[b, b], 0.0).then_inc(consts_ok, 1)
            pool.wait_ge(consts_ok, 6)
            pool.tensor_copy(identr[:, :], ident[:, :]).then_inc(consts_ok, 1)

            def alone(sem, value):
                pool.wait_ge(blocks0, 2)
                pool.wait_ge(sem, value)

            def rstd(c, n, mv, ve):
                alone(mv, n[c])
                pool.tensor_scalar(col(c, VE), col(c, MV + 1), EPS, None, ALU.add).then_inc(ve, 1)
                pool.wait_ge(ve, n[c])
                return pool.tensor_tensor(col(c, RS), col(c, VE), mhalf[:, :], ALU.pow)

            def cm(c, n, loaded):
                alone(adj_in[c], loaded)
                pool.tensor_copy(col(c, MC), mcol[:, c, 0:1]).then_inc(mc_ok, 1)
                alone(mc_ok, n[c])
                pool.tensor_scalar(MM[:, :], mrow[:, c, :], col(c, MC), None, ALU.mult).then_inc(mm_ok, 1)
                alone(mm_ok, n[c])
                pool.tensor_scalar(BT[:, :], MM[:, :], MASKED, -MASKED, ALU.mult, ALU.add).then_inc(bt1, 1)
                pool.wait_ge(bt1, n[c])
                pool.tensor_tensor(BT[:, :], BT[:, :], inside[:, :], ALU.mult).then_inc(bt2, 1)
                pool.tensor_tensor(MM[:, :], MM[:, :], inside[:, :], ALU.mult).then_inc(mm2, 1)
                pool.wait_ge(bt2, n[c])
                pool.tensor_tensor(BS[:, c, :], BT[:, :], outside[:, :], ALU.add).then_inc(bs_ok, 1)
                alone(exp_adj, n[c])
                pool.tensor_scalar(Cm[:, c, :], Cm[:, c, :], LD, None, ALU.mult).then_inc(cm1, 1)
                alone(bs_ok, n[c])
                pool.tensor_scalar(BT[:, :], A[:, c, :], LG, None, ALU.mult).then_inc(bt3, 1)
                pool.wait_ge(bt3, n[c])
                pool.tensor_tensor(Cm[:, c, :], Cm[:, c, :], BT[:, :], ALU.add).then_inc(cm2, 1)
                pool.wait_ge(cm2, n[c])
                pool.tensor_tensor(Cm[:, c, :], Cm[:, c, :], MM[:, :], ALU.mult).then_inc(cm_ok, 1)

            with pool.Fori(0, iters) as it:
                now = [pool.to_reg(it * CH + (c + 1)) for c in range(CH)]
                loaded = pool.to_reg(it * 64 + 64)
                for step, c in ORDER:
                    if step == "cm":
                        cm(c, now, loaded)
                    if step == "rs3":
                        rstd(c, now, mv3, ve3).then_inc(rs3, 1)
                    if step == "rs4":
                        rstd(c, now, mv4, ve4).then_inc(rs4, 1)

        def T(W, c):
            return W[:, :, c * P:(c + 1) * P]

        def by_chunk(ps):
            return ps[:, :].rearrange("p (k j) -> p k j", k=KD)

        def by_pair(ps):
            return ps[:, :].rearrange("p (m j) -> p m j", m=2)

        def bank(p, b):
            return (psA, psB)[b % 2][2 * p + b // 2]

        @block.scalar
        def _(act):
            act.wait_ge(rows_in, 16 * len(BIASES))
            for i in range(len(BIASES)):
                q = slice(32 * i, 32 * i + 2)
                act.copy(rows[q, :], raw[q, :]).then_inc(rows_ok, 1)
            for n, (_, hi, _) in enumerate(pieces):
                act.wait_ge(stage_in[n % slots], 16 * (n // slots + 1))
                act.copy(hi, stage(n)).then_inc(split_hi, 1)

            def adjT(c, n):
                act.wait_ge(adjT_ps, n[c])
                act.copy(AT[:, c, :], psB[c][:, 0:P]).then_inc(at_sb, 1)

            first = [c + 1 for c in range(CH)]
            for step, c in ORDER_PREP:
                if step == "adjT":
                    adjT(c, first)
            with act.Fori(0, iters) as it:
                n = [act.to_reg(it * CH + (c + 1)) for c in range(CH)]
                nxt = [act.to_reg(it * CH + (CH + c + 1)) for c in range(CH)]
                pair = [act.to_reg(it * 2 + (p + 1)) for p in range(2)]
                adj_loaded = act.to_reg(it * 64 + 64)
                for step, c in ORDER:
                    if step in ("t0", "t1", "t2"):
                        i = int(step[1])
                        act.wait_ge(t_ps[i], n[c])
                        act.copy(T(Th, c), by_chunk(psA[c])).then_inc(th[i], 1)
                    if step in ("g0", "g1"):
                        i = int(step[1])
                        act.wait_ge(g_ps[i], n[c])
                        act.activation(H[:, c, :], psB[c][:, :], ACT.Relu).then_inc(g_sb[i], 1)
                    if step == "cm":
                        act.wait_ge(adj_in[c], adj_loaded)
                        act.activation(Cm[:, c, :], A[:, c, :], ACT.Exp, scale=-1.0).then_inc(exp_adj, 1)
                    if step == "xp":
                        act.wait_ge(xp_ps, n[c])
                        act.copy(T(Th, c), by_chunk(psA[c])).then_inc(xph, 1)
                    if step == "v":
                        act.wait_ge(v_ps, n[c])
                        act.copy(H[:, c, :], psB[c][:, :]).then_inc(v_sb, 1)
                    if step == "qk":
                        for b in (0, 2):
                            act.wait_ge(qk_ps[b], pair[c])
                            act.copy(QK[:, 2 * b:2 * b + 2, :], by_pair(bank(c, b))).then_inc(qk_sb[b], 1)
                    if step == "sm":
                        act.wait_ge(nb_ok, n[c])
                        for h in range(HEADS):
                            ps = (psA, psB)[h // HG][c]
                            last = act.activation(E[:, c, h, :], ps[:, h % HG * P:(h % HG + 1) * P], ACT.Exp,
                                                  bias=col(c, NB + h), scale=SCALE, accum_out=col(c, SUM + h))
                        last.then_inc(ex_ok, 1)
                    if step == "ta":
                        act.wait_ge(ta_psA, n[c])
                        act.copy(AA[:, c % 2, 0:HG, :], by_chunk(psA[c])).then_inc(ta_sbA, 1)
                    if step == "av":
                        act.wait_ge(av_ps, n[c])
                        act.copy(T(Th, c), by_chunk(psA[c])).then_inc(avh, 1)
                    if step == "adjT":
                        adjT(c, nxt)

        @block.vector
        def _(dve):
            dve.wait_ge(consts_ok, 7)
            for i in range(len(BIASES)):
                q = slice(32 * i, 32 * i + 2)
                hi, lo = rows[q, :], raw[q, :]
                dve.wait_ge(rows_ok, 4 + 3 * i)
                dve.tensor_tensor(lo, lo, hi.bitcast(F32), ALU.subtract).then_inc(rows_ok, 1)
                dve.wait_ge(rows_ok, 5 + 3 * i)
                dve.tensor_scalar(lo, lo, ident[q, 32 * i + 1:32 * i + 2], None, ALU.mult).then_inc(rows_ok, 1)
                dve.wait_ge(rows_ok, 6 + 3 * i)
                dve.scalar_tensor_tensor(hi, hi.bitcast(F32), ident[q, 32 * i:32 * i + 1], lo, ALU.mult, ALU.add).then_inc(rows_ok, 1)
            for n, (_, hi, lo) in enumerate(pieces):
                dve.wait_ge(split_hi, n + 1)
                dve.tensor_tensor(lo, stage(n), hi.bitcast(F32), ALU.subtract).then_inc(split_lo, 1)

            def alone(sem, value):
                dve.wait_ge(blocks0, 2)
                dve.wait_ge(sem, value)

            def rest(lo, ps, hi):
                return dve.tensor_tensor(lo, ps, hi.bitcast(F32), ALU.subtract)

            def stats(src, c, n, bn, mv):
                dve.bn_stats(col(c, BN, 6), src).then_inc(bn, 1)
                alone(bn, n[c])
                dve.bn_aggr(col(c, MV, 2), col(c, BN, 6)).then_inc(mv, 1)

            with dve.Fori(0, iters) as it:
                n = [dve.to_reg(it * CH + (c + 1)) for c in range(CH)]
                pair = [dve.to_reg(it * 2 + (p + 1)) for p in range(2)]
                stored = [dve.to_reg(it * 32 + 16 * (r + 1)) for r in range(2)]
                for step, c in ORDER:
                    if step in ("t0", "t1", "t2"):
                        i = int(step[1])
                        dve.wait_ge(th[i], n[c])
                        rest(T(Tl, c), by_chunk(psA[c]), T(Th, c)).then_inc(t_sb[i], 1)
                    if step == "z3":
                        dve.wait_ge(g_ps[2], n[c])
                        dve.tensor_tensor(X[:, c, :], psB[c][:, :], X[:, c, :], ALU.add).then_inc(z3, 1)
                        dve.wait_ge(z3, n[c])
                        stats(X[:, c, :], c, n, bn3, mv3)
                    if step == "x3":
                        dve.wait_ge(rs3, n[c])
                        dve.tensor_scalar(X[:, c, :], X[:, c, :], col(c, MV), col(c, RS), ALU.subtract, ALU.mult).then_inc(x3_ok, 1)
                    if step == "xp":
                        dve.wait_ge(xph, n[c])
                        rest(T(Tl, c), by_chunk(psA[c]), T(Th, c)).then_inc(xp_sb, 1)
                    if step == "qk":
                        for b in (1, 3):
                            dve.wait_ge(qk_ps[b], pair[c])
                            dve.tensor_copy(QK[:, 2 * b:2 * b + 2, :], by_pair(bank(c, b))).then_inc(qk_sb[b], 1)
                    if step == "s":
                        dve.wait_ge(s_psA, n[c])
                        dve.reduce_max(col(c, NMX, HG), by_chunk(psA[c]), AX.X)
                        dve.wait_ge(s_psB, n[c])
                        dve.reduce_max(col(c, NMX + HG, HG), by_chunk(psB[c]), AX.X).then_inc(max_ok, 1)
                        dve.wait_ge(max_ok, n[c])
                        dve.tensor_scalar(col(c, NB, HEADS), col(c, NMX, HEADS), -SCALE, None, ALU.mult).then_inc(nb_ok, 1)
                    if step == "sm":
                        dve.wait_ge(ex_ok, n[c])
                        dve.reciprocal(col(c, REC, HEADS), col(c, SUM, HEADS)).then_inc(rec_ok, 1)
                        dve.wait_ge(rec_ok, n[c])
                        dve.tensor_scalar(col(c, RLA, HEADS), col(c, REC, HEADS), LA, None, ALU.mult).then_inc(rla_ok, 1)
                        dve.wait_ge(rla_ok, n[c])
                        dve.wait_ge(cm_ok, n[c])
                        for h in range(HEADS):
                            last = dve.scalar_tensor_tensor(E[:, c, h, :], E[:, c, h, :], col(c, RLA + h), Cm[:, c, :],
                                                            ALU.mult, ALU.add)
                        last.then_inc(attn_ok, 1)
                    if step == "ta":
                        dve.wait_ge(ta_psB, n[c])
                        dve.tensor_copy(AA[:, c % 2, HG:HEADS, :], by_chunk(psB[c])).then_inc(ta_sbB, 1)
                    if step == "av":
                        dve.wait_ge(avh, n[c])
                        rest(T(Tl, c), by_chunk(psA[c]), T(Th, c)).then_inc(av_sb, 1)
                    if step == "z4":
                        dve.wait_ge(wo_ps, n[c])
                        dve.wait_ge(out_stored[c % 2], stored[c // 2])
                        dve.tensor_tensor(Z[:, c % 2, :], psA[c][:, :], X[:, c, :], ALU.add).then_inc(z4, 1)
                        dve.wait_ge(z4, n[c])
                        stats(Z[:, c % 2, :], c, n, bn4, mv4)
                    if step == "x4":
                        dve.wait_ge(rs4, n[c])
                        dve.tensor_scalar(Z[:, c % 2, :], Z[:, c % 2, :], col(c, MV), col(c, RS), ALU.subtract, ALU.mult)\
                            .then_inc(x4_ok, 1)

        @block.tensor
        def _(pe):
            pe.wait_ge(consts_ok, 7)

            def products(out, terms):
                for i, (lhsT, rhs) in enumerate(terms):
                    mm = pe.matmul(out, lhsT, rhs, start=i == 0, stop=i == len(terms) - 1)
                return mm

            def three(lh, ll, rh, rl):
                return [(lh, rh), (lh, rl), (ll, rh)]

            def bias(i):
                return [(ones_row[32 * i:32 * i + 2, :], rows[32 * i:32 * i + 2, :])]

            def project(out, c, W, terms=()):
                terms = list(terms)
                for k in range(KD):
                    terms += three(T(Th, c)[:, k, :], T(Tl, c)[:, k, :], W[0][:, k, :], W[1][:, k, :])
                return products(out, terms)

            def adjT(c, k):
                pe.wait_ge(adj_in[c], k)
                pe.transpose(psB[c][:, 0:P], A[:, c, :], ident[:, :]).then_inc(adjT_ps, 1)

            for step, c in ORDER_PREP:
                if step == "adjT":
                    adjT(c, 64)
            pe.wait_ge(split_lo, len(pieces))
            pe.wait_ge(rows_ok, 4 * len(BIASES))
            with pe.Fori(0, iters) as it:
                n = [pe.to_reg(it * CH + (c + 1)) for c in range(CH)]
                pair = [pe.to_reg(it * 2 + (p + 1)) for p in range(2)]
                loaded, x_loaded = pe.to_reg(it * 64 + 128), pe.to_reg(it * 16 + 16)
                for step, c in ORDER:
                    if step in ("t0", "t1", "t2"):
                        i = int(step[1])
                        if i == 0:
                            pe.wait_ge(at_sb, n[c])
                            pe.wait_ge(x_in[c], x_loaded)
                        else:
                            pe.wait_ge(g_sb[i - 1], n[c])
                        for k in range(KD):
                            f = slice(k * P, (k + 1) * P)
                            mm = products(psA[c][:, f], [((H if i else X)[:, c, f], AT[:, c, :])])
                        mm.then_inc(t_ps[i], 1)
                    if step in ("g0", "g1", "g2"):
                        i = int(step[1])
                        pe.wait_ge(t_sb[i], n[c])
                        project(psB[c][:, :], c, GW[i], bias(i)).then_inc(g_ps[i], 1)
                    if step == "xp":
                        pe.wait_ge(x3_ok, n[c])
                        for k in range(KD):
                            mm = pe.transpose(psA[c][:, k * P:(k + 1) * P], X[:, c, k * P:(k + 1) * P], ident[:, :])
                        mm.then_inc(xp_ps, 1)
                    if step == "v":
                        pe.wait_ge(xp_sb, n[c])
                        project(psB[c][:, :], c, (WQh[:, :, 2, :], WQl[:, :, 2, :])).then_inc(v_ps, 1)
                    if step == "qk":
                        pe.wait_ge(v_sb, n[2 * c + 1])
                        cols = slice(2 * c * P, (2 * c + 2) * P)
                        for b in range(4):
                            for m in range(2):
                                i, f = divmod((2 * b + m) * P, D)
                                terms = []
                                for k in range(KD):
                                    terms += three(WQh[:, k, i, f:f + P], WQl[:, k, i, f:f + P], Th[:, k, cols], Tl[:, k, cols])
                                mm = products(bank(c, b)[:, m * 2 * P:(m + 1) * 2 * P], terms)
                            mm.then_inc(qk_ps[b], 1)
                    if step == "s":
                        if c % 2 == 0:
                            for b in range(4):
                                pe.wait_ge(qk_sb[b], pair[c // 2])
                        pe.wait_ge(bs_ok, n[c])
                        rows_c = slice(c % 2 * P, (c % 2 + 1) * P)
                        for ps in (psA, psB):
                            pe.matmul(ps[c][:, :], identr[:, :], BS[:, c, :].unsqueeze(1).to_broadcast([P, HG, P]), start=True, stop=False)
                        for m in range(HG):
                            for odd, ps in enumerate((psA, psB)):
                                q = slice(odd * DHEAD, (odd + 1) * DHEAD)
                                mm = pe.matmul(ps[c][:, m * P:(m + 1) * P], QK[q, m, rows_c], QK[q, KD + m, rows_c],
                                               start=False, stop=m == HG - 1)
                                if m == HG - 1:
                                    mm.then_inc((s_psA, s_psB)[odd], 1)
                    if step == "ta":
                        pe.wait_ge(attn_ok, n[c])
                        for ps, h0, ready in ((psA, 0, ta_psA), (psB, HG, ta_psB)):
                            for h in range(h0, h0 + HG):
                                mm = pe.transpose(ps[c][:, (h - h0) * P:(h - h0 + 1) * P], E[:, c, h, :], ident[:, :])
                            mm.then_inc(ready, 1)
                    if step == "av":
                        pe.wait_ge(ta_sbA, n[c])
                        pe.wait_ge(ta_sbB, n[c])
                        for h in range(HEADS):
                            q, m = slice(h % 2 * DHEAD, (h % 2 + 1) * DHEAD), h // 2
                            mm = pe.matmul(psA[c][q, m * P:(m + 1) * P], H[:, c, h * DHEAD:(h + 1) * DHEAD],
                                           AA[:, c % 2, h % 2 * HG + m, :], start=True, stop=True)
                        mm.then_inc(av_ps, 1)
                    if step == "wo":
                        pe.wait_ge(av_sb, n[c])
                        project(psA[c][:, :], c, (WOh, WOl), bias(3)).then_inc(wo_ps, 1)
                    if step == "adjT":
                        adjT(c, loaded)


def kernel(**inputs):
    import numpy as np
    import concourse.bacc as bacc
    from concourse.bass_utils import run_bass_kernel_spmd

    nc = bacc.Bacc("TRN2", target_bir_lowering=False, num_devices=1)
    given = {k: np.asarray(v) for k, v in inputs.items()}
    n, c, d = given["x"].shape
    tiles = n * c // P
    mask = given["nodemask"].reshape(tiles, P)
    arrays = {
        "x": given["x"], "adj": given["adj"], "mask_rows": mask, "mask_cols": mask.T,
        "L0_W1T": given["L0_gnn_W1"].T, "L0_b1": given["L0_gnn_b1"], "L0_gamma": given["L0_gnn_gamma"],
        "L0_beta": given["L0_gnn_beta"], "L0_W2T": given["L0_gnn_W2"].T, "L0_b2": given["L0_gnn_b2"],
        "L1_w": given["L1_gnn_w"], "L1_wT": given["L1_gnn_w"].T, "L1_a": given["L1_gnn_a"],
        "L2_W1": given["L2_gnn_W1"], "L2_b1": given["L2_gnn_b1"], "L2_W2": given["L2_gnn_W2"], "L2_b2": given["L2_gnn_b2"],
        "L2_W3": given["L2_gnn_W3"], "L2_b3": given["L2_gnn_b3"],
        "L3_Wqkv": given["L3_gnn_W_qkv"], "L3_Wout": given["L3_gnn_W_out"], "L3_bout": given["L3_gnn_b_out"],
    }
    arrays = {k: np.ascontiguousarray(v) for k, v in arrays.items()}
    ap = {k: nc.dram_tensor("in_" + k, v.shape, mybir.dt.from_np(v.dtype), kind="ExternalInput").ap() for k, v in arrays.items()}
    out = nc.dram_tensor("out", (n, c, d), F32, kind="ExternalOutput").ap()
    x2 = nc.dram_tensor("x2", (tiles, P, d), F32, kind="Internal").ap()
    semaphores = []
    hypergraph_and_pairwise(nc, semaphores, ap["x"], ap["adj"], ap["L0_W1T"], ap["L0_b1"], ap["L0_gamma"], ap["L0_beta"],
                            ap["L0_W2T"], ap["L0_b2"], ap["L1_w"], ap["L1_wT"], ap["L1_a"], x2)
    nc.clear_and_free_semaphores(semaphores)
    nc.all_engine_barrier()
    convolutions_and_attention(nc, [], x2, ap["adj"], ap["mask_rows"], ap["mask_cols"], ap["L2_W1"], ap["L2_b1"],
                               ap["L2_W2"], ap["L2_b2"], ap["L2_W3"], ap["L2_b3"], ap["L3_Wqkv"], ap["L3_Wout"],
                               ap["L3_bout"], out)
    r = run_bass_kernel_spmd(nc, [{"in_" + k: v for k, v in arrays.items()}], core_ids=[0])
    return r.results[0]["out"]
```

```python
from contextlib import ExitStack

import concourse.bass as bass
from concourse import mybir
from concourse.alu_op_type import AluOpType as ALU

F32 = mybir.dt.float32
F32R = mybir.dt.float32r
U8 = mybir.dt.uint8
ACT = mybir.ActivationFunctionType
AX = mybir.AxisListType

P = 128
C = 64
D = 512
DH = 1024
CH = 4
EPS = 1e-5
TINY = 1.2e-38
KD, KH = D // P, DH // P



def order(text):
    return [(step, int(chain.rstrip("+")), int(chain.endswith("+"))) for step, chain in (e.split(".") for e in text.split())]


def counts(it, reg):
    return [[reg(it * CH + (a * CH + c + 1)) for c in range(CH)] for a in (0, 1)]


def number(value):
    return value


def hypergraph_and_pairwise(nc, semaphores, x, adj, W1T, b1, gamma, beta, W2T, b2, w, wT, a, x2, slots, later):
    tiles = x.shape[0] * x.shape[1] // P
    iters = tiles // CH
    x_rows = x.rearrange("(t g) c d -> t (g c) d", g=P // C)
    adj_t = adj.rearrange("(t g) c e -> t g c e", g=P // C)

    with ExitStack() as ctx:
        def sb(name, shape, dt=F32):
            return ctx.enter_context(nc.sbuf_tensor(name, shape, dt))

        def sem(name):
            semaphores.append(nc.alloc_semaphore(name))
            return semaphores[-1]

        W1h, W1l = sb("W1h", [P, KD, DH], F32R), sb("W1l", [P, KD, DH], F32R)
        W2h, W2l = sb("W2h", [P, KH, D], F32R), sb("W2l", [P, KH, D], F32R)
        Wh, Wl = sb("Wh", [P, KD, D], F32R), sb("Wl", [P, KD, D], F32R)
        ident = sb("ident", [P, P])
        ones = sb("ones", [P, 2])
        b1_all = sb("b1_all", [P, DH])
        b2_all = sb("b2_all", [P, D])
        v_all = sb("v_all", [P, D])
        wa_all = sb("wa_all", [P, D])
        ubias = sb("ubias", [P, CH, D])
        gam = sb("gam", [P, KH])
        bet = sb("bet", [P, KH])
        a_col = sb("a_col", [P, KD])
        mhalf = sb("mhalf", [P, 1])
        A = sb("A", [P, CH, P])
        ATn = sb("ATn", [P, CH, P + 1])
        ATc = sb("ATc", [P, CH, P + 1])
        HT = sb("HT", [P, CH, P], F32R)
        HBh, HBl = sb("HBh", [P, CH, P], F32R), sb("HBl", [P, CH, P], F32R)
        DI = sb("DI", [P, CH, P])
        GT = sb("GT", [P, CH, P])
        Fp = sb("Fp", [P, CH, P])
        X = sb("X", [P, CH, D])
        Th, Tl = sb("Th", [P, CH, DH], F32R), sb("Tl", [P, CH, DH], F32R)
        R = sb("R", [P, CH, DH])
        sm = sb("sm", [P, CH, 40])
        WCOL, CNT, CNTM, BINV, G1, VE, RS, S, S8, RI, CI = range(11)
        MV, BN = 12, 14

        def col(c, k, n=1):
            return sm[:, c, k:k + n]

        psA = [ctx.enter_context(nc.psum_tensor(f"psA{c}", [P, D], F32)) for c in range(CH)]
        psB = [ctx.enter_context(nc.psum_tensor(f"psB{c}", [P, D], F32)) for c in range(CH)]

        consts_ok, ident0 = sem("consts_ok"), sem("ident0")
        vec_in, split_hi, split_lo, v_ps, v_sb, wa_ps, wa_sb = map(sem, (
            "vec_in", "split_hi", "split_lo", "v_ps", "v_sb", "wa_ps", "wa_sb"))
        load_in = [sem(f"load_in{i}") for i in range(KH // 2 + KD + 2)]
        wT_in = sem("wT_in")
        later_in = sem("later_in")
        adj_in = [sem(f"adj_in{c}") for c in range(CH)]
        x_in = [sem(f"x_in{c}") for c in range(CH)]
        x2_stored = [sem(f"x2_stored{c}") for c in range(CH)]
        (adjT_ps, adjT_sb, inc_sb, cnt_ok, cntm_ok, binv_ok, hbh_ok, hb_sb, deg_ps, dmx_ok, drec_ok, dinv_ok,
         gt_sb, g1_ps, g1_sb, adjT_cur, tx_ps, t1h, t1_sb, bias_ok, twice_ok, u_ok,
         r_psA, r_psB, b1_A, b1_B, r_sbA, r_sbB, bn1, mv1, ve1, rs1, rc_ok, g2_ok, t2_psA, t2_psB, t2hA, t2hB,
         t2_sb, y2_ps, z1, bn2, mv2, ve2, rs2, x1_ok, s_ok, s8_ok, sb_ps, tanh_ok, lrelu_ok, exp_ok,
         af_ok, t3_ps, t3h, ri_ok, t3_sb, y3_ps, z2, bn3, mv3, ve3, rs3, x2_ok) = map(sem, (
            "adjT_ps adjT_sb inc_sb cnt_ok cntm_ok binv_ok hbh_ok hb_sb deg_ps dmx_ok drec_ok dinv_ok "
            "gt_sb g1_ps g1_sb adjT_cur tx_ps t1h t1_sb bias_ok twice_ok u_ok "
            "r_psA r_psB b1_A b1_B r_sbA r_sbB bn1 mv1 ve1 rs1 rc_ok g2_ok t2_psA t2_psB t2hA t2hB "
            "t2_sb y2_ps z1 bn2 mv2 ve2 rs2 x1_ok s_ok s8_ok sb_ps tanh_ok lrelu_ok exp_ok "
            "af_ok t3_ps t3h ri_ok t3_sb y3_ps z2 bn3 mv3 ve3 rs3 x2_ok").split())

        W1v = W1T.rearrange("(k p) n -> p k n", p=P)
        W2v = W2T.rearrange("(k p) n -> p k n", p=P)
        wv = w.rearrange("(k p) n -> p k n", p=P)
        wTv = wT.rearrange("(k p) n -> p k n", p=P)
        spare = [ubias[:, c:c + 2, :] for c in (0, 2)]

        def two(slot):
            return slot.rearrange("p (k n) -> p k n", k=2)

        pieces = ([(W1v[:, k, :], slots[k], W1h[:, k, :], W1l[:, k, :], None) for k in range(KD)]
                  + [(W2v[:, k:k + 2, :], two(slots[KD + k // 2]), W2h[:, k:k + 2, :], W2l[:, k:k + 2, :], k) for k in range(0, KH, 2)]
                  + [(wv[:, k:k + 2, :], spare[k // 2], Wh[:, k:k + 2, :], Wl[:, k:k + 2, :], None) for k in (0, 2)])
        first_scaled, scaled_pieces = KD, KH // 2
        wT_raw = [two(slots[i])[:, k, :] for i in range(2) for k in range(2)]

        ORDER = order(
            "y1.2 relu.2 y2.0 rs1.1 st1.2 z1.0 tx.3 gs.1 txe.3 rs1.2 rs2.0 gs.2 u.3 adjT.0+ inc.0+ t2.1 cur.1 t2.2 "
            "y1.3 x1.0 t2e.1 deg.0+ t2e.2 y2.1 relu.3 g.0+ s8.0 st1.3 z1.1 cur.2 adjT.1+ rs2.1 sb.0 rs1.3 inc.1+ f.0 "
            "g1.0+ x1.1 s8.1 y2.2 t3.0 adjT.2+ z1.2 deg.1+ gs.3 t2.3 t3e.0 y3.0 inc.2+ rs2.2 sb.1 t2e.3 deg.2+ g.1+ "
            "g.2+ x1.2 f.1 y2.3 s8.2 adjT.3+ cur.3 g1.1+ sb.2 t3.1 z2.0 tx.0+ t3e.1 f.2 g1.2+ z1.3 rs2.3 rs3.0 txe.0+ "
            "inc.3+ y3.1 t3.2 cur.0+ t3e.2 y1.0+ x2.0 x1.3 sb.3 z2.1 deg.3+ g.3+ tx.1+ txe.1+ s8.3 relu.0+ y3.2 "
            "st1.0+ rs3.1 g1.3+ f.3 rs1.0+ z2.2 y1.1+ rs3.2 gs.0+ t3.3 t2.0+ tx.2+ t3e.3 x2.1 u.0+ x2.2 t2e.0+ txe.2+ "
            "u.1+ u.2+ y3.3 z2.3 rs3.3 relu.1+ st1.1+ x2.3")
        END = [e for e in ORDER if not e[2]]
        PREP = order("adjT.0+ inc.0+ adjT.1+ inc.1+ deg.0+ g.0+ adjT.2+ inc.2+ deg.1+ g.1+ g1.0+ adjT.3+ inc.3+ deg.2+ g.2+ g1.1+ "
                     "deg.3+ g.3+ g1.2+ g1.3+ w.0+ w.1+ w.2+ w.3+")
        START = [e for e in ORDER if e[2] and e not in PREP]
        need_W2 = min([i for i, e in enumerate(START) if e[0] in ("u", "y2", "x1")] or [len(START)])
        START = PREP + START[:need_W2] + [("w", n, 1) for n in range(KD, len(pieces))] + START[need_W2:]

        block = ctx.enter_context(nc.Block())

        @block.sync
        def _(sp):
            for c in range(CH):
                if c == 0:
                    sp.wait_ge(consts_ok, 4)
                for g in range(P // C):
                    sp.dma_start(A[g * C:(g + 1) * C, c, g * C:(g + 1) * C], adj_t[c, g]).then_inc(adj_in[c], 16)
                sp.dma_start(X[:, c, :], x_rows[c]).then_inc(x_in[c], 16)
            sp.dma_start(gam[:, :], gamma.rearrange("(k p) -> p k", p=P), allow_slow_non_contiguous=True).then_inc(vec_in, 16)
            sp.dma_start(bet[:, :], beta.rearrange("(k p) -> p k", p=P), allow_slow_non_contiguous=True).then_inc(vec_in, 16)
            sp.dma_start(a_col[:, :], a.rearrange("(k p) -> p k", p=P), allow_slow_non_contiguous=True).then_inc(vec_in, 16)
            sp.dma_start(b2_all[:, :], b2.partition_broadcast(P)).then_inc(vec_in, 16)
            sp.dma_start(b1_all[:, :], b1.partition_broadcast(P)).then_inc(vec_in, 16)
            for c in range(CH):
                sp.sem_inc(x2_stored[c], 16)
            for n, (src, raw, _, _, _) in enumerate(pieces):
                sp.dma_start(raw, src).then_inc(load_in[n], 16)
            for i in range(2):
                sp.wait_ge(split_lo, i + 1)
                sp.dma_start(two(slots[i]), wTv[:, 2 * i:2 * i + 2, :]).then_inc(wT_in, 16)
            sp.wait_ge(wa_ps, 1)
            for n, src in enumerate(later):
                sp.wait_ge(split_lo, n + 1)
                sp.dma_start(two(slots[n]), src).then_inc(later_in, 16)
            def store(t0):
                for c in range(CH):
                    sp.wait_ge(x2_ok, t0 + (c + 1))
                    sp.dma_start(x2[bass.ds(t0 + c, 1)].rearrange("a r d -> (a r) d"), R[:, c, 0:D]).then_inc(x2_stored[c], 16)

            with sp.Fori(0, iters - 1) as it:
                t0 = sp.snap(it * CH)
                for c in range(CH):
                    sp.wait_ge(inc_sb, sp.snap(t0 + (c + 1)))
                    for g in range(P // C):
                        sp.dma_start(A[g * C:(g + 1) * C, c, g * C:(g + 1) * C],
                                     adj_t[bass.ds(t0 + (CH + c), 1), g].rearrange("a c e -> (a c) e")).then_inc(adj_in[c], 16)
                for c in range(CH):
                    sp.wait_ge(z1, sp.snap(t0 + (c + 1)))
                    sp.dma_start(X[:, c, :], x_rows[bass.ds(t0 + (CH + c), 1)].rearrange("a r d -> (a r) d")).then_inc(x_in[c], 16)
                store(t0)
            store((iters - 1) * CH)
            sp.wait_ge(later_in, 16 * len(later))
            for c in range(CH):
                sp.wait_ge(x2_stored[c], 16 * (iters + 1))
                sp.wait_ge(x_in[c], 16 * iters)
                sp.wait_ge(adj_in[c], 32 * iters)

        @block.gpsimd
        def _(pool):
            pool.memset(ident[:, :], 0.0).then_inc(ident0, 1)
            pool.wait_ge(ident0, 1)
            pool.affine_select(out=ident[:, :], in_=ident[:, :], compare_op=ALU.not_equal, fill=1.0, base=0,
                               pattern=[[-1, P]], channel_multiplier=1).then_inc(consts_ok, 1)
            pool.memset(ones[:, :], 1.0).then_inc(consts_ok, 1)
            pool.memset(mhalf[:, :], -0.5).then_inc(consts_ok, 1)
            pool.memset(A[:, :, :], 0.0).then_inc(consts_ok, 1)

            def alone(sem, value):
                pool.wait_ge(consts_ok, 4)
                pool.wait_ge(sem, value)

            def rstd(c, n, mv, ve):
                alone(mv, n[c])
                pool.tensor_scalar(col(c, VE), col(c, MV + 1), EPS, None, ALU.add).then_inc(ve, 1)
                pool.wait_ge(ve, n[c])
                return pool.tensor_tensor(col(c, RS), col(c, VE), mhalf[:, :], ALU.pow)

            def cur(c, n):
                alone(gt_sb, n[c])
                pool.tensor_copy(ATc[:, c, :], ATn[:, c, :]).then_inc(adjT_cur, 1)

            def u(c, n):
                pool.wait_ge(tx_ps, n[c])
                pool.tensor_tensor(X[:, c, :], X[:, c, :], X[:, c, :], ALU.add).then_inc(twice_ok, 1)
                pool.wait_ge(twice_ok, n[c])
                pool.wait_ge(bias_ok, n[c])
                pool.tensor_tensor(X[:, c, :], X[:, c, :], ubias[:, c, :], ALU.add).then_inc(u_ok, 1)

            def rs_first(c, n):
                rstd(c, n, mv1, ve1).then_inc(rs1, 1)

            def rs_second(c, n):
                rstd(c, n, mv2, ve2).then_inc(rs2, 1)

            def rs_third(c, n):
                rstd(c, n, mv3, ve3).then_inc(rs3, 1)

            def steps(entries, it, reg):
                at = counts(it, reg)
                for step, c, ahead in entries:
                    n = at[ahead]
                    if step == "cur":
                        cur(c, n)
                    if step == "u":
                        u(c, n)
                    if step == "rs1":
                        rs_first(c, n)
                    if step == "rs2":
                        rs_second(c, n)
                    if step == "rs3":
                        rs_third(c, n)

            steps(START, -1, number)
            with pool.Fori(0, iters - 1) as it:
                steps(ORDER, it, pool.to_reg)
            steps(END, iters - 1, number)

        @block.scalar
        def _(act):
            def adjT(c, n, after=None):
                act.wait_ge(adjT_ps, n[c])
                if after:
                    act.wait_ge(adjT_cur, after[c])
                act.copy(ATn[:, c, 0:P], psB[c][:, 0:P]).then_inc(adjT_sb, 1)

            def txe(c, n):
                act.wait_ge(tx_ps, n[c])
                act.copy(Th[:, c, 0:D], psA[c][:, :]).then_inc(t1h, 1)

            def relu(c, n):
                act.wait_ge(b1_A, n[c])
                act.activation(R[:, c, 0:D], R[:, c, 0:D], ACT.Relu).then_inc(r_sbA, 1)
                act.wait_ge(b1_B, n[c])
                act.activation(R[:, c, D:DH], R[:, c, D:DH], ACT.Relu).then_inc(r_sbB, 1)

            def gs(c, n):
                act.wait_ge(rs1, n[c])
                act.mul(GT[:, c, :], GT[:, c, :], col(c, RS)).then_inc(g2_ok, 1)

            def t2e(c, n):
                act.wait_ge(t2_psA, n[c])
                act.copy(Th[:, c, 0:D], psA[c][:, :]).then_inc(t2hA, 1)
                act.wait_ge(t2_psB, n[c])
                act.copy(Th[:, c, D:DH], psB[c][:, :]).then_inc(t2hB, 1)

            def s8(c, n):
                act.wait_ge(s_ok, n[c])
                act.mul(col(c, S8), col(c, S), 0.125).then_inc(s8_ok, 1)

            def f(c, n):
                act.wait_ge(sb_ps, n[c])
                act.wait_ge(s8_ok, n[c])
                act.activation(Fp[:, c, :], psA[c][:, 0:P], ACT.Tanh, bias=col(c, S8), scale=0.125).then_inc(tanh_ok, 1)
                act.wait_ge(lrelu_ok, n[c])
                act.activation(Fp[:, c, :], Fp[:, c, :], ACT.Exp, scale=8.0).then_inc(exp_ok, 1)

            def t3e(c, n):
                act.wait_ge(t3_ps, n[c])
                act.copy(Th[:, c, 0:D], psA[c][:, :]).then_inc(t3h, 1)

            def w(i):
                _, raw, hi, _, scaled = pieces[i]
                act.wait_ge(load_in[i], 16)
                if scaled is None:
                    act.copy(hi, raw).then_inc(split_hi, 1)
                else:
                    if scaled == 0:
                        act.wait_ge(vec_in, 5 * 16)
                    act.activation(hi[:, 0, :], raw[:, 0, :], ACT.Copy, scale=gam[:, scaled:scaled + 1])
                    act.activation(hi[:, 1, :], raw[:, 1, :], ACT.Copy, scale=gam[:, scaled + 1:scaled + 2]).then_inc(split_hi, 1)
                if i == first_scaled + scaled_pieces - 1:
                    act.wait_ge(v_ps, scaled_pieces)
                    act.copy(v_all[:, :], psB[CH - 1][:, :]).then_inc(v_sb, 1)
                    act.wait_ge(wa_ps, 1)
                    act.copy(wa_all[:, :], psB[CH - 1][:, :]).then_inc(wa_sb, 1)

            def steps(entries, it, reg):
                at = counts(it, reg)
                for step, c, ahead in entries:
                    n = at[ahead]
                    if step == "w":
                        w(c)
                    if step == "adjT":
                        adjT(c, n, None if entries is START else at[ahead - 1])
                    if step == "txe":
                        txe(c, n)
                    if step == "relu":
                        relu(c, n)
                    if step == "gs":
                        gs(c, n)
                    if step == "t2e":
                        t2e(c, n)
                    if step == "s8":
                        s8(c, n)
                    if step == "f":
                        f(c, n)
                    if step == "t3e":
                        t3e(c, n)

            steps(START, -1, number)
            with act.Fori(0, iters - 1) as it:
                steps(ORDER, it, act.to_reg)
            steps(END, iters - 1, number)

        @block.vector
        def _(dve):
            def alone(sem, value):
                dve.wait_ge(consts_ok, 4)
                dve.wait_ge(sem, value)

            def inc(c, n):
                dve.wait_ge(adjT_sb, n[c])
                dve.tensor_tensor(col(c, WCOL), ATn[:, c, 0:1], ATn[:, c, C:C + 1], ALU.add)
                dve.reduce_sum(ATn[:, c, P:P + 1], A[:, c, :], AX.X)
                dve.tensor_scalar(HT[:, c, :], ATn[:, c, 0:P], 0.0, None, ALU.not_equal).then_inc(inc_sb, 1)
                dve.wait_ge(inc_sb, n[c])
                dve.reduce_sum(col(c, CNT), HT[:, c, :].bitcast(F32), AX.X).then_inc(cnt_ok, 1)
                dve.wait_ge(cnt_ok, n[c])
                dve.tensor_scalar(col(c, CNTM), col(c, CNT), 1.0, None, ALU.max).then_inc(cntm_ok, 1)
                dve.wait_ge(cntm_ok, n[c])
                dve.reciprocal(col(c, BINV), col(c, CNTM)).then_inc(binv_ok, 1)
                dve.wait_ge(binv_ok, n[c])
                dve.tensor_scalar(HBh[:, c, :], HT[:, c, :].bitcast(F32), col(c, BINV), None, ALU.mult).then_inc(hbh_ok, 1)
                dve.wait_ge(hbh_ok, n[c])
                dve.scalar_tensor_tensor(HBl[:, c, :], HT[:, c, :].bitcast(F32), col(c, BINV), HBh[:, c, :].bitcast(F32),
                                         ALU.mult, ALU.subtract).then_inc(hb_sb, 1)

            def g(c, n):
                dve.wait_ge(deg_ps, n[c])
                dve.tensor_scalar(DI[:, c, :], psB[c][:, P:2 * P], TINY, None, ALU.max).then_inc(dmx_ok, 1)
                dve.wait_ge(dmx_ok, n[c])
                dve.reciprocal(DI[:, c, :], DI[:, c, :]).then_inc(drec_ok, 1)
                dve.wait_ge(drec_ok, n[c])
                dve.scalar_tensor_tensor(DI[:, c, :], psB[c][:, P:2 * P], 0.0, DI[:, c, :], ALU.is_gt, ALU.mult).then_inc(dinv_ok, 1)
                dve.wait_ge(dinv_ok, n[c])
                dve.tensor_tensor(GT[:, c, :], psB[c][:, 2 * P:3 * P], DI[:, c, :], ALU.mult).then_inc(gt_sb, 1)

            def g1(c, n):
                dve.wait_ge(g1_ps, n[c])
                dve.tensor_copy(col(c, G1), psB[c][:, 3 * P + 2:3 * P + 3]).then_inc(g1_sb, 1)

            def txe(c, n):
                dve.wait_ge(t1h, n[c])
                dve.tensor_tensor(Tl[:, c, 0:D], psA[c][:, :], Th[:, c, 0:D].bitcast(F32), ALU.subtract).then_inc(t1_sb, 1)

            def relu(c, n, stored):
                dve.wait_ge(r_psA, n[c])
                dve.wait_ge(x2_stored[c], stored)
                dve.tensor_tensor(R[:, c, 0:D], psA[c][:, :], b1_all[:, 0:D], ALU.add).then_inc(b1_A, 1)
                dve.wait_ge(r_psB, n[c])
                dve.tensor_tensor(R[:, c, D:DH], psB[c][:, :], b1_all[:, D:DH], ALU.add).then_inc(b1_B, 1)

            def u(c, n):
                dve.wait_ge(g1_sb, n[c])
                dve.scalar_tensor_tensor(ubias[:, c, :], v_all[:, :], col(c, G1), b2_all[:, :], ALU.mult, ALU.add).then_inc(bias_ok, 1)

            def st1(c, n):
                dve.wait_ge(r_sbA, n[c])
                dve.bn_stats(col(c, BN, 6), R[:, c, 0:D])
                dve.wait_ge(r_sbB, n[c])
                dve.bn_stats(col(c, BN + 6, 6), R[:, c, D:DH]).then_inc(bn1, 1)
                alone(bn1, n[c])
                dve.bn_aggr(col(c, MV, 2), col(c, BN, 12)).then_inc(mv1, 1)
                alone(mv1, n[c])
                dve.tensor_scalar(R[:, c, :], R[:, c, :], col(c, MV), None, ALU.subtract).then_inc(rc_ok, 1)

            def t2e(c, n):
                dve.wait_ge(t2hA, n[c])
                dve.tensor_tensor(Tl[:, c, 0:D], psA[c][:, :], Th[:, c, 0:D].bitcast(F32), ALU.subtract)
                dve.wait_ge(t2hB, n[c])
                dve.tensor_tensor(Tl[:, c, D:DH], psB[c][:, :], Th[:, c, D:DH].bitcast(F32), ALU.subtract).then_inc(t2_sb, 1)

            def stats(c, n, bn, mv):
                dve.bn_stats(col(c, BN, 6), R[:, c, 0:D]).then_inc(bn, 1)
                alone(bn, n[c])
                dve.bn_aggr(col(c, MV, 2), col(c, BN, 6)).then_inc(mv, 1)

            def z_first(c, n):
                dve.wait_ge(y2_ps, n[c])
                dve.wait_ge(u_ok, n[c])
                dve.tensor_tensor(R[:, c, 0:D], psA[c][:, :], X[:, c, :], ALU.add).then_inc(z1, 1)
                dve.wait_ge(z1, n[c])
                stats(c, n, bn2, mv2)

            def x1(c, n):
                dve.wait_ge(rs2, n[c])
                dve.tensor_scalar(R[:, c, D:DH], R[:, c, 0:D], col(c, MV), col(c, RS), ALU.subtract, ALU.mult).then_inc(x1_ok, 1)
                dve.wait_ge(x1_ok, n[c])
                dve.tensor_tensor_reduce(R[:, c, 0:D], R[:, c, D:DH], wa_all[:, :], 1.0, 0.0, ALU.mult, ALU.add,
                                         col(c, S)).then_inc(s_ok, 1)

            def f(c, n):
                dve.wait_ge(tanh_ok, n[c])
                dve.scalar_tensor_tensor(Fp[:, c, :], Fp[:, c, :], 0.1, Fp[:, c, :], ALU.mult, ALU.max).then_inc(lrelu_ok, 1)
                dve.wait_ge(exp_ok, n[c])
                dve.wait_ge(adjT_cur, n[c])
                dve.tensor_tensor(Fp[:, c, :], Fp[:, c, :], ATc[:, c, 0:P], ALU.mult).then_inc(af_ok, 1)

            def t3e(c, n):
                dve.wait_ge(t3_ps, n[c])
                dve.reciprocal(col(c, RI), psB[c][:, P:P + 1]).then_inc(ri_ok, 1)
                dve.wait_ge(ri_ok, n[c])
                dve.tensor_tensor(col(c, CI), col(c, RI), ATc[:, c, P:P + 1], ALU.mult)
                dve.wait_ge(t3h, n[c])
                dve.tensor_tensor(Tl[:, c, 0:D], psA[c][:, :], Th[:, c, 0:D].bitcast(F32), ALU.subtract).then_inc(t3_sb, 1)

            def z_second(c, n, after):
                dve.wait_ge(y3_ps, n[c])
                dve.wait_ge(t3_sb, n[c])
                dve.scalar_tensor_tensor(R[:, c, 0:D], psA[c][:, :], col(c, CI), R[:, c, D:DH], ALU.mult, ALU.add).then_inc(z2, 1)
                dve.wait_ge(z2, after[c])
                stats(c, n, bn3, mv3)

            def x2_norm(c, n):
                dve.wait_ge(rs3, n[c])
                dve.tensor_scalar(R[:, c, 0:D], R[:, c, 0:D], col(c, MV), col(c, RS), ALU.subtract, ALU.mult).then_inc(x2_ok, 1)

            dve.wait_ge(consts_ok, 4)
            def w(i):
                _, raw, hi, lo, scaled = pieces[i]
                dve.wait_ge(split_hi, i + 1)
                if i == 0:
                    dve.wait_ge(vec_in, 5 * 16)
                if scaled is None:
                    dve.tensor_tensor(lo, raw, hi.bitcast(F32), ALU.subtract).then_inc(split_lo, 1)
                else:
                    dve.wait_ge(v_ps, i - first_scaled + 1)
                    for k in range(2):
                        last = dve.scalar_tensor_tensor(lo[:, k, :], raw[:, k, :], gam[:, scaled + k:scaled + k + 1],
                                                        hi[:, k, :].bitcast(F32), ALU.mult, ALU.subtract)
                    last.then_inc(split_lo, 1)
                if i == first_scaled + scaled_pieces - 1:
                    dve.wait_ge(v_sb, 1)
                    dve.wait_ge(wa_sb, 1)
                if i == len(pieces) - 1:
                    dve.wait_ge(split_lo, i + 1)

            def steps(entries, it, reg):
                at, stored = counts(it, reg), [reg(it * 16 + 16 * (a + 1)) for a in (0, 1)]
                for step, c, ahead in entries:
                    n = at[ahead]
                    if step == "w":
                        w(c)
                    if step == "inc":
                        inc(c, n)
                    if step == "g":
                        g(c, n)
                    if step == "g1":
                        g1(c, n)
                    if step == "txe":
                        txe(c, n)
                    if step == "relu":
                        relu(c, n, stored[ahead])
                    if step == "u":
                        u(c, n)
                    if step == "st1":
                        st1(c, n)
                    if step == "t2e":
                        t2e(c, n)
                    if step == "z1":
                        z_first(c, n)
                    if step == "x1":
                        x1(c, n)
                    if step == "f":
                        f(c, n)
                    if step == "t3e":
                        t3e(c, n)
                    if step == "z2":
                        z_second(c, n, at[ahead + 1])
                    if step == "x2":
                        x2_norm(c, n)

            dve.sem_inc(z2, CH)
            steps(START, -1, number)
            with dve.Fori(0, iters - 1) as it:
                steps(ORDER, it, dve.to_reg)
            steps(END, iters - 1, number)

        @block.tensor
        def _(pe):
            pe.wait_ge(consts_ok, 4)

            def products(out, terms, start=True):
                for i, (lhsT, rhs) in enumerate(terms):
                    mm = pe.matmul(out, lhsT, rhs, start=start and i == 0, stop=i == len(terms) - 1)
                return mm

            def three(lh, ll, rh, rl):
                return [(lh, rh), (lh, rl), (ll, rh)]

            def adjT(c, k):
                pe.wait_ge(adj_in[c], k)
                pe.transpose(psB[c][:, 0:P], A[:, c, :], ident[:, :]).then_inc(adjT_ps, 1)

            def deg(c, n):
                pe.wait_ge(hb_sb, n[c])
                products(psB[c][:, P:2 * P], [(col(c, WCOL).to_broadcast([P, P]), HT[:, c, :].bitcast(F32))])
                products(psB[c][:, 2 * P:3 * P], [(HBh[:, c, :], HT[:, c, :]), (HBl[:, c, :], HT[:, c, :])]).then_inc(deg_ps, 1)

            def g1(c, n):
                pe.wait_ge(gt_sb, n[c])
                products(psB[c][:, 3 * P + 2:3 * P + 3], [(GT[:, c, :], ones[:, 0:1])]).then_inc(g1_ps, 1)

            def mix(out, rows, M):
                for j in range(KD):
                    f = slice(j * P, (j + 1) * P)
                    mm = products(out[:, f], [(rows[:, f], M)])
                return mm

            def project(out, c, k, Rh, Rl):
                terms = []
                for j in range(k):
                    f = slice(j * P, (j + 1) * P)
                    terms += three(Th[:, c, f], Tl[:, c, f], Rh(j), Rl(j))
                return products(out, terms)

            def tx(c, n, loaded):
                pe.wait_ge(gt_sb, n[c])
                pe.wait_ge(x_in[c], loaded)
                pe.wait_ge(z2, n[c])
                mix(psA[c][:, :], X[:, c, :], GT[:, c, :]).then_inc(tx_ps, 1)

            def y1(c, n):
                pe.wait_ge(t1_sb, n[c])
                pe.wait_ge(g1_sb, n[c])
                for half, (ps, ready) in enumerate(((psA, r_psA), (psB, r_psB))):
                    h = slice(half * D, (half + 1) * D)
                    project(ps[c][:, :], c, KD, lambda j: W1h[:, j, h], lambda j: W1l[:, j, h]).then_inc(ready, 1)

            def t2(c, n):
                pe.wait_ge(rc_ok, n[c])
                pe.wait_ge(g2_ok, n[c])
                mix(psA[c][:, :], R[:, c, 0:D], GT[:, c, :]).then_inc(t2_psA, 1)
                mix(psB[c][:, :], R[:, c, D:DH], GT[:, c, :]).then_inc(t2_psB, 1)

            def y2(c, n):
                pe.wait_ge(t2_sb, n[c])
                project(psA[c][:, :], c, KH, lambda j: W2h[:, j, :], lambda j: W2l[:, j, :]).then_inc(y2_ps, 1)

            def sbc(c, n):
                pe.wait_ge(s_ok, n[c])
                products(psA[c][:, 0:P], [(col(c, S).to_broadcast([P, P]), ident[:, :])]).then_inc(sb_ps, 1)

            def t3(c, n, after):
                pe.wait_ge(af_ok, n[c])
                if after:
                    pe.wait_ge(g1_sb, after[c])
                products(psB[c][:, P:P + 1], [(Fp[:, c, :], ones[:, 0:1])])
                mix(psA[c][:, :], R[:, c, D:DH], Fp[:, c, :]).then_inc(t3_ps, 1)

            def y3(c, n):
                pe.wait_ge(t3_sb, n[c])
                project(psA[c][:, :], c, KD, lambda j: Wh[:, j, :], lambda j: Wl[:, j, :]).then_inc(y3_ps, 1)

            def w(i):
                if i == first_scaled - 1:
                    pe.wait_ge(split_lo, i + 1)
                v = i - first_scaled
                if 0 <= v < scaled_pieces:
                    pe.wait_ge(load_in[i], 16)
                    pe.wait_ge(vec_in, 5 * 16)
                    for k in range(2):
                        mm = pe.matmul(psB[CH - 1][:, :], bet[:, 2 * v + k:2 * v + k + 1].to_broadcast([P, P]), pieces[i][1][:, k, :],
                                       start=(v + k == 0), stop=(v == scaled_pieces - 1 and k == 1))
                    mm.then_inc(v_ps, 1)
                if v == scaled_pieces - 1:
                    pe.wait_ge(wT_in, 2 * 16)
                    pe.wait_ge(v_sb, 1)
                    products(psB[CH - 1][:, :], [(a_col[:, k:k + 1].to_broadcast([P, P]), wT_raw[k]) for k in range(KD)]).then_inc(wa_ps, 1)
                if i == len(pieces) - 1:
                    pe.wait_ge(split_lo, len(pieces))
                    pe.wait_ge(wa_sb, 1)

            def steps(entries, it, reg):
                at = counts(it, reg)
                adj_loaded, x_loaded = reg(it * 32 + 64), [reg(it * 16 + 16 * (a + 1)) for a in (0, 1)]
                for step, c, ahead in entries:
                    n = at[ahead]
                    if step == "w":
                        w(c)
                    if step == "adjT":
                        adjT(c, adj_loaded)
                    if step == "deg":
                        deg(c, n)
                    if step == "g1":
                        g1(c, n)
                    if step == "tx":
                        tx(c, n, x_loaded[ahead])
                    if step == "y1":
                        y1(c, n)
                    if step == "t2":
                        t2(c, n)
                    if step == "y2":
                        y2(c, n)
                    if step == "sb":
                        sbc(c, n)
                    if step == "t3":
                        t3(c, n, None if entries is END else at[ahead + 1])
                    if step == "y3":
                        y3(c, n)

            steps(START, -1, number)
            with pe.Fori(0, iters - 1) as it:
                steps(ORDER, it, pe.to_reg)
            steps(END, iters - 1, number)


HEADS, DHEAD = 8, 64
HG = HEADS // 2
LA = LD = LG = 0.33
SCALE = DHEAD ** -0.5
FLT_MAX = 3.4028234e38
MASKED = 2.0 ** 100
OUTSIDE = 2.0 ** 126


def convolutions_and_attention(nc, semaphores, x2, adj, mask_rows, mask_cols, E, AA, QK, slots, b1, b2, b3, Wqkv, bout, out):
    tiles = x2.shape[0]
    iters = tiles // CH
    out_rows = out.rearrange("(t g) c d -> t (g c) d", g=P // C)
    adj_t = adj.rearrange("(t g) c e -> t g c e", g=P // C)

    with ExitStack() as ctx:
        def sb(name, shape, dt=F32):
            return ctx.enter_context(nc.sbuf_tensor(name, shape, dt))

        def sem(name):
            semaphores.append(nc.alloc_semaphore(name))
            return semaphores[-1]

        W1hl, W2hl, W3hl, WO = [(sb(f"hi{i}", [P, KD, D], F32R), sb(f"lo{i}", [P, KD, D], F32R)) for i in range(4)]
        GW = [W1hl, W2hl, W3hl]
        WQh, WQl = sb("WQh", [P, KD, 3, D], F32R), sb("WQl", [P, KD, 3, D], F32R)
        ident = sb("ident2", [P, P])
        b1_all, b2_all, b3_all, bout_all = (sb(f"bias{i}_all", [P, D]) for i in range(4))
        inside = sb("inside", [P, P])
        outside = sb("outside", [P, P])
        mhalf = sb("mhalf2", [P, 1])
        A = sb("A2", [P, CH, P])
        AT = sb("AT", [P, CH, P])
        mrow = sb("mrow", [P, CH, P], U8)
        mcol = sb("mcol", [P, CH, 4], U8)
        MM, BT = sb("MM", [P, P]), sb("BT", [P, P])
        BS = sb("BS", [P, CH, P])
        Cm = sb("Cm", [P, CH, P])
        X = sb("X2", [P, CH, D])
        H = sb("H", [P, CH, D])
        Th, Tl = sb("T2h", [P, KD, CH * P], F32R), sb("T2l", [P, KD, CH * P], F32R)
        Z = sb("Z", [P, 2, D])
        sm = sb("sm2", [P, CH, 64])
        MC, VE, RS = range(3)
        MV, BN, NMX, NB, SUM, REC, RLA = 4, 8, 16, 24, 32, 40, 48

        def col(c, k, n=1):
            return sm[:, c, k:k + n]

        psA = [ctx.enter_context(nc.psum_tensor(f"qsA{c}", [P, D], F32)) for c in range(CH)]
        psB = [ctx.enter_context(nc.psum_tensor(f"qsB{c}", [P, D], F32)) for c in range(CH)]

        consts_ok, ident0, blocks0, bias_in, split_hi, split_lo = map(sem, (
            "consts_ok2", "ident02", "blocks0", "bias_in", "split_hi2", "split_lo2"))
        load_in = [sem(f"load2_in{i}") for i in range(KD)]
        adj_in = [sem(f"adj2_in{c}") for c in range(CH)]
        x_in = [sem(f"x2_in{c}") for c in range(CH)]
        out_stored = [sem(f"out_stored{i}") for i in range(2)]
        qk_ps, qk_sb = ([sem(f"{n}{b}") for b in range(4)] for n in ("qk_ps", "qk_sb"))
        b_ok = [sem(f"b_ok{i}") for i in range(2)]
        t_ps, th, t_sb, g_ps, g_sb = ([sem(f"{n}{i}") for i in range(3)] for n in ("t_ps", "th", "t_sb", "g_ps", "g_sb"))
        (adjT_ps, at_sb, mc_ok, mm_ok, bt1, bt2, bs_ok, mm2, exp_adj, cm1, bt3, cm2, cm_ok, b3_ok, bo_ok, z3, bn3, mv3,
         ve3, rs3, x3_ok, xp_ps, xph, xp_sb, v_ps, v_sb, s_psA, s_psB, max_ok, nb_ok, ex_ok, rec_ok, rla_ok, attn_ok,
         ta_psA, ta_psB, ta_sbA, ta_sbB, av_ps, avh, av_sb, wo_ps, z4, bn4, mv4, ve4, rs4, x4_ok) = map(sem, (
            "adjT_ps2 at_sb mc_ok mm_ok bt1 bt2 bs_ok mm2 exp_adj cm1 bt3 cm2 cm_ok b3_ok bo_ok z3 bn3_2 mv3_2 "
            "ve3_2 rs3_2 x3_ok xp_ps xph xp_sb v_ps2 v_sb2 s_psA s_psB max_ok nb_ok ex_ok rec_ok rla_ok attn_ok "
            "ta_psA ta_psB ta_sbA ta_sbB av_ps avh av_sb wo_ps z4 bn4 mv4 ve4 rs4 x4_ok").split())

        raw2 = [slot.rearrange("p (k n) -> p k n", k=2) for slot in slots]
        pieces = [(hi[:, k:k + 2, :], lo[:, k:k + 2, :]) for hi, lo in (W1hl, W2hl, W3hl, WO) for k in (0, 2)]
        pieces = [(raw, hi, lo) for raw, (hi, lo) in zip(raw2, pieces)]
        raw_qkv = [W.rearrange(pattern) for W, pattern in ((E[:, 0:2, :, :], "p c h j -> p (c h j)"), (E[:, 2:4, :, :], "p c h j -> p (c h j)"),
                                                           (AA[:, :, :, :], "p c h j -> p (c h j)"), (QK[:, :, :], "p k j -> p (k j)"))]
        raw_qkv = [W[:, 0:3 * D] for W in raw_qkv]
        by_head = [W.rearrange("p (h i d) -> p h i d", i=3, d=DHEAD) for W in raw_qkv]
        qkv_parts = [[W[:, k, :, :].rearrange("p i (h d) -> p h i d", d=DHEAD) for W in (WQh, WQl)] for k in range(KD)]

        ORDER = order(
            "b3.1 x3.0 b3.2 g1.2 t1.3 g2.1 z3.1 cm.2 t2.2 g1.3 rs3.1 b3.3 xp.0 bo.0 cm.3 x3.1 g2.2 t2.3 xp.1 z3.2 v.0 "
            "rs3.2 v.1 x3.2 g2.3 z3.3 rs3.3 xp.2 bo.1 x3.3 qk.0 xp.3 v.2 v.3 s.0 s.1 sm.0 sm.1 qk.1 ta.0 ta.1 s.2 "
            "av.0 s.3 sm.2 av.1 wo.0 z4.0 sm.3 ta.2 adjT.0+ wo.1 rs4.0 x4.0 t0.0+ z4.1 rs4.1 adjT.1+ ta.3 x4.1 av.2 "
            "g0.0+ av.3 bo.2 t0.1+ wo.2 z4.2 adjT.2+ t1.0+ g0.1+ wo.3 rs4.2 bo.3 x4.2 t0.2+ z4.3 cm.0+ rs4.3 adjT.3+ "
            "t1.1+ g1.0+ b3.0+ g0.2+ t2.0+ cm.1+ g1.1+ x4.3 t0.3+ t1.2+ g2.0+ z3.0+ g0.3+ rs3.0+ t2.1+")
        START, END = [e for e in ORDER if e[2]], [e for e in ORDER if not e[2]]
        PREP = [e for e in START if e[0] == "adjT"]
        START = PREP + [e for e in START if e not in PREP]

        def pair_counts(it, reg):
            return [[reg(it * 2 + (a * 2 + p + 1)) for p in range(2)] for a in (0, 1)]

        block = ctx.enter_context(nc.Block())

        @block.sync
        def _(sp):
            def load(c, tile):
                for g in range(P // C):
                    sp.dma_start(A[g * C:(g + 1) * C, c, g * C:(g + 1) * C],
                                 adj_t[bass.ds(tile, 1), g].rearrange("a c e -> (a c) e")).then_inc(adj_in[c], 16)
                sp.dma_start(mrow[:, c, :], mask_rows[bass.ds(tile, 1)].rearrange("a j -> (a j)").partition_broadcast(P))\
                    .then_inc(adj_in[c], 16)
                sp.dma_start(mcol[:, c, 0:1], mask_cols[:, bass.ds(tile, 1)], allow_slow_non_contiguous=True).then_inc(adj_in[c], 16)

            def load_x(c, tile):
                sp.dma_start(X[:, c, :], x2[bass.ds(tile, 1)].rearrange("a r d -> (a r) d")).then_inc(x_in[c], 16)

            for dst, b in ((b1_all, b1), (b2_all, b2), (b3_all, b3), (bout_all, bout)):
                sp.dma_start(dst[:, :], b.partition_broadcast(P)).then_inc(bias_in, 16)
            sp.wait_ge(consts_ok, 5)
            for c in range(CH):
                load(c, c)
                load_x(c, c)
            for k in range(KD):
                sp.wait_ge(split_lo, (4, 4, 6, 8)[k])
                sp.dma_start(raw_qkv[k], Wqkv[k * P:(k + 1) * P, :]).then_inc(load_in[k], 16)
            for i in range(2):
                sp.sem_inc(out_stored[i], 16)
            def store(c, t0):
                sp.wait_ge(x4_ok, t0 + (c + 1))
                sp.dma_start(out_rows[bass.ds(t0 + c, 1)].rearrange("a r d -> (a r) d"), Z[:, c % 2, :]).then_inc(out_stored[c % 2], 16)

            with sp.Fori(0, iters - 1) as it:
                t0 = sp.snap(it * CH)
                for c in range(CH):
                    sp.wait_ge(adjT_ps, sp.snap(t0 + (c + 1)))
                    sp.wait_ge(cm_ok, sp.snap(t0 + (c + 1)))
                    load(c, t0 + (CH + c))
                for c in range(CH):
                    sp.wait_ge(z4, sp.snap(t0 + (c + 1)))
                    load_x(c, t0 + (CH + c))
                    if c:
                        store(c - 1, t0)
                store(CH - 1, t0)
            for c in range(CH):
                store(c, (iters - 1) * CH)
            for c in range(CH):
                sp.wait_ge(x_in[c], 16 * iters)
                sp.wait_ge(adj_in[c], 64 * iters)
            for i in range(2):
                sp.wait_ge(out_stored[i], 16 * (iters * CH // 2 + 1))

        @block.gpsimd
        def _(pool):
            pool.memset(ident[:, :], 0.0).then_inc(ident0, 1)
            pool.wait_ge(ident0, 1)
            pool.affine_select(out=ident[:, :], in_=ident[:, :], compare_op=ALU.not_equal, fill=1.0, base=0,
                               pattern=[[-1, P]], channel_multiplier=1).then_inc(consts_ok, 1)
            pool.memset(mhalf[:, :], -0.5).then_inc(consts_ok, 1)
            pool.memset(A[:, :, :], 0.0).then_inc(consts_ok, 1)
            pool.memset(inside[:, :], 0.0).then_inc(blocks0, 1)
            pool.memset(outside[:, :], -OUTSIDE).then_inc(blocks0, 1)
            pool.wait_ge(blocks0, 2)
            for g in range(P // C):
                b = slice(g * C, (g + 1) * C)
                pool.memset(inside[b, b], 1.0)
                pool.memset(outside[b, b], 0.0).then_inc(consts_ok, 1)

            def alone(sem, value):
                pool.wait_ge(blocks0, 2)
                pool.wait_ge(sem, value)

            def rstd(c, n, mv, ve):
                alone(mv, n[c])
                pool.tensor_scalar(col(c, VE), col(c, MV + 1), EPS, None, ALU.add).then_inc(ve, 1)
                pool.wait_ge(ve, n[c])
                return pool.tensor_tensor(col(c, RS), col(c, VE), mhalf[:, :], ALU.pow)

            def cm(c, n, loaded):
                alone(adj_in[c], loaded)
                pool.tensor_copy(col(c, MC), mcol[:, c, 0:1]).then_inc(mc_ok, 1)
                alone(mc_ok, n[c])
                pool.tensor_scalar(MM[:, :], mrow[:, c, :], col(c, MC), None, ALU.mult).then_inc(mm_ok, 1)
                alone(mm_ok, n[c])
                pool.tensor_scalar(BT[:, :], MM[:, :], MASKED, -MASKED, ALU.mult, ALU.add).then_inc(bt1, 1)
                pool.wait_ge(bt1, n[c])
                pool.tensor_tensor(BT[:, :], BT[:, :], inside[:, :], ALU.mult).then_inc(bt2, 1)
                pool.tensor_tensor(MM[:, :], MM[:, :], inside[:, :], ALU.mult).then_inc(mm2, 1)
                pool.wait_ge(bt2, n[c])
                pool.tensor_tensor(BS[:, c, :], BT[:, :], outside[:, :], ALU.add).then_inc(bs_ok, 1)
                alone(exp_adj, n[c])
                pool.tensor_scalar(Cm[:, c, :], Cm[:, c, :], LD, None, ALU.mult).then_inc(cm1, 1)
                alone(bs_ok, n[c])
                pool.tensor_scalar(BT[:, :], A[:, c, :], LG, None, ALU.mult).then_inc(bt3, 1)
                pool.wait_ge(bt3, n[c])
                pool.tensor_tensor(Cm[:, c, :], Cm[:, c, :], BT[:, :], ALU.add).then_inc(cm2, 1)
                pool.wait_ge(cm2, n[c])
                pool.tensor_tensor(Cm[:, c, :], Cm[:, c, :], MM[:, :], ALU.mult).then_inc(cm_ok, 1)

            pool.wait_ge(bias_in, 4 * 16)
            def steps(entries, it, reg):
                at = counts(it, reg)
                loaded = [reg(it * 64 + 64 * (a + 1)) for a in (0, 1)]
                for step, c, ahead in entries:
                    n = at[ahead]
                    if step == "cm":
                        cm(c, n, loaded[ahead])
                    if step == "b3":
                        pool.wait_ge(t_ps[0], n[c])
                        pool.tensor_tensor(X[:, c, :], X[:, c, :], b3_all[:, :], ALU.add).then_inc(b3_ok, 1)
                    if step == "bo":
                        pool.wait_ge(xp_ps, n[c])
                        pool.tensor_tensor(X[:, c, :], X[:, c, :], bout_all[:, :], ALU.add).then_inc(bo_ok, 1)
                    if step == "rs3":
                        rstd(c, n, mv3, ve3).then_inc(rs3, 1)
                    if step == "rs4":
                        rstd(c, n, mv4, ve4).then_inc(rs4, 1)

            steps(PREP, -1, number)
            steps(START[len(PREP):], -1, number)
            with pool.Fori(0, iters - 1) as it:
                steps(ORDER, it, pool.to_reg)
            steps(END, iters - 1, number)

        def T(W, c):
            return W[:, :, c * P:(c + 1) * P]

        def by_chunk(ps):
            return ps[:, :].rearrange("p (k j) -> p k j", k=KD)

        def by_pair(ps):
            return ps[:, :].rearrange("p (m j) -> p m j", m=2)

        def bank(p, b):
            return (psA, psB)[b % 2][2 * p + b // 2]

        @block.scalar
        def _(act):
            def adjT(c, n):
                act.wait_ge(adjT_ps, n[c])
                act.copy(AT[:, c, :], psB[c][:, 0:P]).then_inc(at_sb, 1)

            def steps(entries, it, reg):
                at = counts(it, reg)
                pair, adj_loaded = pair_counts(it, reg), [reg(it * 64 + 64 * (a + 1)) for a in (0, 1)]
                for step, c, ahead in entries:
                    n = at[ahead]
                    if step in ("t0", "t1", "t2"):
                        i = int(step[1])
                        act.wait_ge(t_ps[i], n[c])
                        act.copy(T(Th, c), by_chunk(psA[c])).then_inc(th[i], 1)
                    if step in ("g0", "g1"):
                        i = int(step[1])
                        act.wait_ge(b_ok[i], n[c])
                        act.activation(H[:, c, :], H[:, c, :], ACT.Relu).then_inc(g_sb[i], 1)
                    if step == "cm":
                        act.wait_ge(adj_in[c], adj_loaded[ahead])
                        act.activation(Cm[:, c, :], A[:, c, :], ACT.Exp, scale=-1.0).then_inc(exp_adj, 1)
                    if step == "xp":
                        act.wait_ge(xp_ps, n[c])
                        act.copy(T(Th, c), by_chunk(psA[c])).then_inc(xph, 1)
                    if step == "v":
                        act.wait_ge(v_ps, n[c])
                        act.copy(H[:, c, :], psB[c][:, :]).then_inc(v_sb, 1)
                    if step == "qk":
                        for b in (0, 2):
                            act.wait_ge(qk_ps[b], pair[ahead][c])
                            act.copy(QK[:, 2 * b:2 * b + 2, :], by_pair(bank(c, b))).then_inc(qk_sb[b], 1)
                    if step == "sm":
                        act.wait_ge(nb_ok, n[c])
                        for h in range(HEADS):
                            last = act.activation(E[:, c, h, :], E[:, c, h, :], ACT.Exp, bias=col(c, NB + h), scale=SCALE,
                                                  accum_out=col(c, SUM + h))
                        last.then_inc(ex_ok, 1)
                    if step == "ta":
                        act.wait_ge(ta_psA, n[c])
                        act.copy(AA[:, c % 2, 0:HG, :], by_chunk(psA[c])).then_inc(ta_sbA, 1)
                    if step == "av":
                        act.wait_ge(av_ps, n[c])
                        act.copy(T(Th, c), by_chunk(psA[c])).then_inc(avh, 1)
                    if step == "adjT":
                        adjT(c, n)

            for raw_piece, hi, _ in pieces:
                act.copy(hi, raw_piece).then_inc(split_hi, 1)
            steps(PREP, -1, number)
            for k in range(KD):
                act.wait_ge(load_in[k], 16)
                act.copy(qkv_parts[k][0], by_head[k]).then_inc(split_hi, 1)
            steps(START[len(PREP):], -1, number)
            with act.Fori(0, iters - 1) as it:
                steps(ORDER, it, act.to_reg)
            steps(END, iters - 1, number)

        @block.vector
        def _(dve):
            dve.wait_ge(consts_ok, 5)
            dve.wait_ge(bias_in, 4 * 16)
            for n, (raw_piece, hi, lo) in enumerate(pieces):
                dve.wait_ge(split_hi, n + 1)
                dve.tensor_tensor(lo, raw_piece, hi.bitcast(F32), ALU.subtract).then_inc(split_lo, 1)
            for k, (hi, lo) in enumerate(qkv_parts):
                dve.wait_ge(split_hi, len(pieces) + k + 1)
                dve.tensor_tensor(lo, by_head[k], hi.bitcast(F32), ALU.subtract).then_inc(split_lo, 1)

            def alone(sem, value):
                dve.wait_ge(blocks0, 2)
                dve.wait_ge(sem, value)

            def rest(lo, ps, hi):
                return dve.tensor_tensor(lo, ps, hi.bitcast(F32), ALU.subtract)

            def stats(src, c, n, bn, mv):
                dve.bn_stats(col(c, BN, 6), src).then_inc(bn, 1)
                alone(bn, n[c])
                dve.bn_aggr(col(c, MV, 2), col(c, BN, 6)).then_inc(mv, 1)

            def steps(entries, it, reg):
                at = counts(it, reg)
                pair = pair_counts(it, reg)
                stored = [[reg(it * 32 + (32 * a + 16 * (r + 1))) for r in range(2)] for a in (0, 1)]
                for step, c, ahead in entries:
                    n = at[ahead]
                    if step in ("t0", "t1", "t2"):
                        i = int(step[1])
                        dve.wait_ge(th[i], n[c])
                        rest(T(Tl, c), by_chunk(psA[c]), T(Th, c)).then_inc(t_sb[i], 1)
                    if step in ("g0", "g1"):
                        i = int(step[1])
                        dve.wait_ge(g_ps[i], n[c])
                        dve.tensor_tensor(H[:, c, :], psB[c][:, :], (b1_all, b2_all)[i][:, :], ALU.add).then_inc(b_ok[i], 1)
                    if step == "z3":
                        dve.wait_ge(g_ps[2], n[c])
                        dve.wait_ge(b3_ok, n[c])
                        dve.tensor_tensor(X[:, c, :], psB[c][:, :], X[:, c, :], ALU.add).then_inc(z3, 1)
                        dve.wait_ge(z3, n[c])
                        stats(X[:, c, :], c, n, bn3, mv3)
                    if step == "x3":
                        dve.wait_ge(rs3, n[c])
                        dve.tensor_scalar(X[:, c, :], X[:, c, :], col(c, MV), col(c, RS), ALU.subtract, ALU.mult).then_inc(x3_ok, 1)
                    if step == "xp":
                        dve.wait_ge(xph, n[c])
                        rest(T(Tl, c), by_chunk(psA[c]), T(Th, c)).then_inc(xp_sb, 1)
                    if step == "qk":
                        for b in (1, 3):
                            dve.wait_ge(qk_ps[b], pair[ahead][c])
                            dve.tensor_copy(QK[:, 2 * b:2 * b + 2, :], by_pair(bank(c, b))).then_inc(qk_sb[b], 1)
                    if step == "s":
                        alone(bs_ok, n[c])
                        for p in range(HEADS):
                            if p % HG == 0:
                                alone((s_psA, s_psB)[p // HG], n[c])
                            last = dve.tensor_tensor_reduce(E[:, c, p, :], (psA, psB)[p // HG][c][:, p % HG * P:(p % HG + 1) * P], BS[:, c, :],
                                                            1.0, -FLT_MAX, ALU.add, ALU.max, col(c, NMX + p))
                        last.then_inc(max_ok, 1)
                        dve.wait_ge(max_ok, n[c])
                        dve.tensor_scalar(col(c, NB, HEADS), col(c, NMX, HEADS), -SCALE, None, ALU.mult).then_inc(nb_ok, 1)
                    if step == "sm":
                        dve.wait_ge(ex_ok, n[c])
                        dve.reciprocal(col(c, REC, HEADS), col(c, SUM, HEADS)).then_inc(rec_ok, 1)
                        dve.wait_ge(rec_ok, n[c])
                        dve.tensor_scalar(col(c, RLA, HEADS), col(c, REC, HEADS), LA, None, ALU.mult).then_inc(rla_ok, 1)
                        dve.wait_ge(rla_ok, n[c])
                        dve.wait_ge(cm_ok, n[c])
                        for h in range(HEADS):
                            last = dve.scalar_tensor_tensor(E[:, c, h, :], E[:, c, h, :], col(c, RLA + h), Cm[:, c, :],
                                                            ALU.mult, ALU.add)
                        last.then_inc(attn_ok, 1)
                    if step == "ta":
                        dve.wait_ge(ta_psB, n[c])
                        dve.tensor_copy(AA[:, c % 2, HG:HEADS, :], by_chunk(psB[c])).then_inc(ta_sbB, 1)
                    if step == "av":
                        dve.wait_ge(avh, n[c])
                        rest(T(Tl, c), by_chunk(psA[c]), T(Th, c)).then_inc(av_sb, 1)
                    if step == "z4":
                        dve.wait_ge(wo_ps, n[c])
                        dve.wait_ge(bo_ok, n[c])
                        dve.wait_ge(out_stored[c % 2], stored[ahead][c // 2])
                        dve.tensor_tensor(Z[:, c % 2, :], psA[c][:, :], X[:, c, :], ALU.add).then_inc(z4, 1)
                        dve.wait_ge(z4, n[c])
                        stats(Z[:, c % 2, :], c, n, bn4, mv4)
                    if step == "x4":
                        dve.wait_ge(rs4, n[c])
                        dve.tensor_scalar(Z[:, c % 2, :], Z[:, c % 2, :], col(c, MV), col(c, RS), ALU.subtract, ALU.mult)\
                            .then_inc(x4_ok, 1)

            steps(START[len(PREP):], -1, number)
            with dve.Fori(0, iters - 1) as it:
                steps(ORDER, it, dve.to_reg)
            steps(END, iters - 1, number)

        @block.tensor
        def _(pe):
            pe.wait_ge(consts_ok, 5)

            def products(out, terms):
                for i, (lhsT, rhs) in enumerate(terms):
                    mm = pe.matmul(out, lhsT, rhs, start=i == 0, stop=i == len(terms) - 1)
                return mm

            def three(lh, ll, rh, rl):
                return [(lh, rh), (lh, rl), (ll, rh)]

            def project(out, c, W):
                terms = []
                for k in range(KD):
                    terms += three(T(Th, c)[:, k, :], T(Tl, c)[:, k, :], W[0][:, k, :], W[1][:, k, :])
                return products(out, terms)

            def adjT(c, k):
                pe.wait_ge(adj_in[c], k)
                pe.transpose(psB[c][:, 0:P], A[:, c, :], ident[:, :]).then_inc(adjT_ps, 1)

            def steps(entries, it, reg):
                at = counts(it, reg)
                pair, x_loaded = pair_counts(it, reg), [reg(it * 16 + 16 * (a + 1)) for a in (0, 1)]
                adj_loaded = reg(it * 64 + 128)
                for step, c, ahead in entries:
                    n = at[ahead]
                    if step in ("t0", "t1", "t2"):
                        i = int(step[1])
                        if i == 0:
                            pe.wait_ge(at_sb, n[c])
                            pe.wait_ge(x_in[c], x_loaded[ahead])
                        else:
                            pe.wait_ge(g_sb[i - 1], n[c])
                        for k in range(KD):
                            f = slice(k * P, (k + 1) * P)
                            mm = products(psA[c][:, f], [((H if i else X)[:, c, f], AT[:, c, :])])
                        mm.then_inc(t_ps[i], 1)
                    if step in ("g0", "g1", "g2"):
                        i = int(step[1])
                        pe.wait_ge(t_sb[i], n[c])
                        project(psB[c][:, :], c, GW[i]).then_inc(g_ps[i], 1)
                    if step == "xp":
                        pe.wait_ge(x3_ok, n[c])
                        for k in range(KD):
                            mm = pe.transpose(psA[c][:, k * P:(k + 1) * P], X[:, c, k * P:(k + 1) * P], ident[:, :])
                        mm.then_inc(xp_ps, 1)
                    if step == "v":
                        pe.wait_ge(xp_sb, n[c])
                        project(psB[c][:, :], c, (WQh[:, :, 2, :], WQl[:, :, 2, :])).then_inc(v_ps, 1)
                    if step == "qk":
                        pe.wait_ge(v_sb, n[2 * c + 1])
                        cols = slice(2 * c * P, (2 * c + 2) * P)
                        for b in range(4):
                            for m in range(2):
                                i, f = divmod((2 * b + m) * P, D)
                                terms = []
                                for k in range(KD):
                                    terms += three(WQh[:, k, i, f:f + P], WQl[:, k, i, f:f + P], Th[:, k, cols], Tl[:, k, cols])
                                mm = products(bank(c, b)[:, m * 2 * P:(m + 1) * 2 * P], terms)
                            mm.then_inc(qk_ps[b], 1)
                    if step == "s":
                        if c % 2 == 0:
                            for b in range(4):
                                pe.wait_ge(qk_sb[b], pair[ahead][c // 2])
                        rows_c = slice(c % 2 * P, (c % 2 + 1) * P)
                        for m in range(HG):
                            for odd, ps in enumerate((psA, psB)):
                                q = slice(odd * DHEAD, (odd + 1) * DHEAD)
                                mm = pe.matmul(ps[c][:, m * P:(m + 1) * P], QK[q, m, rows_c], QK[q, KD + m, rows_c],
                                               start=True, stop=True)
                                if m == HG - 1:
                                    mm.then_inc((s_psA, s_psB)[odd], 1)
                    if step == "ta":
                        pe.wait_ge(attn_ok, n[c])
                        for ps, h0, ready in ((psA, 0, ta_psA), (psB, HG, ta_psB)):
                            for h in range(h0, h0 + HG):
                                mm = pe.transpose(ps[c][:, (h - h0) * P:(h - h0 + 1) * P], E[:, c, h, :], ident[:, :])
                            mm.then_inc(ready, 1)
                    if step == "av":
                        pe.wait_ge(ta_sbA, n[c])
                        pe.wait_ge(ta_sbB, n[c])
                        for h in range(HEADS):
                            q, m = slice(h % 2 * DHEAD, (h % 2 + 1) * DHEAD), h // 2
                            mm = pe.matmul(psA[c][q, m * P:(m + 1) * P], H[:, c, h * DHEAD:(h + 1) * DHEAD],
                                           AA[:, c % 2, h % 2 * HG + m, :], start=True, stop=True)
                        mm.then_inc(av_ps, 1)
                    if step == "wo":
                        pe.wait_ge(av_sb, n[c])
                        project(psA[c][:, :], c, WO).then_inc(wo_ps, 1)
                    if step == "adjT":
                        adjT(c, adj_loaded)

            steps(PREP, -1, number)
            pe.wait_ge(split_lo, len(pieces) + KD)
            steps(START[len(PREP):], -1, number)
            with pe.Fori(0, iters - 1) as it:
                steps(ORDER, it, pe.to_reg)
            steps(END, iters - 1, number)


def kernel(**inputs):
    import numpy as np
    import concourse.bacc as bacc
    from concourse.bass_utils import run_bass_kernel_spmd

    nc = bacc.Bacc("TRN2", target_bir_lowering=False, num_devices=1)
    given = {k: np.asarray(v) for k, v in inputs.items()}
    n, c, d = given["x"].shape
    tiles = n * c // P
    mask = given["nodemask"].reshape(tiles, P)
    arrays = {
        "x": given["x"], "adj": given["adj"], "mask_rows": mask, "mask_cols": mask.T,
        "L0_W1T": given["L0_gnn_W1"].T, "L0_b1": given["L0_gnn_b1"], "L0_gamma": given["L0_gnn_gamma"],
        "L0_beta": given["L0_gnn_beta"], "L0_W2T": given["L0_gnn_W2"].T, "L0_b2": given["L0_gnn_b2"],
        "L1_w": given["L1_gnn_w"], "L1_wT": given["L1_gnn_w"].T, "L1_a": given["L1_gnn_a"],
        "L2_W1": given["L2_gnn_W1"], "L2_b1": given["L2_gnn_b1"], "L2_W2": given["L2_gnn_W2"], "L2_b2": given["L2_gnn_b2"],
        "L2_W3": given["L2_gnn_W3"], "L2_b3": given["L2_gnn_b3"],
        "L3_Wqkv": given["L3_gnn_W_qkv"], "L3_Wout": given["L3_gnn_W_out"], "L3_bout": given["L3_gnn_b_out"],
    }
    arrays = {k: np.ascontiguousarray(v) for k, v in arrays.items()}
    ap = {k: nc.dram_tensor("in_" + k, v.shape, mybir.dt.from_np(v.dtype), kind="ExternalInput").ap() for k, v in arrays.items()}
    out = nc.dram_tensor("out", (n, c, d), F32, kind="ExternalOutput").ap()
    x2 = nc.dram_tensor("x2", (tiles, P, d), F32, kind="Internal").ap()
    later = ("L2_W1", "L2_W2", "L2_W3", "L3_Wout")
    with ExitStack() as ctx:
        E = ctx.enter_context(nc.sbuf_tensor("E", [P, CH, HEADS, P], F32))
        AA = ctx.enter_context(nc.sbuf_tensor("AA", [P, 2, HEADS, P], F32))
        QK = ctx.enter_context(nc.sbuf_tensor("QK", [P, 2 * KD, 2 * P], F32))
        slots = ([E[:, i, :, :].rearrange("p h j -> p (h j)") for i in range(CH)]
                 + [AA[:, i, :, :].rearrange("p h j -> p (h j)") for i in range(2)]
                 + [QK[:, i * KD:(i + 1) * KD, :].rearrange("p k j -> p (k j)") for i in range(2)])
        semaphores = []
        hypergraph_and_pairwise(nc, semaphores, ap["x"], ap["adj"], ap["L0_W1T"], ap["L0_b1"], ap["L0_gamma"], ap["L0_beta"],
                                ap["L0_W2T"], ap["L0_b2"], ap["L1_w"], ap["L1_wT"], ap["L1_a"], x2, slots,
                                [ap[name].rearrange("(k p) n -> p k n", p=P)[:, k:k + 2, :] for name in later for k in (0, 2)])
        nc.clear_and_free_semaphores(semaphores)
        nc.all_engine_barrier()
        convolutions_and_attention(nc, [], x2, ap["adj"], ap["mask_rows"], ap["mask_cols"], E, AA, QK, slots,
                                   ap["L2_b1"], ap["L2_b2"], ap["L2_b3"], ap["L3_Wqkv"], ap["L3_bout"], out)
    r = run_bass_kernel_spmd(nc, [{"in_" + k: v for k, v in arrays.items()}], core_ids=[0])
    return r.results[0]["out"]
```
